# Optimizing a Trainium2 kernel written in Bass

```python
import numpy as np
import jax
import jax.numpy as jnp

def _softmax(x, axis=-1):
    return jax.nn.softmax(x, axis=axis)

def _gelu(x):
    return jax.nn.gelu(x, approximate=True)

def _silu(x):
    return jax.nn.silu(x)

def _sigmoid(x):
    return jax.nn.sigmoid(x)

def _layernorm(x, axis=-1, eps=1e-05):
    m = jnp.mean(x, axis=axis, keepdims=True)
    v = jnp.var(x, axis=axis, keepdims=True)
    return (x - m) / jnp.sqrt(v + eps)

def _scatter_add(tgt, idx, src, axis=0):
    return tgt.at[idx].add(src)

def _segment_sum(src, seg, n):
    return jax.ops.segment_sum(src, seg, n)
kernel_name = 'mk_audio_tower_d4_tok_audfeat512_r4_6a6d32'

def setup_inputs(seed: int=0):
    np.random.seed(seed)
    _w = jnp.asarray

    def _rec_inputs():
        import jax
        import jax.numpy as jnp
        _rk = jax.random.key(seed)
        x = -7.10856e-05 + 0.999911 * jax.random.normal(jax.random.fold_in(_rk, 1), (64, 256, 128), jnp.float32)
        return x
    x = _rec_inputs()

    def _L0_tok_setup():
        import jax, jax.numpy as jnp
        import numpy as np
        BLOCK = 128
        TOP_K = 16
        key = jax.random.key(seed)
        k1, k2 = jax.random.split(key)
        B, S, D = (8, 4096, 128)
        x = jax.random.normal(k1, (B, S, D), dtype=jnp.float32)
        W = jax.random.normal(k2, (1, D), dtype=jnp.float32) * (1.0 / np.sqrt(D))
        b = jnp.zeros((1,), dtype=jnp.float32)
        return {'x': x, 'W': W, 'b': b}
    _L0_tok_all = _L0_tok_setup()
    _L0_tok_in = {k: v for k, v in _L0_tok_all.items() if k in ('W', 'b')}
    del _L0_tok_all

    def _L0_attn_setup():
        import jax, jax.numpy as jnp
        import numpy as np
        DIM = 128
        HEADS = 8
        DIM_HEAD = 64
        DIM_INNER = HEADS * DIM_HEAD
        SCALE = DIM_HEAD ** (-0.5)
        key = jax.random.key(seed)
        ks = jax.random.split(key, 8)
        b, n = (2, 256)
        x = jax.random.normal(ks[0], (b, n, DIM), dtype=jnp.float32)
        w = lambda k, i, o: jax.random.normal(k, (i, o), dtype=jnp.float32) * 0.02
        return {'x': x, 'w_q_u': w(ks[1], DIM, DIM_INNER), 'w_k_u': w(ks[2], DIM, DIM_INNER), 'w_v_u': w(ks[3], DIM, DIM_INNER), 'w_q_c': w(ks[4], DIM, DIM_INNER), 'w_k_c': w(ks[5], DIM, DIM_INNER), 'w_v_c': w(ks[6], DIM, DIM_INNER), 'w_out': w(ks[7], DIM_INNER, DIM)}
    _L0_attn_all = _L0_attn_setup()
    _L0_attn_in = {k: v for k, v in _L0_attn_all.items() if k in ('w_q_u', 'w_k_u', 'w_v_u', 'w_q_c', 'w_k_c', 'w_v_c', 'w_out')}
    del _L0_attn_all

    def _L0_ffn_setup():
        import jax, jax.numpy as jnp
        import numpy as np
        B, T, D, H = (64, 128, 128, 256)

        def _linear_params(key, out_dim, in_dim):
            kw, kb = jax.random.split(key)
            bound = 1.0 / np.sqrt(in_dim)
            W = jax.random.uniform(kw, (out_dim, in_dim), jnp.float32, -bound, bound)
            b = jax.random.uniform(kb, (out_dim,), jnp.float32, -bound, bound)
            return (W, b)
        key = jax.random.key(seed)
        ks = jax.random.split(key, 8)
        x = jax.random.normal(ks[0], (B, T, D), jnp.float32)
        Wuz, buz = _linear_params(ks[1], H, D)
        Wwz, bwz = _linear_params(ks[2], H, H)
        Wur, bur = _linear_params(ks[3], H, D)
        Wwr, bwr = _linear_params(ks[4], H, H)
        Wu, bu = _linear_params(ks[5], H, D)
        Ww, bw = _linear_params(ks[6], H, H)
        Wo, bo = _linear_params(ks[7], D, H)
        return dict(x=x, Wuz=Wuz, buz=buz, Wwz=Wwz, bwz=bwz, Wur=Wur, bur=bur, Wwr=Wwr, bwr=bwr, Wu=Wu, bu=bu, Ww=Ww, bw=bw, Wo=Wo, bo=bo)
    _L0_ffn_all = _L0_ffn_setup()
    _L0_ffn_in = {k: v for k, v in _L0_ffn_all.items() if k in ('Wuz', 'buz', 'Wwz', 'bwz', 'Wur', 'bur', 'Wwr', 'bwr', 'Wu', 'bu', 'Ww', 'bw', 'Wo', 'bo')}
    del _L0_ffn_all

    def _L1_attn_setup():
        import jax, jax.numpy as jnp
        import numpy as np
        B, S, D, H = (16, 256, 128, 8)
        SCALES = (5, 10, None)

        def _window_bias(seq_len, scale):
            i = jnp.arange(seq_len)
            d = i[:, None] - i[None, :]
            allowed = (d >= 0) & (d < scale)
            return jnp.where(allowed, 0.0, -jnp.inf).astype(jnp.float32)

        def _mha(x, Wqkv, bqkv, Wo, bo, bias):
            b, s, d = x.shape
            hd = d // H
            qkv = x @ Wqkv.T + bqkv
            q, k, v = jnp.split(qkv, 3, axis=-1)
            q = q.reshape(b, s, H, hd) * (1.0 / np.sqrt(hd)).astype(x.dtype)
            k = k.reshape(b, s, H, hd)
            v = v.reshape(b, s, H, hd)
            scores = jnp.einsum('bqhd,bkhd->bhqk', q, k)
            if bias is not None:
                scores = scores + bias
            p = jax.nn.softmax(scores, axis=-1)
            o = jnp.einsum('bhqk,bkhd->bqhd', p, v).reshape(b, s, d)
            return o @ Wo.T + bo
        key = jax.random.key(seed)
        ks = jax.random.split(key, 7)
        x = jax.random.normal(ks[0], (B, S, D), jnp.float32)
        Wqkv = jax.random.normal(ks[1], (3, 3 * D, D), jnp.float32) * 0.02
        bqkv = jax.random.normal(ks[2], (3, 3 * D), jnp.float32) * 0.02
        Wo = jax.random.normal(ks[3], (3, D, D), jnp.float32) * 0.02
        bo = jax.random.normal(ks[4], (3, D), jnp.float32) * 0.02
        Wf = jax.random.normal(ks[5], (D, 3 * D), jnp.float32) * 0.02
        bf = jax.random.normal(ks[6], (D,), jnp.float32) * 0.02
        return {'x': x, 'Wqkv': Wqkv, 'bqkv': bqkv, 'Wo': Wo, 'bo': bo, 'Wf': Wf, 'bf': bf}
    _L1_attn_all = _L1_attn_setup()
    _L1_attn_in = {k: v for k, v in _L1_attn_all.items() if k in ('Wqkv', 'bqkv', 'Wo', 'bo', 'Wf', 'bf')}
    del _L1_attn_all

    def _L1_ffn_setup():
        import jax, jax.numpy as jnp
        import numpy as np
        D = 128
        E = 8
        K = 2
        EXP = 4
        LN_EPS = 1e-05
        key = jax.random.key(seed)
        ks = jax.random.split(key, 8)
        B, T = (8, 512)
        Dh = D * EXP
        x = jax.random.normal(ks[0], (B, T, D), dtype=jnp.float32)
        ln_g = jnp.ones((D,), dtype=jnp.float32)
        ln_b = jnp.zeros((D,), dtype=jnp.float32)
        lim_r = np.sqrt(6.0 / (D + E)).astype(np.float32)
        w_r = jax.random.uniform(ks[1], (E, D), dtype=jnp.float32, minval=-lim_r, maxval=lim_r)
        b_r = jnp.zeros((E,), dtype=jnp.float32)
        lim1 = np.sqrt(6.0 / (D + Dh)).astype(np.float32)
        W1 = jax.random.uniform(ks[2], (E, D, Dh), dtype=jnp.float32, minval=-lim1, maxval=lim1)
        b1 = jnp.zeros((E, Dh), dtype=jnp.float32)
        W2 = jax.random.uniform(ks[3], (E, Dh, D), dtype=jnp.float32, minval=-lim1, maxval=lim1)
        b2 = jnp.zeros((E, D), dtype=jnp.float32)
        return {'x': x, 'ln_g': ln_g, 'ln_b': ln_b, 'w_r': w_r, 'b_r': b_r, 'W1': W1, 'b1': b1, 'W2': W2, 'b2': b2}
    _L1_ffn_all = _L1_ffn_setup()
    _L1_ffn_in = {k: v for k, v in _L1_ffn_all.items() if k in ('ln_g', 'ln_b', 'w_r', 'b_r', 'W1', 'b1', 'W2', 'b2')}
    del _L1_ffn_all

    def _L2_attn_setup():
        import jax, jax.numpy as jnp
        import numpy as np
        T, BATCH, DIM = (512, 32, 128)

        def _layernorm(y, gamma, beta, eps=1e-05):
            mu = jnp.mean(y, axis=-1, keepdims=True)
            var = jnp.mean(jnp.square(y - mu), axis=-1, keepdims=True)
            return (y - mu) * jax.lax.rsqrt(var + eps) * gamma + beta
        key = jax.random.key(seed)
        ks = jax.random.split(key, 9)
        s = 1.0 / np.sqrt(DIM)
        return {'x': jax.random.normal(ks[0], (T, BATCH, DIM), dtype=jnp.float32), 'W_in': jax.random.uniform(ks[1], (2 * DIM, DIM), jnp.float32, -s, s), 'b_in': jax.random.uniform(ks[2], (2 * DIM,), jnp.float32, -s, s), 'W_out': jax.random.uniform(ks[3], (DIM, DIM), jnp.float32, -s, s), 'b_out': jax.random.uniform(ks[4], (DIM,), jnp.float32, -s, s), 'A': jax.random.normal(ks[5], (DIM,), dtype=jnp.float32) * 0.1, 'B': jax.random.normal(ks[6], (DIM,), dtype=jnp.float32) * 0.1, 'gamma': jnp.ones((DIM,), dtype=jnp.float32), 'beta': jnp.zeros((DIM,), dtype=jnp.float32)}
    _L2_attn_all = _L2_attn_setup()
    _L2_attn_in = {k: v for k, v in _L2_attn_all.items() if k in ('W_in', 'b_in', 'W_out', 'b_out', 'A', 'B', 'gamma', 'beta')}
    del _L2_attn_all

    def _L2_ffn_setup():
        import jax, jax.numpy as jnp
        import numpy as np
        D = 128
        H = 8
        K = 4
        HD = D // H

        def _ln(x, w, b, eps=1e-05):
            m = x.mean(-1, keepdims=True)
            v = ((x - m) ** 2).mean(-1, keepdims=True)
            return (x - m) / jnp.sqrt(v + eps) * w + b

        def _spatial_experts(xn, idx, in_w, in_b, out_w, out_b):
            W = in_w[idx]
            qkv = jnp.einsum('btd,bed->bte', xn, W) + in_b[idx][:, None, :]
            q, k, v = jnp.split(qkv, 3, axis=-1)
            B, T, _ = xn.shape
            q = q.reshape(B, T, H, HD) * HD ** (-0.5)
            k = k.reshape(B, T, H, HD)
            v = v.reshape(B, T, H, HD)
            att = jax.nn.softmax(jnp.einsum('bthd,bshd->bhts', q, k), axis=-1)
            o = jnp.einsum('bhts,bshd->bthd', att, v).reshape(B, T, D)
            return jnp.einsum('btd,bod->bto', o, out_w[idx]) + out_b[idx][:, None, :]

        def _temporal_experts(xt, idx, qw, qb, kw, kb, vw, vb, pw, pb):
            B, T, _ = xt.shape
            q = (jnp.einsum('btd,bod->bto', xt, qw[idx]) + qb[idx][:, None, :]).reshape(B, T, H, HD)
            k = (jnp.einsum('btd,bod->bto', xt, kw[idx]) + kb[idx][:, None, :]).reshape(B, T, H, HD)
            v = (jnp.einsum('btd,bod->bto', xt, vw[idx]) + vb[idx][:, None, :]).reshape(B, T, H, HD)
            logits = jnp.einsum('bthd,bshd->bhts', q, k) * HD ** (-0.5)
            causal = jnp.tril(jnp.ones((T, T), dtype=bool))
            logits = jnp.where(causal, logits, -jnp.inf)
            att = jax.nn.softmax(logits, axis=-1)
            o = jnp.einsum('bhts,bshd->bthd', att, v).reshape(B, T, D)
            o = jnp.einsum('btd,bod->bto', o, pw[idx]) + pb[idx][:, None, :]
            return xt + o

        def _cross_mha(q_in, kv_in, in_w, in_b, out_w, out_b):
            B, T, _ = q_in.shape
            S = kv_in.shape[1]
            Wq, Wk, Wv = (in_w[:D], in_w[D:2 * D], in_w[2 * D:])
            bq, bk, bv = (in_b[:D], in_b[D:2 * D], in_b[2 * D:])
            q = (q_in @ Wq.T + bq).reshape(B, T, H, HD) * HD ** (-0.5)
            k = (kv_in @ Wk.T + bk).reshape(B, S, H, HD)
            v = (kv_in @ Wv.T + bv).reshape(B, S, H, HD)
            att = jax.nn.softmax(jnp.einsum('bthd,bshd->bhts', q, k), axis=-1)
            o = jnp.einsum('bhts,bshd->bthd', att, v).reshape(B, T, D)
            return o @ out_w.T + out_b
        key = jax.random.key(seed)
        ks = iter(jax.random.split(key, 40))
        B, T = (64, 64)
        p = lambda *shape: jax.random.normal(next(ks), shape, dtype=jnp.float32) * 0.02
        inp = {'x': jax.random.normal(next(ks), (B, T, D), dtype=jnp.float32), 'router_w1': p(128, D), 'router_b1': jnp.zeros((128,), jnp.float32), 'router_w2': p(2 * K, 128), 'router_b2': jnp.zeros((2 * K,), jnp.float32), 'norm_s_w': jnp.ones((D,), jnp.float32), 'norm_s_b': jnp.zeros((D,), jnp.float32), 'norm_t_w': jnp.ones((D,), jnp.float32), 'norm_t_b': jnp.zeros((D,), jnp.float32), 'sp_in_w': p(K, 3 * D, D), 'sp_in_b': jnp.zeros((K, 3 * D), jnp.float32), 'sp_out_w': p(K, D, D), 'sp_out_b': jnp.zeros((K, D), jnp.float32), 'tq_w': p(K, D, D), 'tq_b': jnp.zeros((K, D), jnp.float32), 'tk_w': p(K, D, D), 'tk_b': jnp.zeros((K, D), jnp.float32), 'tv_w': p(K, D, D), 'tv_b': jnp.zeros((K, D), jnp.float32), 'tp_w': p(K, D, D), 'tp_b': jnp.zeros((K, D), jnp.float32), 'cross_in_w': p(3 * D, D), 'cross_in_b': jnp.zeros((3 * D,), jnp.float32), 'cross_out_w': p(D, D), 'cross_out_b': jnp.zeros((D,), jnp.float32), 'norm_mlp_w': jnp.ones((D,), jnp.float32), 'norm_mlp_b': jnp.zeros((D,), jnp.float32), 'mlp_w1': p(4 * D, D), 'mlp_b1': jnp.zeros((4 * D,), jnp.float32), 'mlp_w2': p(D, 4 * D), 'mlp_b2': jnp.zeros((D,), jnp.float32)}
        return inp
    _L2_ffn_all = _L2_ffn_setup()
    _L2_ffn_in = {k: v for k, v in _L2_ffn_all.items() if k in ('router_w1', 'router_b1', 'router_w2', 'router_b2', 'norm_s_w', 'norm_s_b', 'norm_t_w', 'norm_t_b', 'sp_in_w', 'sp_in_b', 'sp_out_w', 'sp_out_b', 'tq_w', 'tq_b', 'tk_w', 'tk_b', 'tv_w', 'tv_b', 'tp_w', 'tp_b', 'cross_in_w', 'cross_in_b', 'cross_out_w', 'cross_out_b', 'norm_mlp_w', 'norm_mlp_b', 'mlp_w1', 'mlp_b1', 'mlp_w2', 'mlp_b2')}
    del _L2_ffn_all

    def _L3_attn_setup():
        import jax, jax.numpy as jnp
        import numpy as np
        NUM_HEADS = 8
        WINDOW = 64
        key = jax.random.key(seed)
        k1, k2, k3, k4, k5 = jax.random.split(key, 5)
        B, T, D = (1, 1024, 128)
        x = jax.random.normal(k1, (B, T, D), dtype=jnp.float32)
        Wq = jax.random.normal(k2, (D, D), dtype=jnp.float32) * D ** (-0.5)
        Wk = jax.random.normal(k3, (D, D), dtype=jnp.float32) * D ** (-0.5)
        Wv = jax.random.normal(k4, (D, D), dtype=jnp.float32) * D ** (-0.5)
        rel_pos_bias = jax.random.normal(k5, (1, NUM_HEADS, 2 * WINDOW - 1), dtype=jnp.float32)
        return {'x': x, 'Wq': Wq, 'Wk': Wk, 'Wv': Wv, 'rel_pos_bias': rel_pos_bias}
    _L3_attn_all = _L3_attn_setup()
    _L3_attn_in = {k: v for k, v in _L3_attn_all.items() if k in ('Wq', 'Wk', 'Wv', 'rel_pos_bias')}
    del _L3_attn_all

    def _L3_ffn_setup():
        import jax, jax.numpy as jnp
        import numpy as np
        B, T, H = (8, 2048, 128)
        E, R = (4, 16)
        SCALE = 0.04
        key = jax.random.key(seed)
        ks = jax.random.split(key, 7)
        return {'x': jax.random.normal(ks[0], (B, T, H), jnp.float32), 'gate_w': jax.random.normal(ks[1], (E, H), jnp.float32) * SCALE, 'thr_w': jax.random.normal(ks[2], (1, H), jnp.float32) * SCALE, 'fc1_w': jax.random.normal(ks[3], (E, H, H), jnp.float32) * SCALE, 'lora_A': jax.random.normal(ks[4], (E, H, R), jnp.float32) * SCALE, 'lora_B': jax.random.normal(ks[5], (E, R, H), jnp.float32) * SCALE, 'fc2_w': jax.random.normal(ks[6], (E, H, H), jnp.float32) * SCALE}
    _L3_ffn_all = _L3_ffn_setup()
    _L3_ffn_in = {k: v for k, v in _L3_ffn_all.items() if k in ('gate_w', 'thr_w', 'fc1_w', 'lora_A', 'lora_B', 'fc2_w')}
    del _L3_ffn_all
    return {'x': x, 'L0_tok_W': _L0_tok_in['W'], 'L0_tok_b': _L0_tok_in['b'], 'L0_attn_w_q_u': _L0_attn_in['w_q_u'], 'L0_attn_w_k_u': _L0_attn_in['w_k_u'], 'L0_attn_w_v_u': _L0_attn_in['w_v_u'], 'L0_attn_w_q_c': _L0_attn_in['w_q_c'], 'L0_attn_w_k_c': _L0_attn_in['w_k_c'], 'L0_attn_w_v_c': _L0_attn_in['w_v_c'], 'L0_attn_w_out': _L0_attn_in['w_out'], 'L0_ffn_Wuz': _L0_ffn_in['Wuz'], 'L0_ffn_buz': _L0_ffn_in['buz'], 'L0_ffn_Wwz': _L0_ffn_in['Wwz'], 'L0_ffn_bwz': _L0_ffn_in['bwz'], 'L0_ffn_Wur': _L0_ffn_in['Wur'], 'L0_ffn_bur': _L0_ffn_in['bur'], 'L0_ffn_Wwr': _L0_ffn_in['Wwr'], 'L0_ffn_bwr': _L0_ffn_in['bwr'], 'L0_ffn_Wu': _L0_ffn_in['Wu'], 'L0_ffn_bu': _L0_ffn_in['bu'], 'L0_ffn_Ww': _L0_ffn_in['Ww'], 'L0_ffn_bw': _L0_ffn_in['bw'], 'L0_ffn_Wo': _L0_ffn_in['Wo'], 'L0_ffn_bo': _L0_ffn_in['bo'], 'L1_attn_Wqkv': _L1_attn_in['Wqkv'], 'L1_attn_bqkv': _L1_attn_in['bqkv'], 'L1_attn_Wo': _L1_attn_in['Wo'], 'L1_attn_bo': _L1_attn_in['bo'], 'L1_attn_Wf': _L1_attn_in['Wf'], 'L1_attn_bf': _L1_attn_in['bf'], 'L1_ffn_ln_g': _L1_ffn_in['ln_g'], 'L1_ffn_ln_b': _L1_ffn_in['ln_b'], 'L1_ffn_w_r': _L1_ffn_in['w_r'], 'L1_ffn_b_r': _L1_ffn_in['b_r'], 'L1_ffn_W1': _L1_ffn_in['W1'], 'L1_ffn_b1': _L1_ffn_in['b1'], 'L1_ffn_W2': _L1_ffn_in['W2'], 'L1_ffn_b2': _L1_ffn_in['b2'], 'L2_attn_W_in': _L2_attn_in['W_in'], 'L2_attn_b_in': _L2_attn_in['b_in'], 'L2_attn_W_out': _L2_attn_in['W_out'], 'L2_attn_b_out': _L2_attn_in['b_out'], 'L2_attn_A': _L2_attn_in['A'], 'L2_attn_B': _L2_attn_in['B'], 'L2_attn_gamma': _L2_attn_in['gamma'], 'L2_attn_beta': _L2_attn_in['beta'], 'L2_ffn_router_w1': _L2_ffn_in['router_w1'], 'L2_ffn_router_b1': _L2_ffn_in['router_b1'], 'L2_ffn_router_w2': _L2_ffn_in['router_w2'], 'L2_ffn_router_b2': _L2_ffn_in['router_b2'], 'L2_ffn_norm_s_w': _L2_ffn_in['norm_s_w'], 'L2_ffn_norm_s_b': _L2_ffn_in['norm_s_b'], 'L2_ffn_norm_t_w': _L2_ffn_in['norm_t_w'], 'L2_ffn_norm_t_b': _L2_ffn_in['norm_t_b'], 'L2_ffn_sp_in_w': _L2_ffn_in['sp_in_w'], 'L2_ffn_sp_in_b': _L2_ffn_in['sp_in_b'], 'L2_ffn_sp_out_w': _L2_ffn_in['sp_out_w'], 'L2_ffn_sp_out_b': _L2_ffn_in['sp_out_b'], 'L2_ffn_tq_w': _L2_ffn_in['tq_w'], 'L2_ffn_tq_b': _L2_ffn_in['tq_b'], 'L2_ffn_tk_w': _L2_ffn_in['tk_w'], 'L2_ffn_tk_b': _L2_ffn_in['tk_b'], 'L2_ffn_tv_w': _L2_ffn_in['tv_w'], 'L2_ffn_tv_b': _L2_ffn_in['tv_b'], 'L2_ffn_tp_w': _L2_ffn_in['tp_w'], 'L2_ffn_tp_b': _L2_ffn_in['tp_b'], 'L2_ffn_cross_in_w': _L2_ffn_in['cross_in_w'], 'L2_ffn_cross_in_b': _L2_ffn_in['cross_in_b'], 'L2_ffn_cross_out_w': _L2_ffn_in['cross_out_w'], 'L2_ffn_cross_out_b': _L2_ffn_in['cross_out_b'], 'L2_ffn_norm_mlp_w': _L2_ffn_in['norm_mlp_w'], 'L2_ffn_norm_mlp_b': _L2_ffn_in['norm_mlp_b'], 'L2_ffn_mlp_w1': _L2_ffn_in['mlp_w1'], 'L2_ffn_mlp_b1': _L2_ffn_in['mlp_b1'], 'L2_ffn_mlp_w2': _L2_ffn_in['mlp_w2'], 'L2_ffn_mlp_b2': _L2_ffn_in['mlp_b2'], 'L3_attn_Wq': _L3_attn_in['Wq'], 'L3_attn_Wk': _L3_attn_in['Wk'], 'L3_attn_Wv': _L3_attn_in['Wv'], 'L3_attn_rel_pos_bias': _L3_attn_in['rel_pos_bias'], 'L3_ffn_gate_w': _L3_ffn_in['gate_w'], 'L3_ffn_thr_w': _L3_ffn_in['thr_w'], 'L3_ffn_fc1_w': _L3_ffn_in['fc1_w'], 'L3_ffn_lora_A': _L3_ffn_in['lora_A'], 'L3_ffn_lora_B': _L3_ffn_in['lora_B'], 'L3_ffn_fc2_w': _L3_ffn_in['fc2_w']}

def reference(x, L0_tok_W, L0_tok_b, L0_attn_w_q_u, L0_attn_w_k_u, L0_attn_w_v_u, L0_attn_w_q_c, L0_attn_w_k_c, L0_attn_w_v_c, L0_attn_w_out, L0_ffn_Wuz, L0_ffn_buz, L0_ffn_Wwz, L0_ffn_bwz, L0_ffn_Wur, L0_ffn_bur, L0_ffn_Wwr, L0_ffn_bwr, L0_ffn_Wu, L0_ffn_bu, L0_ffn_Ww, L0_ffn_bw, L0_ffn_Wo, L0_ffn_bo, L1_attn_Wqkv, L1_attn_bqkv, L1_attn_Wo, L1_attn_bo, L1_attn_Wf, L1_attn_bf, L1_ffn_ln_g, L1_ffn_ln_b, L1_ffn_w_r, L1_ffn_b_r, L1_ffn_W1, L1_ffn_b1, L1_ffn_W2, L1_ffn_b2, L2_attn_W_in, L2_attn_b_in, L2_attn_W_out, L2_attn_b_out, L2_attn_A, L2_attn_B, L2_attn_gamma, L2_attn_beta, L2_ffn_router_w1, L2_ffn_router_b1, L2_ffn_router_w2, L2_ffn_router_b2, L2_ffn_norm_s_w, L2_ffn_norm_s_b, L2_ffn_norm_t_w, L2_ffn_norm_t_b, L2_ffn_sp_in_w, L2_ffn_sp_in_b, L2_ffn_sp_out_w, L2_ffn_sp_out_b, L2_ffn_tq_w, L2_ffn_tq_b, L2_ffn_tk_w, L2_ffn_tk_b, L2_ffn_tv_w, L2_ffn_tv_b, L2_ffn_tp_w, L2_ffn_tp_b, L2_ffn_cross_in_w, L2_ffn_cross_in_b, L2_ffn_cross_out_w, L2_ffn_cross_out_b, L2_ffn_norm_mlp_w, L2_ffn_norm_mlp_b, L2_ffn_mlp_w1, L2_ffn_mlp_b1, L2_ffn_mlp_w2, L2_ffn_mlp_b2, L3_attn_Wq, L3_attn_Wk, L3_attn_Wv, L3_attn_rel_pos_bias, L3_ffn_gate_w, L3_ffn_thr_w, L3_ffn_fc1_w, L3_ffn_lora_A, L3_ffn_lora_B, L3_ffn_fc2_w):
    import jax
    import jax.numpy as jnp

    def _L0_tok_ref(x, W, b):
        import jax, jax.numpy as jnp
        import numpy as np
        BLOCK = 128
        TOP_K = 16
        B, S, D = x.shape
        n_blocks = S // BLOCK
        scores = jnp.einsum('bsd,d->bs', x, W[0]) + b[0]
        block_scores = scores.reshape(B, n_blocks, BLOCK)
        _, top_idx = jax.lax.top_k(block_scores, TOP_K)
        offsets = (jnp.arange(n_blocks, dtype=top_idx.dtype) * BLOCK)[None, :, None]
        sel_idx = (top_idx + offsets).reshape(B, n_blocks * TOP_K)
        selected_tokens = jnp.take_along_axis(x, sel_idx[:, :, None], axis=1)
        return selected_tokens

    def _L0_attn_ref(x, w_q_u, w_k_u, w_v_u, w_q_c, w_k_c, w_v_c, w_out):
        import jax, jax.numpy as jnp
        import numpy as np
        DIM = 128
        HEADS = 8
        DIM_HEAD = 64
        DIM_INNER = HEADS * DIM_HEAD
        SCALE = DIM_HEAD ** (-0.5)
        b, n, _ = x.shape

        def proj(w):
            return (x @ w).reshape(b, n, HEADS, DIM_HEAD).transpose(0, 2, 1, 3)
        q_u, k_u, v_u = (proj(w_q_u), proj(w_k_u), proj(w_v_u))
        q_c, k_c, v_c = (proj(w_q_c), proj(w_k_c), proj(w_v_c))
        idx = jnp.arange(n)
        causal = idx[:, None] >= idx[None, :]
        term1 = jnp.einsum('bhid,bhjd->bhij', q_c, v_u) * SCALE
        term1 = term1 * causal.astype(term1.dtype)
        logits_u = jnp.einsum('bhid,bhjd->bhij', q_u, k_u) * SCALE
        sig = jax.nn.sigmoid(jnp.where(causal, -jnp.inf, logits_u))
        S_u = jnp.einsum('bhij,bhkj->bhik', term1, sig)
        S_c = jnp.einsum('bhid,bhjd->bhij', q_c, k_c) * SCALE
        S_c = jnp.where(causal, S_c, -jnp.inf)
        final_scores = S_c - jax.nn.silu(S_u)
        attn = jax.nn.softmax(final_scores, axis=-1)
        out = jnp.einsum('bhij,bhjd->bhid', attn, v_c)
        out = out.transpose(0, 2, 1, 3).reshape(b, n, DIM_INNER)
        return out @ w_out

    def _L0_ffn_ref(x, Wuz, buz, Wwz, bwz, Wur, bur, Wwr, bwr, Wu, bu, Ww, bw, Wo, bo):
        import jax, jax.numpy as jnp
        import numpy as np
        B, T, D, H = (64, 128, 128, 256)

        def _linear_params(key, out_dim, in_dim):
            kw, kb = jax.random.split(key)
            bound = 1.0 / np.sqrt(in_dim)
            W = jax.random.uniform(kw, (out_dim, in_dim), jnp.float32, -bound, bound)
            b = jax.random.uniform(kb, (out_dim,), jnp.float32, -bound, bound)
            return (W, b)
        b_, t_, _ = x.shape
        h_dim = Wwz.shape[0]
        xz = (jnp.einsum('btd,hd->bth', x, Wuz) + buz).transpose(1, 0, 2)
        xr = (jnp.einsum('btd,hd->bth', x, Wur) + bur).transpose(1, 0, 2)
        xc = (jnp.einsum('btd,hd->bth', x, Wu) + bu).transpose(1, 0, 2)

        def step(h, inp):
            xz_t, xr_t, xc_t = inp
            z = jax.nn.sigmoid(xz_t + h @ Wwz.T + bwz)
            r = jax.nn.sigmoid(xr_t + h @ Wwr.T + bwr)
            c = jnp.tanh(xc_t + h * r @ Ww.T + bw)
            h_new = z * h + (1.0 - z) * c
            return (h_new, h_new)
        h0 = jnp.zeros((b_, h_dim), x.dtype)
        _, hs = jax.lax.scan(step, h0, (xz, xr, xc))
        out = jax.nn.sigmoid(jnp.einsum('tbh,dh->btd', hs, Wo) + bo)
        return out

    def _L1_attn_ref(x, Wqkv, bqkv, Wo, bo, Wf, bf):
        import jax, jax.numpy as jnp
        import numpy as np
        B, S, D, H = (16, 256, 128, 8)
        SCALES = (5, 10, None)

        def _window_bias(seq_len, scale):
            i = jnp.arange(seq_len)
            d = i[:, None] - i[None, :]
            allowed = (d >= 0) & (d < scale)
            return jnp.where(allowed, 0.0, -jnp.inf).astype(jnp.float32)

        def _mha(x, Wqkv, bqkv, Wo, bo, bias):
            b, s, d = x.shape
            hd = d // H
            qkv = x @ Wqkv.T + bqkv
            q, k, v = jnp.split(qkv, 3, axis=-1)
            q = q.reshape(b, s, H, hd) * (1.0 / np.sqrt(hd)).astype(x.dtype)
            k = k.reshape(b, s, H, hd)
            v = v.reshape(b, s, H, hd)
            scores = jnp.einsum('bqhd,bkhd->bhqk', q, k)
            if bias is not None:
                scores = scores + bias
            p = jax.nn.softmax(scores, axis=-1)
            o = jnp.einsum('bhqk,bkhd->bqhd', p, v).reshape(b, s, d)
            return o @ Wo.T + bo
        s = x.shape[1]
        outs = []
        for i, scale in enumerate(SCALES):
            bias = None if scale is None else _window_bias(s, scale)
            outs.append(_mha(x, Wqkv[i], bqkv[i], Wo[i], bo[i], bias))
        combined = jnp.concatenate(outs, axis=-1)
        return combined @ Wf.T + bf

    def _L1_ffn_ref(x, ln_g, ln_b, w_r, b_r, W1, b1, W2, b2):
        import jax, jax.numpy as jnp
        import numpy as np
        D = 128
        E = 8
        K = 2
        EXP = 4
        LN_EPS = 1e-05
        B, T, d = x.shape
        mu = jnp.mean(x, axis=-1, keepdims=True)
        var = jnp.mean(jnp.square(x - mu), axis=-1, keepdims=True)
        h = (x - mu) * jax.lax.rsqrt(var + LN_EPS) * ln_g + ln_b
        logits = jnp.einsum('btd,ed->bte', h, w_r) + b_r
        topk_vals, topk_idx = jax.lax.top_k(logits, K)
        gates = jax.nn.softmax(topk_vals, axis=-1)
        hf = h.reshape(B * T, d)
        hid = jax.nn.gelu(jnp.einsum('nd,edf->nef', hf, W1) + b1, approximate=False)
        expert_stack = jnp.einsum('nef,efd->ned', hid, W2) + b2
        idx_flat = topk_idx.reshape(B * T, K)
        gates_flat = gates.reshape(B * T, K)
        gathered = jnp.take_along_axis(expert_stack, idx_flat[:, :, None], axis=1)
        mixed = jnp.sum(gathered * gates_flat[:, :, None], axis=1).reshape(B, T, d)
        return x + mixed

    def _L2_attn_ref(x, W_in, b_in, W_out, b_out, A, B, gamma, beta):
        import jax, jax.numpy as jnp
        import numpy as np
        T, BATCH, DIM = (512, 32, 128)

        def _layernorm(y, gamma, beta, eps=1e-05):
            mu = jnp.mean(y, axis=-1, keepdims=True)
            var = jnp.mean(jnp.square(y - mu), axis=-1, keepdims=True)
            return (y - mu) * jax.lax.rsqrt(var + eps) * gamma + beta
        zg = jnp.einsum('tbd,ed->tbe', x, W_in) + b_in
        z, g = jnp.split(zg, 2, axis=-1)
        g = jax.nn.sigmoid(g)
        Bz = B * z
        gA = g * A

        def step(prev, inp):
            ga_t, bz_t = inp
            curr = ga_t * prev + bz_t
            return (curr, curr)
        h0 = jnp.zeros((x.shape[1], x.shape[2]), dtype=x.dtype)
        _, h = jax.lax.scan(step, h0, (gA, Bz))
        out = jnp.einsum('tbd,ed->tbe', h, W_out) + b_out
        return _layernorm(x + out, gamma, beta)

    def _L2_ffn_ref(x, router_w1, router_b1, router_w2, router_b2, norm_s_w, norm_s_b, norm_t_w, norm_t_b, sp_in_w, sp_in_b, sp_out_w, sp_out_b, tq_w, tq_b, tk_w, tk_b, tv_w, tv_b, tp_w, tp_b, cross_in_w, cross_in_b, cross_out_w, cross_out_b, norm_mlp_w, norm_mlp_b, mlp_w1, mlp_b1, mlp_w2, mlp_b2):
        import jax, jax.numpy as jnp
        import numpy as np
        D = 128
        H = 8
        K = 4
        HD = D // H

        def _ln(x, w, b, eps=1e-05):
            m = x.mean(-1, keepdims=True)
            v = ((x - m) ** 2).mean(-1, keepdims=True)
            return (x - m) / jnp.sqrt(v + eps) * w + b

        def _spatial_experts(xn, idx, in_w, in_b, out_w, out_b):
            W = in_w[idx]
            qkv = jnp.einsum('btd,bed->bte', xn, W) + in_b[idx][:, None, :]
            q, k, v = jnp.split(qkv, 3, axis=-1)
            B, T, _ = xn.shape
            q = q.reshape(B, T, H, HD) * HD ** (-0.5)
            k = k.reshape(B, T, H, HD)
            v = v.reshape(B, T, H, HD)
            att = jax.nn.softmax(jnp.einsum('bthd,bshd->bhts', q, k), axis=-1)
            o = jnp.einsum('bhts,bshd->bthd', att, v).reshape(B, T, D)
            return jnp.einsum('btd,bod->bto', o, out_w[idx]) + out_b[idx][:, None, :]

        def _temporal_experts(xt, idx, qw, qb, kw, kb, vw, vb, pw, pb):
            B, T, _ = xt.shape
            q = (jnp.einsum('btd,bod->bto', xt, qw[idx]) + qb[idx][:, None, :]).reshape(B, T, H, HD)
            k = (jnp.einsum('btd,bod->bto', xt, kw[idx]) + kb[idx][:, None, :]).reshape(B, T, H, HD)
            v = (jnp.einsum('btd,bod->bto', xt, vw[idx]) + vb[idx][:, None, :]).reshape(B, T, H, HD)
            logits = jnp.einsum('bthd,bshd->bhts', q, k) * HD ** (-0.5)
            causal = jnp.tril(jnp.ones((T, T), dtype=bool))
            logits = jnp.where(causal, logits, -jnp.inf)
            att = jax.nn.softmax(logits, axis=-1)
            o = jnp.einsum('bhts,bshd->bthd', att, v).reshape(B, T, D)
            o = jnp.einsum('btd,bod->bto', o, pw[idx]) + pb[idx][:, None, :]
            return xt + o

        def _cross_mha(q_in, kv_in, in_w, in_b, out_w, out_b):
            B, T, _ = q_in.shape
            S = kv_in.shape[1]
            Wq, Wk, Wv = (in_w[:D], in_w[D:2 * D], in_w[2 * D:])
            bq, bk, bv = (in_b[:D], in_b[D:2 * D], in_b[2 * D:])
            q = (q_in @ Wq.T + bq).reshape(B, T, H, HD) * HD ** (-0.5)
            k = (kv_in @ Wk.T + bk).reshape(B, S, H, HD)
            v = (kv_in @ Wv.T + bv).reshape(B, S, H, HD)
            att = jax.nn.softmax(jnp.einsum('bthd,bshd->bhts', q, k), axis=-1)
            o = jnp.einsum('bhts,bshd->bthd', att, v).reshape(B, T, D)
            return o @ out_w.T + out_b
        pooled = x.mean(axis=1)
        h = jax.nn.gelu(pooled @ router_w1.T + router_b1, approximate=False)
        route = jax.nn.softmax(h @ router_w2.T + router_b2, axis=-1)
        idx_s = jnp.argmax(route[:, :K], axis=-1)
        idx_t = jnp.argmax(route[:, K:], axis=-1)
        xn = _ln(x, norm_s_w, norm_s_b)
        spatial_out = _spatial_experts(xn, idx_s, sp_in_w, sp_in_b, sp_out_w, sp_out_b)
        xt = _ln(x, norm_t_w, norm_t_b)
        temporal_out = _temporal_experts(xt, idx_t, tq_w, tq_b, tk_w, tk_b, tv_w, tv_b, tp_w, tp_b)
        fused = _cross_mha(spatial_out, temporal_out, cross_in_w, cross_in_b, cross_out_w, cross_out_b)
        x = x + fused
        h2 = _ln(x, norm_mlp_w, norm_mlp_b)
        x = x + (jax.nn.gelu(h2 @ mlp_w1.T + mlp_b1, approximate=False) @ mlp_w2.T + mlp_b2)
        return x

    def _L3_attn_ref(x, Wq, Wk, Wv, rel_pos_bias):
        import jax, jax.numpy as jnp
        import numpy as np
        NUM_HEADS = 8
        WINDOW = 64
        B, T, D = x.shape
        H = NUM_HEADS
        hd = D // H
        scale = hd ** (-0.5)
        q = (x @ Wq.T).reshape(B, T, H, hd).transpose(0, 2, 1, 3)
        k = (x @ Wk.T).reshape(B, T, H, hd).transpose(0, 2, 1, 3)
        v = (x @ Wv.T).reshape(B, T, H, hd).transpose(0, 2, 1, 3)
        pos = jnp.arange(T)
        rel = jnp.clip(pos[:, None] - pos[None, :], -(WINDOW - 1), WINDOW - 1) + (WINDOW - 1)
        bias = rel_pos_bias[0][:, rel]
        scores = jnp.einsum('bhid,bhjd->bhij', q, k) * scale + bias[None]
        attn = jax.nn.softmax(scores, axis=-1)
        out = jnp.einsum('bhij,bhjd->bhid', attn, v)
        return out.transpose(0, 2, 1, 3).reshape(B, T, D)

    def _L3_ffn_ref(x, gate_w, thr_w, fc1_w, lora_A, lora_B, fc2_w):
        import jax, jax.numpy as jnp
        import numpy as np
        B, T, H = (8, 2048, 128)
        E, R = (4, 16)
        SCALE = 0.04
        b, t, h = x.shape
        e = gate_w.shape[0]
        xf = x.reshape(-1, h)
        gate_logits = jax.nn.softmax(xf @ gate_w.T, axis=-1)
        thresholds = jax.nn.sigmoid(xf @ thr_w.T) * (1.0 / e)
        adapted = gate_logits - thresholds
        selected = (adapted >= 0).astype(xf.dtype)
        weights = adapted * selected
        wsum = jnp.sum(weights, axis=-1, keepdims=True)
        wsum = jnp.where(wsum == 0, jnp.ones_like(wsum), wsum)
        weights = weights / wsum
        hidden = jax.nn.relu(jnp.einsum('ni,ehi->neh', xf, fc1_w))
        lo = jnp.einsum('neh,ehr->ner', hidden, lora_A)
        lo = jnp.einsum('ner,ero->neo', lo, lora_B)
        expert_out = jnp.einsum('neo,edo->ned', lo, fc2_w)
        out = jnp.einsum('ne,ned->nd', weights, expert_out)
        return out.reshape(b, t, h)
    h = _L0_tok_ref(x, L0_tok_W, L0_tok_b)
    h = h + _L0_attn_ref(_layernorm(h, axis=-1), L0_attn_w_q_u, L0_attn_w_k_u, L0_attn_w_v_u, L0_attn_w_q_c, L0_attn_w_k_c, L0_attn_w_v_c, L0_attn_w_out)
    h = h + _L0_ffn_ref(_layernorm(h, axis=-1), L0_ffn_Wuz, L0_ffn_buz, L0_ffn_Wwz, L0_ffn_bwz, L0_ffn_Wur, L0_ffn_bur, L0_ffn_Wwr, L0_ffn_bwr, L0_ffn_Wu, L0_ffn_bu, L0_ffn_Ww, L0_ffn_bw, L0_ffn_Wo, L0_ffn_bo)
    h = h + _L1_attn_ref(_layernorm(h, axis=-1), L1_attn_Wqkv, L1_attn_bqkv, L1_attn_Wo, L1_attn_bo, L1_attn_Wf, L1_attn_bf)
    h = h + _L1_ffn_ref(_layernorm(h, axis=-1), L1_ffn_ln_g, L1_ffn_ln_b, L1_ffn_w_r, L1_ffn_b_r, L1_ffn_W1, L1_ffn_b1, L1_ffn_W2, L1_ffn_b2)
    h = h + _L2_attn_ref(_layernorm(h, axis=-1), L2_attn_W_in, L2_attn_b_in, L2_attn_W_out, L2_attn_b_out, L2_attn_A, L2_attn_B, L2_attn_gamma, L2_attn_beta)
    h = h + _L2_ffn_ref(_layernorm(h, axis=-1), L2_ffn_router_w1, L2_ffn_router_b1, L2_ffn_router_w2, L2_ffn_router_b2, L2_ffn_norm_s_w, L2_ffn_norm_s_b, L2_ffn_norm_t_w, L2_ffn_norm_t_b, L2_ffn_sp_in_w, L2_ffn_sp_in_b, L2_ffn_sp_out_w, L2_ffn_sp_out_b, L2_ffn_tq_w, L2_ffn_tq_b, L2_ffn_tk_w, L2_ffn_tk_b, L2_ffn_tv_w, L2_ffn_tv_b, L2_ffn_tp_w, L2_ffn_tp_b, L2_ffn_cross_in_w, L2_ffn_cross_in_b, L2_ffn_cross_out_w, L2_ffn_cross_out_b, L2_ffn_norm_mlp_w, L2_ffn_norm_mlp_b, L2_ffn_mlp_w1, L2_ffn_mlp_b1, L2_ffn_mlp_w2, L2_ffn_mlp_b2)
    h = h + _L3_attn_ref(_layernorm(h, axis=-1), L3_attn_Wq, L3_attn_Wk, L3_attn_Wv, L3_attn_rel_pos_bias)
    h = h + _L3_ffn_ref(_layernorm(h, axis=-1), L3_ffn_gate_w, L3_ffn_thr_w, L3_ffn_fc1_w, L3_ffn_lora_A, L3_ffn_lora_B, L3_ffn_fc2_w)
    return h

_drawn_inputs = setup_inputs


def setup_inputs(seed=0):
    import zlib

    import numpy as np

    out = dict(_drawn_inputs(seed))
    spreads = {'L1_ffn_ln_g': (1.0, 0.2),
     'L1_ffn_ln_b': (0.0, 0.1),
     'L1_ffn_b_r': (0.0, 0.428),
     'L1_ffn_b1': (0.0, 0.1),
     'L1_ffn_b2': (0.0, 0.1),
     'L2_attn_gamma': (1.0, 0.2),
     'L2_attn_beta': (0.0, 0.268),
     'L2_ffn_router_b1': (0.0, 0.1),
     'L2_ffn_router_b2': (0.0, 0.8),
     'L2_ffn_norm_s_w': (1.0, 0.6),
     'L2_ffn_norm_s_b': (0.0, 0.8),
     'L2_ffn_norm_t_w': (1.0, 0.6),
     'L2_ffn_norm_t_b': (0.0, 0.8),
     'L2_ffn_sp_in_b': (0.0, 0.8),
     'L2_ffn_sp_out_b': (0.0, 0.8),
     'L2_ffn_tq_b': (0.0, 0.8),
     'L2_ffn_tk_b': (0.0, 2.0),
     'L2_ffn_tv_b': (0.0, 0.8),
     'L2_ffn_tp_b': (0.0, 0.8),
     'L2_ffn_cross_in_b': (0.0, 0.8),
     'L2_ffn_cross_out_b': (0.0, 1.137),
     'L2_ffn_norm_mlp_w': (1.0, 0.6),
     'L2_ffn_norm_mlp_b': (0.0, 0.8),
     'L2_ffn_mlp_b1': (0.0, 0.8),
     'L2_ffn_mlp_b2': (0.0, 0.317)}
    factors = {'L0_attn_w_q_u': 8.0,
     'L0_attn_w_k_u': 8.0,
     'L0_attn_w_v_u': 8.0,
     'L0_attn_w_q_c': 8.0,
     'L0_attn_w_k_c': 8.0,
     'L0_ffn_Wuz': 3.838,
     'L0_ffn_buz': 8.0,
     'L0_ffn_Wwz': 8.0,
     'L0_ffn_bwz': 8.0,
     'L0_ffn_Wur': 8.0,
     'L0_ffn_bur': 8.0,
     'L0_ffn_Wwr': 8.0,
     'L0_ffn_bwr': 8.0,
     'L0_ffn_bu': 8.0,
     'L0_ffn_Ww': 4.752,
     'L0_ffn_bw': 7.155,
     'L0_ffn_bo': 4.454,
     'L1_attn_Wqkv': 4.966,
     'L1_attn_bqkv': 8.0,
     'L1_attn_Wo': 4.925,
     'L1_attn_bo': 5.051,
     'L1_attn_Wf': 3.445,
     'L2_attn_W_in': 4.976,
     'L2_attn_b_in': 8.0,
     'L2_attn_W_out': 4.901,
     'L2_attn_b_out': 3.178,
     'L2_attn_A': 8.0,
     'L2_attn_B': 4.72,
     'L2_ffn_sp_in_w': 8.0,
     'L2_ffn_sp_out_w': 8.0,
     'L2_ffn_tq_w': 8.0,
     'L2_ffn_tk_w': 8.0,
     'L2_ffn_tv_w': 8.0,
     'L2_ffn_tp_w': 8.0,
     'L2_ffn_cross_in_w': 8.0,
     'L2_ffn_cross_out_w': 8.0,
     'L2_ffn_mlp_w1': 4.22,
     'L2_ffn_mlp_w2': 3.873,
     'L3_ffn_gate_w': 8.0,
     'L3_ffn_thr_w': 8.0,
     'L3_ffn_fc1_w': 8.0,
     'L3_ffn_lora_A': 8.0,
     'L3_ffn_lora_B': 8.0,
     'L3_ffn_fc2_w': 8.0,
     'L3_attn_Wq': 4.702,
     'L3_attn_Wk': 4.615,
     'L3_attn_rel_pos_bias': 3.969}
    for name, (base, spread) in spreads.items():
        noise = np.random.default_rng([zlib.crc32(name.encode()), seed]).standard_normal(out[name].shape)
        drawn = base * np.exp(spread * noise) if base else spread * noise
        out[name] = jnp.asarray(drawn.astype(out[name].dtype))
    for name, factor in factors.items():
        out[name] = (out[name] * factor).astype(out[name].dtype)
    return out
```

```python
from contextlib import ExitStack

import numpy as np

import concourse.bass as bass
from concourse import mybir

F32 = mybir.dt.float32
U32 = mybir.dt.uint32
ALU = mybir.AluOpType
ACT = mybir.ActivationFunctionType
AX_X = mybir.AxisListType.X

P = 128
D = 128
B = 64
S_IN = 256
BLOCK = 128
TOP = 16
T = S_IN // BLOCK * TOP
TOK = B * T
CH = 512
NCH = TOK // CH
CB = CH // T
NT = CH // P
E1 = 8
E2 = 4
E3 = 4
R3 = 16
EPS = 1e-5
NEG = -1e30
WIDE = 2.0 ** -10
XG = 8



def _blocks(w):
    k = w.shape[0] // P
    return w.reshape(k, P, w.shape[1]).transpose(1, 0, 2).reshape(P, k * w.shape[1])


def _rows(w):
    out = np.zeros((P, w.shape[1]), w.dtype)
    out[: w.shape[0]] = w
    return out


def _cols(v):
    return v.reshape(-1, P).T


def _adapter_a(w):
    out = np.zeros((P, E3 * R3 * E3), w.dtype)
    for e in range(E3):
        at = e * E3 * R3 + e * R3
        out[:, at:at + R3] = w[e]
    return out


def _adapter_b(w):
    out = np.zeros((P, E3 * D), w.dtype)
    for e in range(E3):
        out[e * R3:(e + 1) * R3, e * D:(e + 1) * D] = w[e]
    return out


def _relative(w):
    i, j = np.arange(T)[:, None], np.arange(T)[None, :]
    m = w[0][:, i - j + 63].reshape(2, 4, T, T)
    return m.transpose(1, 2, 0, 3).reshape(P, 2 * T)


def weight_list():
    w = []

    def add(name, n, lay):
        w.append((name, n, lay))
    for n in ("q_u", "k_u", "v_u", "q_c", "k_c", "v_c"):
        add(n, 512, lambda a, n=n: a["L0_attn_w_" + n])
    add("l0_out", 512, lambda a: _blocks(a["L0_attn_w_out"]))
    for n in ("uz", "ur", "u"):
        add("g_" + n, 256, lambda a, n=n: a["L0_ffn_W" + n].T)
    for n in ("wz", "wr", "w"):
        add("g_" + n, 512, lambda a, n=n: _blocks(a["L0_ffn_W" + n].T))
    add("g_o", 256, lambda a: _blocks(a["L0_ffn_Wo"].T))
    for s in range(3):
        add(f"l1_qkv{s}", 384, lambda a, s=s: a["L1_attn_Wqkv"][s].T)
        add(f"l1_o{s}", 128, lambda a, s=s: a["L1_attn_Wo"][s].T)
    add("l1_f", 384, lambda a: _blocks(a["L1_attn_Wf"].T))
    add("moe_r", 8, lambda a: a["L1_ffn_w_r"].T)
    add("moe_br", 8, lambda a: _rows(a["L1_ffn_b_r"][None]))
    add("moe_b2", 128, lambda a: _rows(a["L1_ffn_b2"]))
    for e in range(E1):
        add(f"moe_1_{e}", 512, lambda a, e=e: a["L1_ffn_W1"][e])
        add(f"moe_2_{e}", 512, lambda a, e=e: _blocks(a["L1_ffn_W2"][e]))
    add("l2_in", 256, lambda a: a["L2_attn_W_in"].T)
    add("l2_out", 128, lambda a: a["L2_attn_W_out"].T)
    add("rt_1", 128, lambda a: a["L2_ffn_router_w1"].T)
    add("rt_2", 8, lambda a: a["L2_ffn_router_w2"].T)
    add("rt_b2", 8, lambda a: _rows(a["L2_ffn_router_b2"][None]))
    for e in range(E2):
        add(f"sp_q{e}", 128, lambda a, e=e: a["L2_ffn_sp_in_w"][e][:D].T)
        add(f"sp_k{e}", 128, lambda a, e=e: a["L2_ffn_sp_in_w"][e][D:2 * D].T)
        add(f"sp_v{e}", 128, lambda a, e=e: a["L2_ffn_sp_in_w"][e][2 * D:].T)
        add(f"sp_o{e}", 128, lambda a, e=e: a["L2_ffn_sp_out_w"][e].T)
        for n in "qkvp":
            add(f"t{n}_{e}", 128, lambda a, e=e, n=n: a[f"L2_ffn_t{n}_w"][e].T)
    add("sp_in_b", 384, lambda a: _rows(a["L2_ffn_sp_in_b"]))
    add("sp_out_b", 128, lambda a: _rows(a["L2_ffn_sp_out_b"]))
    for n in "qkvp":
        add(f"t{n}_b", 128, lambda a, n=n: _rows(a[f"L2_ffn_t{n}_b"]))
    add("cr_in", 384, lambda a: a["L2_ffn_cross_in_w"].T)
    add("cr_out", 128, lambda a: a["L2_ffn_cross_out_w"].T)
    add("mlp_1", 512, lambda a: a["L2_ffn_mlp_w1"].T)
    add("mlp_2", 512, lambda a: _blocks(a["L2_ffn_mlp_w2"].T))
    for n in "qkv":
        add("l3_" + n, 128, lambda a, n=n: a["L3_attn_W" + n].T)
    add("l3_rel", 2 * T, lambda a: _relative(a["L3_attn_rel_pos_bias"]))
    add("l3_gate", 4, lambda a: a["L3_ffn_gate_w"].T)
    add("l3_thr", 1, lambda a: a["L3_ffn_thr_w"].T)
    for e in range(E3):
        add(f"fc1_{e}", 128, lambda a, e=e: a["L3_ffn_fc1_w"][e].T)
        add(f"fc2_{e}", 128, lambda a, e=e: a["L3_ffn_fc2_w"][e].T)
    add("lora_a", E3 * E3 * R3, lambda a: _adapter_a(a["L3_ffn_lora_A"]))
    add("lora_b", E3 * D, lambda a: _adapter_b(a["L3_ffn_lora_B"]))
    add("tok_w", D, lambda a: np.broadcast_to(a["L0_tok_W"], (P, D)))
    add("tok_b", 1, lambda a: np.broadcast_to(a["L0_tok_b"][None], (P, 1)))
    for n in ("buz", "bwz", "bur", "bwr", "bu", "bw"):
        add(n, 2, lambda a, n=n: _cols(a["L0_ffn_" + n]))
    add("g_bo", 1, lambda a: _cols(a["L0_ffn_bo"]))
    for s in range(3):
        add(f"l1_bqkv{s}", 3, lambda a, s=s: _cols(a["L1_attn_bqkv"][s]))
        add(f"l1_bo{s}", 1, lambda a, s=s: _cols(a["L1_attn_bo"][s]))
    add("l1_bf", 1, lambda a: _cols(a["L1_attn_bf"]))
    add("ln_g", 1, lambda a: _cols(a["L1_ffn_ln_g"]))
    add("ln_b", 1, lambda a: _cols(a["L1_ffn_ln_b"]))
    add("moe_b1", 4 * E1, lambda a: _cols(a["L1_ffn_b1"].reshape(-1)))
    add("l2_bin", 2, lambda a: _cols(a["L2_attn_b_in"]))
    for n in ("b_out", "A", "B", "gamma", "beta"):
        add("l2_" + n, 1, lambda a, n=n: _cols(a["L2_attn_" + n]))
    for n in ("router_b1", "norm_s_w", "norm_s_b", "norm_t_w", "norm_t_b", "norm_mlp_w", "norm_mlp_b",
              "cross_out_b", "mlp_b2"):
        add(n, 1, lambda a, n=n: _cols(a["L2_ffn_" + n]))
    add("cross_in_b", 3, lambda a: _cols(a["L2_ffn_cross_in_b"]))
    add("mlp_b1", 4, lambda a: _cols(a["L2_ffn_mlp_b1"]))
    return w


VECTORS_FROM, SECOND_FROM, THIRD_FROM = "tok_w", "l2_in", "l3_q"


def constant_list():
    p = np.arange(P)
    row = p % T
    j, q = np.arange(T), np.arange(4)
    f = np.arange(P)
    later = (j[None, :] >= row[:, None])
    same = (p[:, None] // 32 == q[None, :])

    def band(width):
        d = row[:, None] - j[None, :]
        return np.where((d >= 0) & (d < width), 0.0, NEG)
    return [
        ("ident", np.eye(P)),
        ("mean", np.full((P, P), 1.0 / P)),
        ("half", p[:, None] // 64 == np.arange(2)[None]),
        ("head", (p[:, None] // 16) % 4 == q[None]),
        ("v16", (f[None] // 16) % 4 == p[:, None] // 32),
        ("v64", f[None] // 64 == (p[:, None] // 32) % 2),
        ("t1m", (same[:, :, None] * later[:, None, :] * 0.125).reshape(P, P)),
        ("sgm", row[:, None] > j[None, :]),
        ("causal", band(T)), ("band5", band(5)), ("band10", band(10)),
        ("base", p[:, None] * BLOCK),
        ("iota8", np.broadcast_to(np.arange(8), (P, 8))),
        ("row0", np.broadcast_to(p[:, None] == 0, (P, P))),
        ("pick", (p[:, None, None] == q[None, :, None]) * np.ones((1, 1, P))),
        ("eps", np.full((P, 1), EPS)),
        ("eps_wide", np.full((P, 1), EPS * WIDE ** 2)),
        ("zero", np.zeros((P, 1))),
    ]


def offsets(items):
    at, out = 0, {}
    for name, n in items:
        out[name] = (at, n)
        at += n
    return out, at


W_AT, W_COLS = offsets([(n, c) for n, c, _ in weight_list()])
C_AT, C_COLS = offsets([(n, int(np.prod(np.asarray(a).shape[1:]))) for n, a in constant_list()])


class Steps:

    def __init__(self, known):
        self.known = known
        self.table, self.banks, self.sems, self.log = {}, {}, {}, {}

    def begin(self, who, stage):
        self.who, self.stage, self.count = who, stage, 0

    def did(self, key):
        self.count += 1
        assert (self.stage, key) not in self.table, (self.stage, key)
        self.table[self.stage, key] = (self.who, self.count)
        self.log.setdefault((self.stage, self.who), []).append(("did", key))
        return self.sems[self.stage, self.who], 1

    def after(self, key):
        self.log.setdefault((self.stage, self.who), []).append(("after", key))
        by, n = self.known.table[self.stage, key] if self.known else (ENGINES[0], 1)
        return self.sems[self.stage, by], n

    def last(self):
        return self.sems[self.stage, self.who], self.count

    def check_order(self):
        for stage in dict.fromkeys(s for s, _ in self.log):
            lists = {w: l for (s, w), l in self.log.items() if s == stage}
            at, done = dict.fromkeys(lists, 0), set()
            moved = True
            while moved:
                moved = False
                for w, l in lists.items():
                    while at[w] < len(l) and (l[at[w]][0] == "did" or l[at[w]][1] in done):
                        if l[at[w]][0] == "did":
                            done.add(l[at[w]][1])
                        at[w] += 1
                        moved = True
            stuck = {w: l[at[w]] for w, l in lists.items() if at[w] < len(l)}
            assert not stuck, (stage, stuck)


STAGES = ["select", "l0_attention", "gru_input", "gru_start", "gru", "gru_output", "l1_attention", "experts",
          "l2_input", "l2_scan", "l2_output", "pool", "route", "l2_spatial", "l2_temporal", "l2_cross", "l2_mlp",
          "l3_attention", "l3_experts", "write"]
ENGINES = ("tensor", "vector", "scalar", "gpsimd")


def tower(nc, x, weights, constants, out, known):
    steps = Steps(known)
    did, after, last = steps.did, steps.after, steps.last
    with ExitStack() as ctx:
        def sem(name):
            return ctx.enter_context(nc.semaphore(name))

        h = ctx.enter_context(nc.sbuf_tensor("h", [P, TOK], F32))
        ln2 = ctx.enter_context(nc.sbuf_tensor("ln2", [P, TOK], F32))
        vec_at, second_at = W_AT[VECTORS_FROM][0], W_AT[SECOND_FROM][0]
        wt = ctx.enter_context(nc.sbuf_tensor("wt", [P, second_at], F32))
        third_at, experts_at = W_AT[THIRD_FROM][0], W_AT["moe_r"][0]
        assert third_at - second_at <= experts_at
        vec = ctx.enter_context(nc.sbuf_tensor("vec", [P, W_COLS - vec_at], F32))
        cs = ctx.enter_context(nc.sbuf_tensor("cs", [P, C_COLS], F32))
        arena = ctx.enter_context(nc.sbuf_tensor("arena", [P, 18432], F32))
        psum = ctx.enter_context(nc.psum_tensor("psum", [P, 8, 512], F32))
        small = ctx.enter_context(nc.sbuf_tensor("small", [P, 880], F32))

        for s in STAGES:
            for who in ENGINES:
                steps.sems[s, who] = sem(f"{s}_{who}_done")
        x_loaded = [sem("x_loaded0"), sem("x_loaded1")]
        c_loaded, w_loaded = sem("constants_loaded"), sem("weights_loaded")
        gathered, stored = sem("rows_gathered"), [sem("output_stored0"), sem("output_stored1")]
        arrived = sem("engines_arrived")
        go = {who: sem(f"{who}_may_go") for who in ENGINES}

        def W(name, a=0, b=None):
            at, n = W_AT[name]
            b = n if b is None else b
            if at >= vec_at:
                return vec[:, at - vec_at + a:at - vec_at + b]
            if at >= third_at:
                at += experts_at - third_at
            elif at >= second_at:
                at -= second_at
            return wt[:, at + a:at + b]

        def C(name, a=0, b=None):
            at, n = C_AT[name]
            return cs[:, at + a:at + (n if b is None else b)]

        class Places:

            def __init__(self, buf, size):
                self.buf, self.at, self.size = buf, 0, size

            def take(self, n):
                a = self.at
                self.at += n
                assert self.at <= self.size, (self.at, self.size)
                return self.buf[:, a:a + n]

        def new_arena():
            return Places(arena, 18432)
        keep = Places(small, 880)

        def meet(eng, who, stage):
            eng.drain()
            eng.sem_inc(arrived, 1)
            eng.wait_ge(go[who], 1)
            eng.sem_clear(go[who])

        def lead(sp, stage):
            sp.wait_ge(arrived, len(ENGINES))
            sp.sem_clear(arrived)
            for who in ENGINES:
                sp.sem_clear(steps.sems[stage, who])
            for who in ENGINES:
                sp.sem_inc(go[who], 1)

        ring = {"next": 0, "reader": {}}

        def fill(pe, key, reader):
            b = ring["next"]
            ring["next"] = (b + 1) % 8
            if b in ring["reader"]:
                pe.wait_ge(*after(ring["reader"][b]))
            ring["reader"][b] = reader
            steps.banks[steps.stage, key] = b
            return psum[:, b, :]

        def bank(who, key):
            if steps.known is None:
                return psum[:, 0, :]
            return psum[:, steps.known.banks[steps.stage, key], :]

        def begin(who, stage):
            steps.begin(who, stage)
            if who == "tensor":
                ring["next"], ring["reader"] = 0, {}

        def ln_tensor(pe, k, src, ready):
            ps = fill(pe, f"{k}.mean", f"{k}.xc")
            for step in ready:
                pe.wait_ge(*after(step))
            pe.matmul(ps, C("mean"), src, start=True, stop=True).then_inc(*did(f"{k}.mean"))
            ps = fill(pe, f"{k}.var", f"{k}.log")
            pe.wait_ge(*after(f"{k}.sq"))
            pe.matmul(ps, C("mean"), ln_sq, start=True, stop=True).then_inc(*did(f"{k}.var"))

        def ln_vector(v, k, src, dst, ready=(), before=(), wide=False):
            v.wait_ge(*after(f"{k}.mean"))
            for step in ready:
                v.wait_ge(*after(step))
            v.wait_ge(*last())
            v.tensor_tensor(ln_xc, src, bank("vector", f"{k}.mean"), ALU.subtract).then_inc(*did(f"{k}.xc"))
            if wide:
                v.wait_ge(*after(f"{k}.var"))
                v.wait_ge(*last())
                v.tensor_scalar(ln_sq, bank("vector", f"{k}.var"), 2.0 ** 128 * WIDE ** 2 / P, None,
                                ALU.is_lt).then_inc(*did(f"{k}.fits"))
                v.wait_ge(*after(f"{k}.log"))
                v.reciprocal(ln_rs, ln_rs).then_inc(*did(f"{k}.rstd"))
                v.wait_ge(*last())
                v.tensor_tensor(ln_rs, ln_rs, ln_sq, ALU.mult).then_inc(*did(f"{k}.zeroed"))
                v.wait_ge(*last())
                v.scalar_tensor_tensor(out=dst, in0=ln_xc, scalar=WIDE, in1=ln_rs, op0=ALU.mult,
                                       op1=ALU.mult).then_inc(*did(f"{k}.n"))
                return
            v.wait_ge(*after(f"{k}.rstd"))
            for step in before:
                v.wait_ge(*after(step))
            v.wait_ge(*last())
            v.tensor_tensor(dst, ln_xc, ln_rs, ALU.mult).then_inc(*did(f"{k}.n"))

        def ln_scalar(a, k, wide=False):
            a.wait_ge(*after(f"{k}.xc"))
            a.wait_ge(*last())
            a.activation(ln_sq, ln_xc, ACT.Square, scale=WIDE if wide else 1.0).then_inc(*did(f"{k}.sq"))
            a.wait_ge(*after(f"{k}.fits" if wide else f"{k}.var"))
            a.wait_ge(*last())
            if wide:
                a.activation(ln_rs, bank("scalar", f"{k}.var"), ACT.Sqrt,
                             bias=C("eps_wide")).then_inc(*did(f"{k}.log"))
                return
            a.activation(ln_rs, bank("scalar", f"{k}.var"), ACT.Ln, bias=C("eps")).then_inc(*did(f"{k}.log"))
            a.wait_ge(*last())
            a.activation(ln_rs, ln_rs, ACT.Exp, scale=-0.5, bias=C("zero")).then_inc(*did(f"{k}.rstd"))

        ln_buf = ctx.enter_context(nc.sbuf_tensor("ln_buf", [P, 3, CH], F32))
        ln_xc, ln_sq, ln_rs = ln_buf[:, 0, :], ln_buf[:, 1, :], ln_buf[:, 2, :]
        hc = ctx.enter_context(nc.sbuf_tensor("hc", [P, CH], F32))[:, :]
        xn = ctx.enter_context(nc.sbuf_tensor("xn", [P, CH], F32))[:, :]

        def mm(pe, key, reader, needs, products):
            ps = fill(pe, key, reader)
            for step in needs:
                pe.wait_ge(*after(step))
            n = len(products)
            for i, (lhs, rhs) in enumerate(products):
                m = lhs.shape[1]
                ins = pe.matmul(ps[0:m, 0:rhs.shape[-1]] if len(rhs.shape) == 2 else ps[0:m, :].rearrange("p (a b) -> p a b", b=rhs.shape[-1]),
                                lhs, rhs, start=i == 0, stop=i == n - 1)
            ins.then_inc(*did(key))

        HB = lambda ap: ap.rearrange("p (b t) -> p b t", t=T)

        ar = new_arena()
        xin = [ar.take(2048), ar.take(2048)]
        prod = ar.take(2048)
        rows = ar.take(TOP * D)
        score, work = ar.take(BLOCK), ar.take(BLOCK)
        val, idx, idf = ar.take(TOP), ar.take(TOP).bitcast(U32), ar.take(TOP)
        x_blocks = x.rearrange("b (n s) d -> (b n) (s d)", s=BLOCK)
        x_rows = x.rearrange("b s d -> (b s) d")

        def select_sync(sp):
            for n in range(XG):
                if n >= 2:
                    sp.wait_ge(*after(f"prod{n - 2}"))
                sp.dma_start(xin[n % 2], x_blocks[:, 2048 * n:2048 * (n + 1)]).then_inc(x_loaded[n % 2], 16)
                if n == 1:
                    sp.dma_start(cs[:, :], constants).then_inc(c_loaded, 16)
            for a in range(0, second_at, W_STEP):
                b = min(a + W_STEP, second_at)
                sp.dma_start(wt[:, a:b], weights[:, a:b]).then_inc(w_loaded, 16)

        W_STEP = 4096
        n_weight_loads = len(range(0, second_at, W_STEP))

        def select_vector(v):
            w_row = W("tok_w").unsqueeze(1).to_broadcast([P, 16, D])
            v.wait_ge(tok_loaded, 16)
            for n in range(XG):
                v.wait_ge(x_loaded[n % 2], 16 * (n // 2 + 1))
                v.wait_ge(*last())
                v.tensor_tensor(prod.rearrange("p (s d) -> p s d", d=D), xin[n % 2].rearrange("p (s d) -> p s d", d=D),
                                w_row, ALU.mult).then_inc(*did(f"prod{n}"))
                v.wait_ge(*last())
                v.tensor_reduce(score[:, 16 * n:16 * n + 16], prod.rearrange("p (s d) -> p s d", d=D), AX_X,
                                ALU.add).then_inc(*did(f"score{n}"))
            v.wait_ge(*last())
            v.tensor_scalar(score, score, tok_b[:, 0:1], None, ALU.add).then_inc(*did("score"))
            src = score
            for r in range(2):
                v.wait_ge(*last())
                v.max(val[:, 8 * r:8 * r + 8], src).then_inc(*did(f"max{r}"))
                v.wait_ge(*last())
                v.max_index(idx[:, 8 * r:8 * r + 8], val[:, 8 * r:8 * r + 8], src).then_inc(*did(f"index{r}"))
                if r == 0:
                    v.wait_ge(*last())
                    v.match_replace(work, val[:, 0:8], src, -3e38).then_inc(*did("taken"))
                    src = work
            v.wait_ge(*last())
            v.tensor_copy(idf, idx).then_inc(*did("index_f"))
            v.wait_ge(c_loaded, 16)
            v.wait_ge(*last())
            v.tensor_scalar(idx, idf, C("base"), None, ALU.add).then_inc(*did("row_index"))

        def select_gpsimd(g):
            g.wait_ge(*after("row_index"))
            for r in range(TOP):
                g.indirect_dma_start(out=rows[:, r * D:(r + 1) * D], out_offset=None, in_=x_rows,
                                     in_offset=bass.IndirectOffsetOnAxis(ap=idx[:, r:r + 1], axis=0)).then_inc(gathered, 16)

        def select_tensor(pe):
            pe.wait_ge(c_loaded, 16)
            pe.wait_ge(gathered, 16 * TOP)
            for q in range(4):
                ps = fill(pe, f"turn{q}", f"h{q}")
                for r in range(4):
                    at = 4 * q + r
                    ins = pe.transpose(ps[:, r * P:(r + 1) * P], rows[:, at * D:(at + 1) * D], C("ident"))
                ins.then_inc(*did(f"turn{q}"))

        def select_scalar(a):
            for q in range(4):
                a.wait_ge(*after(f"turn{q}"))
                a.wait_ge(*last())
                a.activation(h[:, :].rearrange("p (n r) -> p r n", r=TOP)[:, 4 * q:4 * q + 4, :],
                             bank("scalar", f"turn{q}").rearrange("p (r n) -> p r n", n=P), ACT.Copy).then_inc(*did(f"h{q}"))
            a.wait_ge(w_loaded, 16 * n_weight_loads)
            a.wait_ge(c_loaded, 16)
            a.wait_ge(tok_loaded, 16)

        tok_loaded = sem("vectors_loaded")
        second_loaded, third_loaded = sem("layer2_weights_loaded"), sem("layer3_weights_loaded")
        tok_b = W("tok_b")

        def head_scalar(a, i):
            a.wait_ge(*last())
            a.activation(hc, h[:, bass.ts(i, CH)], ACT.Copy).then_inc(*did("hc"))
            ln_scalar(a, "ln")

        def head_tensor(pe):
            ln_tensor(pe, "ln", hc, ["hc"])

        def head_vector(v):
            ln_vector(v, "ln", hc, xn, ["hc"])

        def softmax_vector(v, k, s, st):
            s3 = HB(s)
            v.wait_ge(*last())
            v.tensor_reduce(st[:, 0:CB], s3, AX_X, ALU.max).then_inc(*did(f"{k}.max"))
            v.wait_ge(*last())
            v.tensor_tensor(s3, s3, st[:, 0:CB].unsqueeze(2).to_broadcast([P, CB, T]), ALU.subtract).then_inc(*did(f"{k}.sub"))

        def softmax_scalar(a, k, s, scale):
            a.wait_ge(*after(f"{k}.sub"))
            a.wait_ge(*last())
            a.activation(s, s, ACT.Exp, scale=scale).then_inc(*did(f"{k}.exp"))

        def softmax_vector2(v, k, s, st, p_t, before=()):
            s3 = HB(s)
            v.wait_ge(*after(f"{k}.exp"))
            v.wait_ge(*last())
            v.tensor_reduce(st[:, CB:2 * CB], s3, AX_X, ALU.add).then_inc(*did(f"{k}.sum"))
            v.wait_ge(*last())
            v.reciprocal(st[:, 2 * CB:3 * CB], st[:, CB:2 * CB]).then_inc(*did(f"{k}.rec"))
            v.wait_ge(*last())
            v.tensor_tensor(s3, s3, st[:, 2 * CB:3 * CB].unsqueeze(2).to_broadcast([P, CB, T]), ALU.mult).then_inc(*did(f"{k}.norm"))
            for step in before:
                v.wait_ge(*after(step))
            v.wait_ge(*last())
            v.transpose(p_t, s).then_inc(*did(f"{k}.turned"))

        att = Places(ctx.enter_context(nc.sbuf_tensor("att", [P, 8800], F32)), 8800)
        at_q, at_rep, at_kx, at_vx = att.take(CH), att.take(4 * CH), att.take(4 * CH), att.take(CB * D)
        at_s = [att.take(CH), att.take(CH)]
        at_p = [att.take(CH), att.take(CH)]
        at_st = [att.take(3 * CB), att.take(3 * CB)]
        rep4 = at_rep.rearrange("p (b q t) -> p b q t", q=4, t=T)
        kx4 = at_kx.rearrange("p (b q t) -> p b q t", q=4, t=T)

        def core_tensor(pe, k, wv, v_ready, qk_ready):
            for g in range(4):
                ps = fill(pe, f"{k}.v{g}", f"{k}.vx{g}")
                for step in v_ready:
                    pe.wait_ge(*after(step))
                for b in range(4):
                    ins = pe.matmul(ps[:, b * D:(b + 1) * D], at_rep[:, (4 * g + b) * P:(4 * g + b + 1) * P], wv,
                                    start=True, stop=True)
                ins.then_inc(*did(f"{k}.v{g}"))
            for hh in range(2):
                ps = fill(pe, f"{k}.s{hh}", f"{k}.in{hh}")
                for step in qk_ready:
                    pe.wait_ge(*after(step))
                for b in range(CB):
                    ins = pe.matmul(ps[:, b * T:(b + 1) * T], at_kx[64 * hh:64 * hh + 64, b * P:(b + 1) * P],
                                    at_q[64 * hh:64 * hh + 64, b * T:(b + 1) * T], start=True, stop=True)
                ins.then_inc(*did(f"{k}.s{hh}"))
            ps = fill(pe, f"{k}.o", f"{k}.o_read")
            for hh in range(2):
                pe.wait_ge(*after(f"{k}.{hh}.turned"))
                pe.wait_ge(*after(f"{k}.vx3"))
                for b in range(CB):
                    ins = pe.matmul(ps[64 * hh:64 * hh + 64, b * T:(b + 1) * T],
                                    at_vx[:, b * D + 64 * hh:b * D + 64 * hh + 64],
                                    at_p[hh][:, b * T:(b + 1) * T], start=True, stop=True)
            ins.then_inc(*did(f"{k}.o"))

        def core_vector(v, k, scale, mask=None):
            for g in range(4):
                v.wait_ge(*after(f"{k}.v{g}"))
                v.wait_ge(*last())
                v.tensor_tensor(at_vx[:, 4 * g * D:4 * (g + 1) * D].rearrange("p (b f) -> p b f", f=D),
                                bank("vector", f"{k}.v{g}").rearrange("p (b f) -> p b f", f=D),
                                C("v16").unsqueeze(1).to_broadcast([P, 4, D]), ALU.mult).then_inc(*did(f"{k}.vx{g}"))
            for hh in range(2):
                kk = f"{k}.{hh}"
                v.wait_ge(*after(f"{k}.s{hh}"))
                v.wait_ge(*last())
                v.transpose(at_s[hh], bank("vector", f"{k}.s{hh}")).then_inc(*did(f"{k}.in{hh}"))
                if mask is not None:
                    v.wait_ge(*last())
                    v.scalar_tensor_tensor(out=HB(at_s[hh]), in0=HB(at_s[hh]), scalar=scale,
                                           in1=mask(hh).unsqueeze(1).to_broadcast([P, CB, T]),
                                           op0=ALU.mult, op1=ALU.add).then_inc(*did(f"{kk}.mask"))
                softmax_vector(v, kk, at_s[hh], at_st[hh])
            for hh in range(2):
                softmax_vector2(v, f"{k}.{hh}", at_s[hh], at_st[hh], at_p[hh])

        def core_scalar(a, k, scale):
            for hh in range(2):
                softmax_scalar(a, f"{k}.{hh}", at_s[hh], scale)

        def rep_scalar(a, k, src, needs, before=()):
            for q in range(4):
                for step in needs:
                    a.wait_ge(*after(step))
                for step in before:
                    a.wait_ge(*after(step))
                a.wait_ge(*last())
                a.activation(rep4[:, :, q, :], HB(src), ACT.Copy).then_inc(*did(f"{k}.rep{q}"))

        def kx_scalar(a, k, bias=None, before=()):
            for q in range(4):
                a.wait_ge(*after(f"{k}.k"))
                for step in before:
                    a.wait_ge(*after(step))
                a.wait_ge(*last())
                if bias is None:
                    a.activation(kx4[:, :, q, :], HB(bank("scalar", f"{k}.k")), ACT.Copy,
                                 scale=C("head", q, q + 1)).then_inc(*did(f"{k}.kx{q}"))
                else:
                    a.activation(kx4[:, :, q, :], HB(bank("scalar", f"{k}.k")), ACT.Identity,
                                 scale=C("head", q, q + 1), bias=bias[:, q:q + 1]).then_inc(*did(f"{k}.kx{q}"))

        ar = new_arena()
        qu, qc, kc = ar.take(4 * CH), ar.take(4 * CH), ar.take(4 * CH)
        kux, vux = ar.take(8 * CH), ar.take(8 * CH)

        t1x = at_kx
        qcx_ = ar.take(8 * CH)
        sg = at_q
        sc = at_s
        pt = at_p
        su_s = ln_sq
        xr2 = at_rep[:, 0:2 * CH]
        vcx = kux
        o_t = qu

        def l0_tensor(pe, i):
            head_tensor(pe)
            for name in ("q_u", "k_u", "v_u", "q_c", "k_c"):
                for f in range(4):
                    mm(pe, f"{name}{f}", f"{name}{f}.read", ["ln.n"], [(W(name, f * P, (f + 1) * P), xn)])
            for hh in range(2):
                def pairs(key, reader, lhs, rhs, needs):
                    ps = fill(pe, key, reader)
                    for step in needs:
                        pe.wait_ge(*after(step))
                    for f in (2 * hh, 2 * hh + 1):
                        for b in range(CB):
                            ins = pe.matmul(ps[64 * (f % 2):64 * (f % 2) + 64, b * T:(b + 1) * T],
                                            lhs[:, f * 2 * CH + b * 64:f * 2 * CH + b * 64 + 64],
                                            rhs[:, f * CH + b * T:f * CH + (b + 1) * T], start=True, stop=True)
                    ins.then_inc(*did(key))
                both = (2 * hh, 2 * hh + 1)
                pairs(f"t1_{hh}", f"t1x_{hh}", vux, qc, [f"v_u{f}.read" for f in both] + [f"q_c{f}.plain" for f in both])
                pairs(f"lu_{hh}", f"sig_{hh}", kux, qu, [f"k_u{f}.read" for f in both] + [f"q_u{f}.read" for f in both])
                pairs(f"sc_{hh}", f"masked_{hh}", qcx_, kc, [f"q_c{f}.read" for f in both] + [f"k_c{f}.read" for f in both])
                ps = fill(pe, f"su_{hh}", f"silu_{hh}")
                pe.wait_ge(*after(f"t1x_{hh}"))
                pe.wait_ge(*after(f"sigm_{hh}"))
                for b in range(CB):
                    ins = pe.matmul(ps[:, b * T:(b + 1) * T], t1x[:, b * P:(b + 1) * P], sg[:, b * T:(b + 1) * T],
                                    start=True, stop=True)
                ins.then_inc(*did(f"su_{hh}"))
            wv = W("v_c").rearrange("p (u w f) -> p w u f", u=2, w=2)
            for g in range(CB // 2):
                ps = fill(pe, f"v{g}", f"vx{g}")
                pe.wait_ge(*after("x.rep1"))
                for b in range(2):
                    for w in range(2):
                        ins = pe.matmul(ps[64 * w:64 * w + 64, b * 256:(b + 1) * 256].rearrange("p (u f) -> p u f", u=2),
                                        xr2[:, (2 * g + b) * 64:(2 * g + b + 1) * 64], wv[:, w], start=True, stop=True)
                ins.then_inc(*did(f"v{g}"))
            for f in range(4):
                hh, w = f // 2, f % 2
                ps = fill(pe, f"o{f}", f"o{f}.read")
                pe.wait_ge(*after(f"a{hh}.turned"))
                pe.wait_ge(*after(f"vx{CB // 2 - 1}"))
                for b in range(CB):
                    ins = pe.matmul(ps[:, b * T:(b + 1) * T], vcx[64 * w:64 * w + 64, b * 256 + hh * D:b * 256 + (hh + 1) * D],
                                    pt[hh][64 * w:64 * w + 64, b * T:(b + 1) * T], start=True, stop=True)
                ins.then_inc(*did(f"o{f}"))
            mm(pe, "proj", "h_new", [f"o{f}.read" for f in range(4)],
               [(W("l0_out", f * P, (f + 1) * P), o_t[:, f * CH:(f + 1) * CH]) for f in range(4)])

        def expand(eng, who, name, dst, f):
            d4 = dst[:, f * 2 * CH:(f + 1) * 2 * CH].rearrange("p (b q t) -> p b q t", q=2, t=T)
            for q in range(2):
                key = f"{name}{f}.x{q}" if q == 0 else f"{name}{f}.read"
                eng.wait_ge(*after(f"{name}{f}"))
                eng.wait_ge(*last())
                if who == "scalar":
                    eng.activation(d4[:, :, q, :], HB(bank(who, f"{name}{f}")), ACT.Copy, scale=C("half", q, q + 1)).then_inc(*did(key))
                else:
                    eng.tensor_scalar(d4[:, :, q, :], HB(bank(who, f"{name}{f}")), C("half", q, q + 1), None, ALU.mult).then_inc(*did(key))

        def l0_vector(v, i):
            head_vector(v)
            for f in range(4):
                expand(v, "vector", "k_u", kux, f)
            for f in range(4):
                v.wait_ge(*after(f"q_c{f}"))
                v.wait_ge(*last())
                v.tensor_copy(qc[:, f * CH:(f + 1) * CH], bank("vector", f"q_c{f}")).then_inc(*did(f"q_c{f}.plain"))
                expand(v, "vector", "q_c", qcx_, f)
            for hh in range(2):
                v.wait_ge(*after(f"t1_{hh}"))
                if hh:
                    v.wait_ge(*after(f"su_{hh - 1}"))
                v.wait_ge(*last())
                v.tensor_tensor(t1x.rearrange("p (b q t) -> p b q t", q=4, t=T),
                                HB(bank("vector", f"t1_{hh}")).unsqueeze(2).to_broadcast([P, CB, 4, T]),
                                C("t1m").rearrange("p (q t) -> p q t", t=T).unsqueeze(1).to_broadcast([P, CB, 4, T]),
                                ALU.mult).then_inc(*did(f"t1x_{hh}"))
                v.wait_ge(*after(f"sig_{hh}"))
                v.wait_ge(*last())
                v.tensor_tensor(HB(sg), HB(sg), C("sgm").unsqueeze(1).to_broadcast([P, CB, T]), ALU.mult).then_inc(*did(f"sigm_{hh}"))
                v.wait_ge(*after(f"sc_{hh}"))
                v.wait_ge(*last())
                v.scalar_tensor_tensor(out=HB(sc[hh]), in0=HB(bank("vector", f"sc_{hh}")), scalar=0.125,
                                       in1=C("causal").unsqueeze(1).to_broadcast([P, CB, T]),
                                       op0=ALU.mult, op1=ALU.add).then_inc(*did(f"masked_{hh}"))
                v.wait_ge(*after(f"susig_{hh}"))
                v.wait_ge(*last())
                v.tensor_tensor(su_s, su_s, bank("vector", f"su_{hh}"), ALU.mult).then_inc(*did(f"silu_{hh}"))
                v.wait_ge(*last())
                v.tensor_tensor(sc[hh], sc[hh], su_s, ALU.subtract).then_inc(*did(f"final_{hh}"))
                softmax_vector(v, f"a{hh}", sc[hh], at_st[hh])
            for g in range(CB // 2):
                v.wait_ge(*after(f"v{g}"))
                v.wait_ge(*after("lu_1"))
                v.wait_ge(*last())
                v.tensor_tensor(vcx[:, g * 512:(g + 1) * 512].rearrange("p (b f) -> p b f", f=D),
                                bank("vector", f"v{g}").rearrange("p (b f) -> p b f", f=D),
                                C("v64").unsqueeze(1).to_broadcast([P, 4, D]), ALU.mult).then_inc(*did(f"vx{g}"))
            for hh in range(2):
                softmax_vector2(v, f"a{hh}", sc[hh], at_st[hh], pt[hh])
            residual_vector(v, i, "proj")

        def residual_vector(v, i, key):
            v.wait_ge(*after(key))
            v.wait_ge(*last())
            v.tensor_tensor(h[:, bass.ts(i, CH)], hc, bank("vector", key), ALU.add).then_inc(*did("h_new"))

        def l0_scalar(a, i):
            head_scalar(a, i)
            for q in range(2):
                a.wait_ge(*after("ln.n"))
                a.wait_ge(*last())
                a.activation(xr2.rearrange("p (b q t) -> p b q t", q=2, t=T)[:, :, q, :], HB(xn), ACT.Copy).then_inc(*did(f"x.rep{q}"))
            for name, dst in (("q_u", qu), ("v_u", vux), ("k_c", kc)):
                for f in range(4):
                    if dst is vux:
                        expand(a, "scalar", name, dst, f)
                    else:
                        a.wait_ge(*after(f"{name}{f}"))
                        a.wait_ge(*last())
                        a.activation(dst[:, f * CH:(f + 1) * CH], bank("scalar", f"{name}{f}"), ACT.Copy).then_inc(*did(f"{name}{f}.read"))
            for hh in range(2):
                a.wait_ge(*after(f"lu_{hh}"))
                if hh:
                    a.wait_ge(*after(f"su_{hh - 1}"))
                a.wait_ge(*last())
                a.activation(sg, bank("scalar", f"lu_{hh}"), ACT.Sigmoid, scale=0.125).then_inc(*did(f"sig_{hh}"))
                a.wait_ge(*after(f"su_{hh}"))
                if hh:
                    a.wait_ge(*after(f"final_{hh - 1}"))
                a.wait_ge(*last())
                a.activation(su_s, bank("scalar", f"su_{hh}"), ACT.Sigmoid).then_inc(*did(f"susig_{hh}"))
            for hh in range(2):
                softmax_scalar(a, f"a{hh}", sc[hh], 1.0)
            for f in range(4):
                a.wait_ge(*after(f"o{f}"))
                a.wait_ge(*after("lu_1"))
                a.wait_ge(*last())
                a.activation(o_t[:, f * CH:(f + 1) * CH], bank("scalar", f"o{f}"), ACT.Copy).then_inc(*did(f"o{f}.read"))

        ar = new_arena()
        gx = {g: ar.take(T * 2 * B) for g in ("z", "r", "c")}
        hs = ar.take((T + 1) * 2 * B)
        gb = keep.take(6)
        GRU_IN = (("z", "g_uz", "buz", "bwz"), ("r", "g_ur", "bur", "bwr"), ("c", "g_u", "bu", "bw"))

        def gru_input_tensor(pe, i):
            head_tensor(pe)
            for g, w, _, _ in GRU_IN:
                for m in range(2):
                    mm(pe, f"{g}{m}", f"{g}{m}.read", ["ln.n"], [(W(w, m * P, (m + 1) * P), xn)])

        def gru_input_vector(v, i):
            head_vector(v)
            for n, (g, _, b1, b2) in enumerate(GRU_IN):
                v.wait_ge(*last())
                v.tensor_tensor(gb[:, 2 * n:2 * n + 2], W(b1), W(b2), ALU.add).then_inc(*did(f"bias{g}"))
            for n, (g, _, _, _) in enumerate(GRU_IN):
                m = 0
                v.wait_ge(*after(f"{g}{m}"))
                v.wait_ge(*last())
                v.tensor_scalar(gx_chunk(g, m, i), HB(bank("vector", f"{g}{m}")), gb[:, 2 * n + m:2 * n + m + 1], None,
                                ALU.add).then_inc(*did(f"{g}{m}.read"))

        def gx_chunk(g, m, i):
            v4 = gx[g].rearrange("p (t m b) -> p m b t", m=2, b=B)
            return v4[:, m, bass.ts(i, CB), :]

        def gru_input_scalar(a, i):
            head_scalar(a, i)
            for n, (g, _, _, _) in enumerate(GRU_IN):
                m = 1
                a.wait_ge(*after(f"{g}{m}"))
                a.wait_ge(*after(f"bias{g}"))
                a.wait_ge(*last())
                a.activation(gx_chunk(g, m, i), HB(bank("scalar", f"{g}{m}")), ACT.Identity,
                             bias=gb[:, 2 * n + m:2 * n + m + 1]).then_inc(*did(f"{g}{m}.read"))

        gru = Places(at_kx, 4 * CH)
        gz = gru.take(2 * B)
        gr = gru.take(2 * B)
        gc = gru.take(2 * B)
        gt = gru.take(2 * B)
        gw = gru.take(2 * B)
        gh = gru.take(2 * B)
        HW = 2 * B

        def gru_tensor(pe, t):
            for g in ("r", "z"):
                ps = fill(pe, g, f"{g}.sig")
                pe.matmul(ps[:, 0:HW], C("ident"), gx[g][:, bass.ts(t, HW)], start=True, stop=False)
                for m in range(2):
                    for k in range(2):
                        ins = pe.matmul(ps[:, m * B:(m + 1) * B], W("g_wz" if g == "z" else "g_wr", k * 256 + m * P, k * 256 + (m + 1) * P),
                                        gh[:, k * B:(k + 1) * B], start=False, stop=m == 1 and k == 1)
                ins.then_inc(*did(g))
            ps = fill(pe, "c", "c.tanh")
            pe.matmul(ps[:, 0:HW], C("ident"), gx["c"][:, bass.ts(t, HW)], start=True, stop=False)
            pe.wait_ge(*after("hr"))
            for m in range(2):
                for k in range(2):
                    ins = pe.matmul(ps[:, m * B:(m + 1) * B], W("g_w", k * 256 + m * P, k * 256 + (m + 1) * P),
                                    gt[:, k * B:(k + 1) * B], start=False, stop=m == 1 and k == 1)
            ins.then_inc(*did("c"))

        def gru_scalar(a, t):
            a.wait_ge(*after("r"))
            a.wait_ge(*last())
            a.activation(gr, bank("scalar", "r")[:, 0:HW], ACT.Sigmoid).then_inc(*did("r.sig"))
            a.wait_ge(*after("z"))
            a.wait_ge(*last())
            a.activation(gz, bank("scalar", "z")[:, 0:HW], ACT.Sigmoid).then_inc(*did("z.sig"))
            a.wait_ge(*after("c"))
            a.wait_ge(*last())
            a.activation(gc, bank("scalar", "c")[:, 0:HW], ACT.Tanh).then_inc(*did("c.tanh"))

        def gru_vector(v, t):
            v.wait_ge(*after("r.sig"))
            v.wait_ge(*last())
            v.tensor_tensor(gt, gh, gr, ALU.mult).then_inc(*did("hr"))
            v.wait_ge(*after("z.sig"))
            v.wait_ge(*after("z"))
            v.wait_ge(*last())
            v.tensor_tensor(gw, gh, gz, ALU.mult).then_inc(*did("zh"))
            v.wait_ge(*last())
            v.tensor_scalar(gz, gz, -1.0, 1.0, ALU.mult, ALU.add).then_inc(*did("omz"))
            v.wait_ge(*after("c.tanh"))
            v.wait_ge(*last())
            v.tensor_tensor(gc, gc, gz, ALU.mult).then_inc(*did("zc"))
            v.wait_ge(*after("z"))
            v.wait_ge(*last())
            v.tensor_tensor(gh, gc, gw, ALU.add).then_inc(*did("state"))
            v.wait_ge(*last())
            v.tensor_copy(hs[:, bass.ts(t, HW)], gh).then_inc(*did("kept"))

        def gru_output_tensor(pe, i):
            mm(pe, "out", "sig", ["state0", "state1"], [(W("g_o", m * D, (m + 1) * D), hsc[:, m * CH:(m + 1) * CH]) for m in range(2)])

        hsc = at_rep

        def gru_output_scalar(a, i):
            hv = hs[:, 0:T * HW].rearrange("p (t m b) -> p m b t", m=2, b=B)
            for m in range(2):
                a.wait_ge(*last())
                a.activation(HB(hsc[:, m * CH:(m + 1) * CH]), hv[:, m, bass.ts(i, CB), :], ACT.Copy).then_inc(*did(f"state{m}"))
            a.wait_ge(*after("out"))
            a.wait_ge(*last())
            a.activation(xn, bank("scalar", "out"), ACT.Sigmoid, bias=W("g_bo")).then_inc(*did("sig"))

        def gru_output_vector(v, i):
            v.wait_ge(*after("sig"))
            v.wait_ge(*last())
            v.tensor_tensor(h[:, bass.ts(i, CH)], h[:, bass.ts(i, CH)], xn, ALU.add).then_inc(*did("h_new"))

        ar = new_arena()
        l1_o, l1_y = ar.take(CH), ar.take(3 * CH)
        l1_kb = keep.take(12)
        bands = ["band5", "band10", None]

        def l1_tensor(pe, i):
            head_tensor(pe)
            for s in range(3):
                k = f"s{s}"
                mm(pe, f"{k}.q", f"{k}.q_read", ["ln.n"], [(W(f"l1_qkv{s}", 0, D), xn)])
                mm(pe, f"{k}.k", f"{k}.kx3", ["ln.n"], [(W(f"l1_qkv{s}", D, 2 * D), xn)])
                core_tensor(pe, k, W(f"l1_qkv{s}", 2 * D, 3 * D), ["x.rep3"], [f"{k}.q_read", f"{k}.kx3"])
                mm(pe, f"{k}.y", f"{k}.y_read", [f"{k}.o_read"], [(W(f"l1_o{s}"), l1_o)])
            mm(pe, "f", "h_new", ["s2.y_read"], [(W("l1_f", s * D, (s + 1) * D), l1_y[:, s * CH:(s + 1) * CH]) for s in range(3)])

        def l1_vector(v, i):
            for s in range(3):
                v.wait_ge(*last())
                v.tensor_scalar(l1_kb[:, 4 * s:4 * s + 4], C("head"), W(f"l1_bqkv{s}", 1, 2), None, ALU.mult).then_inc(*did(f"kb{s}"))
            head_vector(v)
            for s in range(3):
                mask = None if bands[s] is None else (lambda hh, s=s: C(bands[s]))
                core_vector(v, f"s{s}", 0.25, mask)
            v.wait_ge(*after("f"))
            v.wait_ge(*last())
            v.tensor_scalar(hc, hc, W("l1_bf"), None, ALU.add).then_inc(*did("h_bias"))
            residual_vector(v, i, "f")

        def l1_scalar(a, i):
            head_scalar(a, i)
            rep_scalar(a, "x", xn, ["ln.n"])
            for s in range(3):
                k = f"s{s}"
                a.wait_ge(*after(f"{k}.q"))
                if s:
                    a.wait_ge(*after(f"s{s - 1}.s1"))
                a.wait_ge(*last())
                a.activation(at_q, bank("scalar", f"{k}.q"), ACT.Identity, bias=W(f"l1_bqkv{s}", 0, 1)).then_inc(*did(f"{k}.q_read"))
                kx_scalar(a, k, l1_kb[:, 4 * s:4 * s + 4], [f"kb{s}"])
                core_scalar(a, k, 1.0 if bands[s] else 0.25)
                a.wait_ge(*after(f"{k}.o"))
                if s:
                    a.wait_ge(*after(f"s{s - 1}.y"))
                a.wait_ge(*last())
                a.activation(l1_o, bank("scalar", f"{k}.o"), ACT.Identity, bias=W(f"l1_bqkv{s}", 2, 3)).then_inc(*did(f"{k}.o_read"))
                a.wait_ge(*after(f"{k}.y"))
                a.wait_ge(*last())
                a.activation(l1_y[:, s * CH:(s + 1) * CH], bank("scalar", f"{k}.y"), ACT.Identity, bias=W(f"l1_bo{s}")).then_inc(*did(f"{k}.y_read"))

        ar = new_arena()
        en = ar.take(CH)
        hid = [[ar.take(CH) for _ in range(4)] for _ in range(2)]
        mix = ar.take(CH)
        lg, top, topi, topf = ar.take(32), ar.take(32), ar.take(32).bitcast(U32), ar.take(32)
        g2 = ar.take(12)
        oh, gate = ar.take(32), ar.take(32)
        gate_t = ar.take(CH)
        T8 = lambda ap: ap.rearrange("p (t e) -> p t e", t=NT)

        def experts_tensor(pe, i):
            head_tensor(pe)
            ln_tensor(pe, "ln_in", xn, ["ln.n"])
            ps = fill(pe, "logits", "logits_read")
            pe.wait_ge(*after("en"))
            for t in range(NT):
                pe.matmul(ps[:, 8 * t:8 * t + 8], en[:, t * P:(t + 1) * P], W("moe_r"), start=True, stop=False)
                ins = pe.matmul(ps[:, 8 * t:8 * t + 8], C("row0"), W("moe_br"), start=False, stop=True)
            ins.then_inc(*did("logits"))

            def up(e):
                for f in range(4):
                    mm(pe, f"u{e}.{f}", f"g{e}.{f}", [], [(W(f"moe_1_{e}", f * P, (f + 1) * P), en)])

            def down(e):
                ps = fill(pe, f"y{e}", f"mix{e}.3")
                for t in range(NT):
                    for f in range(4):
                        pe.wait_ge(*after(f"g{e}.{f}"))
                        ins = pe.matmul(ps[:, t * P:(t + 1) * P], hid[e % 2][f][:, t * P:(t + 1) * P],
                                        W(f"moe_2_{e}", f * D, (f + 1) * D), start=f == 0, stop=f == 3)
                ins.then_inc(*did(f"y{e}"))
            up(0)
            for e in range(E1):
                if e + 1 < E1:
                    up(e + 1)
                if e == 1:
                    ps = fill(pe, "gate_t", "gate_t_read")
                    pe.wait_ge(*after("gate"))
                    for t in range(NT):
                        ins = pe.transpose(ps[0:8, t * P:(t + 1) * P], gate[:, 8 * t:8 * t + 8], C("ident"))
                    ins.then_inc(*did("gate_t"))
                down(e)
            ps = fill(pe, "mixed", "h_new")
            pe.wait_ge(*after(f"mix{E1 - 1}.3"))
            pe.wait_ge(*after("gate_t_read"))
            pe.matmul(ps, W("moe_b2"), gate_t, start=True, stop=False)
            for t in range(NT):
                ins = pe.matmul(ps[:, t * P:(t + 1) * P], mix[:, t * P:(t + 1) * P], C("ident"), start=False, stop=t == NT - 1)
            ins.then_inc(*did("mixed"))

        def experts_vector(v, i):
            head_vector(v)
            ln_vector(v, "ln_in", xn, en, [])
            v.wait_ge(*last())
            v.tensor_scalar(en, en, W("ln_g"), W("ln_b"), ALU.mult, ALU.add).then_inc(*did("en"))
            v.wait_ge(*last())
            v.tensor_tensor(hc, hc, xn, ALU.add).then_inc(*did("h_sum"))
            v.wait_ge(*after("logits"))
            v.wait_ge(*last())
            v.tensor_copy(lg, bank("vector", "logits")[:, 0:32]).then_inc(*did("logits_read"))
            for t in range(NT):
                v.wait_ge(*last())
                v.max(top[:, 8 * t:8 * t + 8], lg[:, 8 * t:8 * t + 8]).then_inc(*did(f"top{t}"))
                v.wait_ge(*last())
                v.max_index(topi[:, 8 * t:8 * t + 8], top[:, 8 * t:8 * t + 8], lg[:, 8 * t:8 * t + 8]).then_inc(*did(f"topi{t}"))
            v.wait_ge(*last())
            v.tensor_copy(topf, topi).then_inc(*did("topf"))
            v.wait_ge(*last())
            v.tensor_tensor(g2[:, 0:4], T8(top)[:, :, 1], T8(top)[:, :, 0], ALU.subtract).then_inc(*did("gap"))
            v.wait_ge(*after("gap_exp"))
            v.wait_ge(*last())
            v.tensor_scalar(g2[:, 8:12], g2[:, 4:8], 1.0, None, ALU.add).then_inc(*did("gate_sum"))
            v.wait_ge(*last())
            v.reciprocal(g2[:, 0:4], g2[:, 8:12]).then_inc(*did("gate_1"))
            v.wait_ge(*last())
            v.tensor_tensor(g2[:, 4:8], g2[:, 4:8], g2[:, 0:4], ALU.mult).then_inc(*did("gate_2"))
            for n, dst in ((0, gate), (1, oh)):
                v.wait_ge(*last())
                v.tensor_tensor(T8(dst), C("iota8").unsqueeze(1).to_broadcast([P, NT, 8]),
                                T8(topf)[:, :, n:n + 1].to_broadcast([P, NT, 8]), ALU.is_equal).then_inc(*did(f"hot{n}"))
                v.wait_ge(*last())
                v.tensor_tensor(T8(dst), T8(dst), g2[:, 4 * n:4 * n + 4].unsqueeze(2).to_broadcast([P, NT, 8]),
                                ALU.mult).then_inc(*did(f"weighted{n}"))
            v.wait_ge(*last())
            v.tensor_tensor(gate, gate, oh, ALU.add).then_inc(*did("gate"))
            v.wait_ge(*last())
            v.memset(gate_t, 0.0).then_inc(*did("gate_t_zero"))
            for e in range(E1):
                for t in range(NT):
                    v.wait_ge(*after(f"y{e}"))
                    v.wait_ge(*last())
                    cols = slice(t * P, (t + 1) * P)
                    y = bank("vector", f"y{e}")[:, cols]
                    if e == 0:
                        v.tensor_scalar(mix[:, cols], y, gate[:, 8 * t + e:8 * t + e + 1], None, ALU.mult).then_inc(*did(f"mix{e}.{t}"))
                    else:
                        v.scalar_tensor_tensor(out=mix[:, cols], in0=y, scalar=gate[:, 8 * t + e:8 * t + e + 1], in1=mix[:, cols],
                                               op0=ALU.mult, op1=ALU.add).then_inc(*did(f"mix{e}.{t}"))
                if e == 1:
                    v.wait_ge(*after("gate_t"))
                    v.wait_ge(*last())
                    v.tensor_copy(gate_t[0:8, :], bank("vector", "gate_t")[0:8, :]).then_inc(*did("gate_t_read"))
            residual_vector(v, i, "mixed")

        def experts_scalar(a, i):
            head_scalar(a, i)
            ln_scalar(a, "ln_in")
            a.wait_ge(*after("gap"))
            a.wait_ge(*last())
            a.activation(g2[:, 4:8], g2[:, 0:4], ACT.Exp).then_inc(*did("gap_exp"))
            for e in range(E1):
                for f in range(4):
                    a.wait_ge(*after(f"u{e}.{f}"))
                    if e >= 2:
                        a.wait_ge(*after(f"y{e - 2}"))
                    a.wait_ge(*last())
                    a.activation(hid[e % 2][f], bank("scalar", f"u{e}.{f}"), ACT.Gelu,
                                 bias=W("moe_b1", 4 * e + f, 4 * e + f + 1)).then_inc(*did(f"g{e}.{f}"))

        ar = new_arena()
        ga, bz, hscan = ar.take(TOK), ar.take(TOK), ar.take(TOK)
        l2_bb = keep.take(1)
        gsig, hsc2 = ar.take(CH), ar.take(CH)
        yv, pool_ = ar.take(CH), keep.take(B)

        def pos_major(ap, i):
            return ap.rearrange("p (t b) -> p b t", b=B)[:, bass.ts(i, CB), :]

        def l2_input_tensor(pe, i):
            head_tensor(pe)
            for n, r in ((0, "bz"), (1, "g_sig")):
                mm(pe, f"in{n}", r, ["ln.n"], [(W("l2_in", n * D, (n + 1) * D), xn)])

        def l2_input_vector(v, i):
            v.wait_ge(*last())
            v.tensor_tensor(l2_bb, W("l2_bin", 0, 1), W("l2_B"), ALU.mult).then_inc(*did("bias_b"))
            head_vector(v)
            v.wait_ge(*after("ln.n"))
            v.wait_ge(*last())
            v.tensor_copy(ln2[:, bass.ts(i, CH)], xn).then_inc(*did("kept"))
            v.wait_ge(*after("in0"))
            v.wait_ge(*last())
            v.tensor_scalar(pos_major(bz, i), HB(bank("vector", "in0")), W("l2_B"), l2_bb, ALU.mult, ALU.add).then_inc(*did("bz"))
            v.wait_ge(*after("g_sig"))
            v.wait_ge(*last())
            v.tensor_scalar(pos_major(ga, i), HB(gsig), W("l2_A"), None, ALU.mult).then_inc(*did("ga"))

        def l2_input_scalar(a, i):
            head_scalar(a, i)
            a.wait_ge(*after("in1"))
            a.wait_ge(*last())
            a.activation(gsig, bank("scalar", "in1"), ACT.Sigmoid, bias=W("l2_bin", 1, 2)).then_inc(*did("g_sig"))

        def l2_scan_vector(v):
            v.wait_ge(*last())
            v.memset(ga.rearrange("p (t b) -> p t b", b=B)[:, :, 0:1], 0.0).then_inc(*did("starts"))
            v.wait_ge(*last())
            v.tensor_tensor_scan(hscan, ga, bz, 0.0, ALU.mult, ALU.add).then_inc(*did("scan"))

        def l2_output_tensor(pe, i):
            mm(pe, "out", "y", ["hsc"], [(W("l2_out"), hsc2)])
            ln_tensor(pe, "ln_out", yv, ["y"])

        def l2_output_vector(v, i):
            v.wait_ge(*last())
            v.tensor_scalar(xn, ln2[:, bass.ts(i, CH)], W("l2_b_out"), None, ALU.add).then_inc(*did("x"))
            v.wait_ge(*after("out"))
            v.wait_ge(*last())
            v.tensor_tensor(yv, xn, bank("vector", "out"), ALU.add).then_inc(*did("y"))
            ln_vector(v, "ln_out", yv, xn, wide=True)
            v.wait_ge(*last())
            v.tensor_scalar(xn, xn, W("l2_gamma"), W("l2_beta"), ALU.mult, ALU.add).then_inc(*did("scaled"))
            v.wait_ge(*last())
            v.tensor_tensor(h[:, bass.ts(i, CH)], h[:, bass.ts(i, CH)], xn, ALU.add).then_inc(*did("h_new"))

        def l2_output_scalar(a, i):
            a.wait_ge(*last())
            a.activation(HB(hsc2), pos_major(hscan, i), ACT.Copy).then_inc(*did("hsc"))
            ln_scalar(a, "ln_out", wide=True)

        r_h, r_sel = keep.take(B), keep.take(8)
        r_t = keep.take(2 * B)
        r_b = keep.take(8 * B)
        r_w = keep.take(64)

        def route_each_tensor(pe, i):
            head_tensor(pe)

        def route_tensor(pe):
            mm(pe, "h", "gelu", [], [(W("rt_1"), pool_)])
            ps = fill(pe, "logits", "logits_read")
            pe.wait_ge(*after("gelu"))
            pe.matmul(ps[0:B, 0:8], r_h, W("rt_2"), start=True, stop=False)
            pe.matmul(ps[0:B, 0:8], C("row0", 0, B), W("rt_b2"), start=False, stop=True).then_inc(*did("logits"))
            ps = fill(pe, "turned", "turned_read")
            pe.wait_ge(*after("sel"))
            for n in range(2):
                ins = pe.transpose(ps[0:4, n * B:(n + 1) * B], r_sel[0:B, 4 * n:4 * n + 4], C("ident")[0:B, 0:B])
            ins.then_inc(*did("turned"))
            ps = fill(pe, "spread", "spread_read")
            pe.wait_ge(*after("turned_read"))
            for n in range(2):
                for e in range(E2):
                    ins = pe.matmul(ps[:, (4 * n + e) * B:(4 * n + e + 1) * B], C("pick", e * P, (e + 1) * P),
                                    r_t[:, n * B:(n + 1) * B], start=True, stop=True)
            ins.then_inc(*did("spread"))

        def route_scalar(a):
            a.wait_ge(*after("h"))
            a.wait_ge(*last())
            a.activation(r_h, bank("scalar", "h")[:, 0:B], ACT.Gelu, bias=W("router_b1")).then_inc(*did("gelu"))

        def route_vector(v):
            l3 = r_w[0:B, 0:8].rearrange("p (n e) -> p n e", n=2)
            s3 = r_sel[0:B, :].rearrange("p (n e) -> p n e", n=2)
            c3 = r_w[0:B, 16:24].rearrange("p (n e) -> p n e", n=2)
            v.wait_ge(*after("logits"))
            v.wait_ge(*last())
            v.tensor_copy(r_w[0:B, 0:8], bank("vector", "logits")[0:B, 0:8]).then_inc(*did("logits_read"))
            v.wait_ge(*last())
            v.tensor_reduce(r_w[0:B, 8:10], l3, AX_X, ALU.max).then_inc(*did("max"))
            v.wait_ge(*last())
            v.tensor_tensor(s3, l3, r_w[0:B, 8:10].unsqueeze(2).to_broadcast([B, 2, 4]), ALU.is_ge).then_inc(*did("is_max"))
            v.wait_ge(*last())
            v.tensor_copy(c3, s3).then_inc(*did("count0"))
            for e in range(1, 4):
                v.wait_ge(*last())
                v.tensor_tensor(c3[:, :, e:e + 1], c3[:, :, e:e + 1], c3[:, :, e - 1:e], ALU.add).then_inc(*did(f"count{e}"))
            v.wait_ge(*last())
            v.tensor_scalar(c3, c3, 1.0, None, ALU.is_equal).then_inc(*did("first"))
            v.wait_ge(*last())
            v.tensor_tensor(s3, s3, c3, ALU.mult).then_inc(*did("sel"))
            v.wait_ge(*last())
            v.memset(r_t, 0.0).then_inc(*did("zeroed"))
            v.wait_ge(*after("turned"))
            v.wait_ge(*last())
            v.tensor_copy(r_t[0:4, :], bank("vector", "turned")[0:4, 0:2 * B]).then_inc(*did("turned_read"))
            v.wait_ge(*after("spread"))
            v.wait_ge(*last())
            v.tensor_copy(r_b, bank("vector", "spread")[:, 0:8 * B]).then_inc(*did("spread_read"))

        def pool_vector(v, i):
            head_vector(v)
            v.wait_ge(*after("ln.n"))
            v.wait_ge(*last())
            v.tensor_copy(ln2[:, bass.ts(i, CH)], xn).then_inc(*did("kept"))
            v.wait_ge(*last())
            v.tensor_reduce(gt[:, 0:CB], HB(xn), AX_X, ALU.add).then_inc(*did("sum"))
            v.wait_ge(*last())
            v.tensor_scalar(pool_[:, bass.ts(i, CB)], gt[:, 0:CB], 1.0 / T, None, ALU.mult).then_inc(*did("pooled"))

        ar = new_arena()
        ex = ar.take(4 * CH)
        ex_o = ar.take(4 * CH)
        selb = ar.take(CH)
        l2o = ar.take(CH)
        nrm = ar.take(CH)
        spatial, temporal = ar.take(TOK), ar.take(TOK)
        cr_kb = keep.take(4)

        def routed(n, name, wq, wk, wv, bias, wo, bo, w_gain, w_bias, mask):
            def mask_of(i):
                return r_b.rearrange("p (e b) -> p e b", b=B)[:, 4 * n:4 * n + 4, bass.ts(i, CB)]

            def tensor(pe, i):
                ln_tensor(pe, "ln", xn, ["xc"])
                for key, w, b, reader in (("q", wq, bias[0], "a.q_read"), ("k", wk, bias[1], "a.kx3"), ("v", wv, bias[2], "a.rep3")):
                    mm(pe, f"a.{key}", reader, ["ex3", "selb"],
                       [(w(e), ex[:, e * CH:(e + 1) * CH]) for e in range(4)] + [(b, selb)])
                core_tensor(pe, "a", C("ident"), ["a.rep3"], ["a.q_read", "a.kx3"])
                mm(pe, "y", "stored", ["exo3"], [(wo(e), ex_o[:, e * CH:(e + 1) * CH]) for e in range(4)] + [(bo, selb)])

            def vector(v, i):
                v.wait_ge(*last())
                v.memset(selb, 0.0).then_inc(*did("zero"))
                v.wait_ge(*last())
                v.tensor_copy(HB(selb[0:4, :]), r_t[0:4, n * B:(n + 1) * B][:, bass.ts(i, CB)].unsqueeze(2).to_broadcast([4, CB, T])).then_inc(*did("selb"))
                ln_vector(v, "ln", xn, nrm, ["xc"])
                v.wait_ge(*last())
                v.tensor_scalar(nrm, nrm, w_gain, w_bias, ALU.mult, ALU.add).then_inc(*did("gained"))
                for e in range(4):
                    v.wait_ge(*last())
                    v.tensor_tensor(HB(ex[:, e * CH:(e + 1) * CH]), HB(nrm),
                                    mask_of(i)[:, e, :].unsqueeze(2).to_broadcast([P, CB, T]), ALU.mult).then_inc(*did(f"ex{e}"))
                core_vector(v, "a", 0.25, mask)
                for e in range(4):
                    v.wait_ge(*after("a.o_read"))
                    v.wait_ge(*last())
                    v.tensor_tensor(HB(ex_o[:, e * CH:(e + 1) * CH]), HB(l2o),
                                    mask_of(i)[:, e, :].unsqueeze(2).to_broadcast([P, CB, T]), ALU.mult).then_inc(*did(f"exo{e}"))
                if n == 0:
                    v.wait_ge(*after("y"))
                    v.wait_ge(*last())
                    v.tensor_copy(spatial[:, bass.ts(i, CH)], bank("vector", "y")).then_inc(*did("stored"))
                else:
                    v.wait_ge(*after("y"))
                    v.wait_ge(*last())
                    v.tensor_tensor(temporal[:, bass.ts(i, CH)], nrm, bank("vector", "y"), ALU.add).then_inc(*did("stored"))

            def scalar(a, i):
                a.wait_ge(*last())
                a.activation(xn, ln2[:, bass.ts(i, CH)], ACT.Copy).then_inc(*did("xc"))
                ln_scalar(a, "ln")
                a.wait_ge(*after("a.q"))
                a.wait_ge(*last())
                a.activation(at_q, bank("scalar", "a.q"), ACT.Copy).then_inc(*did("a.q_read"))
                kx_scalar(a, "a")
                rep_scalar(a, "a", bank("scalar", "a.v"), ["a.v"])
                core_scalar(a, "a", 0.25 if mask is None else 1.0)
                a.wait_ge(*after("a.o"))
                a.wait_ge(*last())
                a.activation(l2o, bank("scalar", "a.o"), ACT.Copy).then_inc(*did("a.o_read"))
            return tensor, vector, scalar

        sp_bias = [W("sp_in_b", j * D, (j + 1) * D) for j in range(3)]
        spatial_stage = routed(0, "spatial", lambda e: W(f"sp_q{e}"), lambda e: W(f"sp_k{e}"), lambda e: W(f"sp_v{e}"),
                               sp_bias, lambda e: W(f"sp_o{e}"), W("sp_out_b"), W("norm_s_w"), W("norm_s_b"), None)
        temporal_stage = routed(1, "temporal", lambda e: W(f"tq_{e}"), lambda e: W(f"tk_{e}"), lambda e: W(f"tv_{e}"),
                                [W("tq_b"), W("tk_b"), W("tv_b")], lambda e: W(f"tp_{e}"), W("tp_b"),
                                W("norm_t_w"), W("norm_t_b"), lambda hh: C("causal"))

        def cross_tensor(pe, i):
            mm(pe, "a.q", "a.q_read", ["qin"], [(W("cr_in", 0, D), nrm)])
            mm(pe, "a.k", "a.kx3", ["kin"], [(W("cr_in", D, 2 * D), ex[:, 0:CH])])
            core_tensor(pe, "a", W("cr_in", 2 * D, 3 * D), ["a.rep3"], ["a.q_read", "a.kx3"])
            mm(pe, "y", "sum", ["a.o_read"], [(W("cr_out"), l2o)])

        def cross_vector(v, i):
            v.wait_ge(*last())
            v.tensor_scalar(cr_kb, C("head"), W("cross_in_b", 1, 2), None, ALU.mult).then_inc(*did("kb"))
            core_vector(v, "a", 0.25)
            v.wait_ge(*last())
            v.tensor_scalar(xn, ln2[:, bass.ts(i, CH)], W("cross_out_b"), None, ALU.add).then_inc(*did("x_bias"))
            v.wait_ge(*after("y"))
            v.wait_ge(*last())
            v.tensor_tensor(ln2[:, bass.ts(i, CH)], xn, bank("vector", "y"), ALU.add).then_inc(*did("sum"))

        def cross_scalar(a, i):
            a.wait_ge(*last())
            a.activation(nrm, spatial[:, bass.ts(i, CH)], ACT.Copy).then_inc(*did("qin"))
            a.wait_ge(*last())
            a.activation(ex[:, 0:CH], temporal[:, bass.ts(i, CH)], ACT.Copy).then_inc(*did("kin"))
            rep_scalar(a, "a", ex[:, 0:CH], ["kin"])
            a.wait_ge(*after("a.q"))
            a.wait_ge(*last())
            a.activation(at_q, bank("scalar", "a.q"), ACT.Identity, bias=W("cross_in_b", 0, 1)).then_inc(*did("a.q_read"))
            kx_scalar(a, "a", cr_kb, ["kb"])
            core_scalar(a, "a", 0.25)
            a.wait_ge(*after("a.o"))
            a.wait_ge(*last())
            a.activation(l2o, bank("scalar", "a.o"), ACT.Identity, bias=W("cross_in_b", 2, 3)).then_inc(*did("a.o_read"))

        def mlp_tensor(pe, i):
            ln_tensor(pe, "ln", xn, ["xc"])
            for f in range(4):
                mm(pe, f"u{f}", f"g{f}", ["gained"], [(W("mlp_1", f * P, (f + 1) * P), nrm)])
            mm(pe, "y", "h_new", ["g3"], [(W("mlp_2", f * D, (f + 1) * D), ex[:, f * CH:(f + 1) * CH]) for f in range(4)])

        def mlp_vector(v, i):
            ln_vector(v, "ln", xn, nrm, ["xc"])
            v.wait_ge(*last())
            v.tensor_scalar(nrm, nrm, W("norm_mlp_w"), W("norm_mlp_b"), ALU.mult, ALU.add).then_inc(*did("gained"))
            v.wait_ge(*last())
            v.tensor_scalar(hc, xn, W("mlp_b2"), None, ALU.add).then_inc(*did("x_bias"))
            v.wait_ge(*last())
            v.tensor_tensor(hc, hc, h[:, bass.ts(i, CH)], ALU.add).then_inc(*did("x_h"))
            residual_vector(v, i, "y")

        def mlp_scalar(a, i):
            a.wait_ge(*last())
            a.activation(xn, ln2[:, bass.ts(i, CH)], ACT.Copy).then_inc(*did("xc"))
            ln_scalar(a, "ln")
            for f in range(4):
                a.wait_ge(*after(f"u{f}"))
                a.wait_ge(*last())
                a.activation(ex[:, f * CH:(f + 1) * CH], bank("scalar", f"u{f}"), ACT.Gelu,
                             bias=W("mlp_b1", f, f + 1)).then_inc(*did(f"g{f}"))

        def l3_tensor(pe, i):
            head_tensor(pe)
            mm(pe, "a.q", "a.q_read", ["ln.n"], [(W("l3_q"), xn)])
            mm(pe, "a.k", "a.kx3", ["ln.n"], [(W("l3_k"), xn)])
            core_tensor(pe, "a", W("l3_v"), ["a.rep3"], ["a.q_read", "a.kx3"])

        def l3_vector(v, i):
            head_vector(v)
            core_vector(v, "a", 0.25, lambda hh: W("l3_rel", hh * T, (hh + 1) * T))
            v.wait_ge(*after("a.o"))
            v.wait_ge(*last())
            v.tensor_tensor(h[:, bass.ts(i, CH)], hc, bank("vector", "a.o"), ALU.add).then_inc(*did("a.o_read"))

        def l3_scalar(a, i):
            head_scalar(a, i)
            rep_scalar(a, "a", xn, ["ln.n"])
            a.wait_ge(*after("a.q"))
            a.wait_ge(*last())
            a.activation(at_q, bank("scalar", "a.q"), ACT.Copy).then_inc(*did("a.q_read"))
            kx_scalar(a, "a")
            core_scalar(a, "a", 1.0)

        ar = new_arena()
        r3 = [ar.take(CH) for _ in range(4)]
        lo2 = [ar.take(CH) for _ in range(4)]
        gl, gw3, gs3 = ar.take(NT * 5), ar.take(NT * 4), ar.take(64)
        wide = ar.take(NT * 64)
        wide_t, wlo = ar.take(CH), ar.take(CH)
        ER = E3 * R3

        def l3e_tensor(pe, i):
            head_tensor(pe)
            ps = fill(pe, "gates", "gates_read")
            pe.wait_ge(*after("ln.n"))
            for t in range(NT):
                ins = pe.matmul(ps[:, 5 * t:5 * t + 5], xn[:, t * P:(t + 1) * P], W("l3_gate", 0, 5),
                                start=True, stop=True)
            ins.then_inc(*did("gates"))
            for e in range(4):
                mm(pe, f"f{e}", f"relu{e}", [], [(W(f"fc1_{e}"), xn)])
            mm(pe, "lo", "wlo", ["relu3"], [(W("lora_a", e * ER, (e + 1) * ER), r3[e]) for e in range(4)])
            ps = fill(pe, "wide_t", "wide_t_read")
            pe.wait_ge(*after("wide"))
            for t in range(NT):
                ins = pe.transpose(ps[0:ER, t * P:(t + 1) * P], wide[:, t * ER:(t + 1) * ER], C("ident"))
            ins.then_inc(*did("wide_t"))
            for e in range(4):
                mm(pe, f"l{e}", f"lo{e}", ["wlo"], [(W("lora_b", e * D, (e + 1) * D)[0:ER, :], wlo[0:ER, :])])
            mm(pe, "y", "h_new", ["lo2", "lo3"], [(W(f"fc2_{e}"), lo2[e]) for e in range(4)])

        def l3e_vector(v, i):
            head_vector(v)
            g3 = gl.rearrange("p (t e) -> p t e", e=5)
            w3 = gw3.rearrange("p (t e) -> p t e", e=4)
            col = lambda n: gs3[:, 4 * n:4 * n + 4]
            sp = lambda n: col(n).unsqueeze(2).to_broadcast([P, NT, 4])
            v.wait_ge(*after("gates"))
            v.wait_ge(*last())
            v.tensor_copy(gl, bank("vector", "gates")[:, 0:20]).then_inc(*did("gates_read"))
            v.wait_ge(*last())
            v.tensor_reduce(col(0), g3[:, :, 0:4], AX_X, ALU.max).then_inc(*did("max"))
            v.wait_ge(*last())
            v.tensor_tensor(w3, g3[:, :, 0:4], sp(0), ALU.subtract).then_inc(*did("sub"))
            v.wait_ge(*after("gexp"))
            v.wait_ge(*last())
            v.tensor_reduce(col(1), w3, AX_X, ALU.add).then_inc(*did("esum"))
            v.wait_ge(*last())
            v.reciprocal(col(2), col(1)).then_inc(*did("erec"))
            v.wait_ge(*last())
            v.tensor_tensor(w3, w3, sp(2), ALU.mult).then_inc(*did("soft"))
            v.wait_ge(*after("tsig"))
            v.wait_ge(*last())
            v.tensor_scalar(col(4), col(3), 1.0 / E3, None, ALU.mult).then_inc(*did("thr"))
            v.wait_ge(*last())
            v.tensor_tensor(w3, w3, sp(4), ALU.subtract).then_inc(*did("adapted"))
            v.wait_ge(*last())
            v.tensor_scalar(gw3, gw3, 0.0, None, ALU.max).then_inc(*did("selected"))
            v.wait_ge(*last())
            v.tensor_reduce(col(5), w3, AX_X, ALU.add).then_inc(*did("wsum"))
            v.wait_ge(*last())
            v.tensor_scalar(col(6), col(5), 0.0, None, ALU.is_equal).then_inc(*did("none"))
            v.wait_ge(*last())
            v.tensor_tensor(col(5), col(5), col(6), ALU.add).then_inc(*did("wsum1"))
            v.wait_ge(*last())
            v.reciprocal(col(7), col(5)).then_inc(*did("wrec"))
            v.wait_ge(*last())
            v.tensor_tensor(w3, w3, sp(7), ALU.mult).then_inc(*did("weights"))
            v.wait_ge(*last())
            v.tensor_copy(wide.rearrange("p (te r) -> p te r", r=R3), gw3.unsqueeze(2).to_broadcast([P, NT * 4, R3])).then_inc(*did("wide"))
            v.wait_ge(*after("wide_t"))
            v.wait_ge(*last())
            v.tensor_copy(wide_t[0:ER, :], bank("vector", "wide_t")[0:ER, :]).then_inc(*did("wide_t_read"))
            v.wait_ge(*after("lo"))
            v.wait_ge(*last())
            v.tensor_tensor(wlo[0:ER, :], wide_t[0:ER, :], bank("vector", "lo")[0:ER, :], ALU.mult).then_inc(*did("wlo"))
            for e in range(1, 4, 2):
                v.wait_ge(*after(f"l{e}"))
                v.wait_ge(*last())
                v.tensor_copy(lo2[e], bank("vector", f"l{e}")).then_inc(*did(f"lo{e}"))
            residual_vector(v, i, "y")

        def l3e_scalar(a, i):
            head_scalar(a, i)
            a.wait_ge(*after("sub"))
            a.wait_ge(*last())
            a.activation(gw3, gw3, ACT.Exp).then_inc(*did("gexp"))
            for e in range(4):
                a.wait_ge(*after(f"f{e}"))
                a.wait_ge(*last())
                a.activation(r3[e], bank("scalar", f"f{e}"), ACT.Relu).then_inc(*did(f"relu{e}"))
            a.wait_ge(*last())
            a.activation(gs3[:, 12:16], gl.rearrange("p (t e) -> p t e", e=5)[:, :, 4], ACT.Sigmoid).then_inc(*did("tsig"))
            for e in range(0, 4, 2):
                a.wait_ge(*after(f"l{e}"))
                a.wait_ge(*last())
                a.activation(lo2[e], bank("scalar", f"l{e}"), ACT.Copy).then_inc(*did(f"lo{e}"))

        o_rows = new_arena().take(2 * CH).rearrange("p (k c) -> p k c", k=2)
        out_tiles = out.rearrange("b t d -> (b t) d").rearrange("(c k p) d -> c p k d", k=NT, p=P)

        def write_tensor(pe):
            for c in range(NCH):
                ps = fill(pe, f"t{c}", f"r{c}")
                for t in range(NT):
                    at = c * CH + t * P
                    ins = pe.transpose(ps[:, t * P:(t + 1) * P], h[:, at:at + P], C("ident"))
                ins.then_inc(*did(f"t{c}"))

        def write_scalar(a):
            for c in range(NCH):
                if c >= 2:
                    a.wait_ge(stored[c % 2], 16 * (c // 2))
                a.wait_ge(*after(f"t{c}"))
                a.wait_ge(*last())
                a.activation(o_rows[:, c % 2, :], bank("scalar", f"t{c}"), ACT.Copy).then_inc(*did(f"r{c}"))

        def write_sync(sp):
            for c in range(NCH):
                sp.wait_ge(*after(f"r{c}"))
                sp.dma_start(out_tiles[c], o_rows[:, c % 2, :].rearrange("p (k d) -> p k d", d=D)).then_inc(stored[c % 2], 16)
            for n in range(2):
                sp.wait_ge(stored[n], 16 * NCH // 2)

        def start_vector(v):
            v.wait_ge(*last())
            v.memset(gh, 0.0).then_inc(*did("h0"))

        block = ctx.enter_context(nc.Block())

        @block.sync
        def _(sp):
            sp.dma_start(vec[:, :], weights[:, vec_at:W_COLS]).then_inc(tok_loaded, 16)
            begin("sync", "select")
            select_sync(sp)
            lead(sp, "select")
            begin("sync", "l0_attention")
            with sp.Fori(0, NCH):
                lead(sp, "l0_attention")
            begin("sync", "gru_input")
            with sp.Fori(0, NCH):
                lead(sp, "gru_input")
            begin("sync", "gru_start")
            lead(sp, "gru_start")
            begin("sync", "gru")
            with sp.Fori(0, T):
                lead(sp, "gru")
            begin("sync", "gru_output")
            with sp.Fori(0, NCH):
                lead(sp, "gru_output")
            begin("sync", "l1_attention")
            with sp.Fori(0, NCH):
                lead(sp, "l1_attention")
            begin("sync", "experts")
            sp.dma_start(wt[:, 0:third_at - second_at], weights[:, second_at:third_at]).then_inc(second_loaded, 16)
            with sp.Fori(0, NCH):
                lead(sp, "experts")
            begin("sync", "l2_input")
            sp.dma_start(wt[:, experts_at:experts_at + vec_at - third_at],
                         weights[:, third_at:vec_at]).then_inc(third_loaded, 16)
            with sp.Fori(0, NCH):
                lead(sp, "l2_input")
            begin("sync", "l2_scan")
            lead(sp, "l2_scan")
            begin("sync", "l2_output")
            with sp.Fori(0, NCH):
                lead(sp, "l2_output")
            begin("sync", "pool")
            with sp.Fori(0, NCH):
                lead(sp, "pool")
            begin("sync", "route")
            lead(sp, "route")
            begin("sync", "l2_spatial")
            with sp.Fori(0, NCH):
                lead(sp, "l2_spatial")
            begin("sync", "l2_temporal")
            with sp.Fori(0, NCH):
                lead(sp, "l2_temporal")
            begin("sync", "l2_cross")
            with sp.Fori(0, NCH):
                lead(sp, "l2_cross")
            begin("sync", "l2_mlp")
            with sp.Fori(0, NCH):
                lead(sp, "l2_mlp")
            begin("sync", "l3_attention")
            with sp.Fori(0, NCH):
                lead(sp, "l3_attention")
            begin("sync", "l3_experts")
            with sp.Fori(0, NCH):
                lead(sp, "l3_experts")
            begin("sync", "write")
            write_sync(sp)
            lead(sp, "write")

        @block.tensor
        def _(pe):
            begin("tensor", "select")
            select_tensor(pe)
            meet(pe, "tensor", "select")
            begin("tensor", "l0_attention")
            with pe.Fori(0, NCH) as i:
                l0_tensor(pe, i)
                meet(pe, "tensor", "l0_attention")
            begin("tensor", "gru_input")
            with pe.Fori(0, NCH) as i:
                gru_input_tensor(pe, i)
                meet(pe, "tensor", "gru_input")
            begin("tensor", "gru_start")
            meet(pe, "tensor", "gru_start")
            begin("tensor", "gru")
            with pe.Fori(0, T) as i:
                gru_tensor(pe, i)
                meet(pe, "tensor", "gru")
            begin("tensor", "gru_output")
            with pe.Fori(0, NCH) as i:
                gru_output_tensor(pe, i)
                meet(pe, "tensor", "gru_output")
            begin("tensor", "l1_attention")
            with pe.Fori(0, NCH) as i:
                l1_tensor(pe, i)
                meet(pe, "tensor", "l1_attention")
            begin("tensor", "experts")
            with pe.Fori(0, NCH) as i:
                experts_tensor(pe, i)
                meet(pe, "tensor", "experts")
            begin("tensor", "l2_input")
            pe.wait_ge(second_loaded, 16)
            with pe.Fori(0, NCH) as i:
                l2_input_tensor(pe, i)
                meet(pe, "tensor", "l2_input")
            begin("tensor", "l2_scan")
            meet(pe, "tensor", "l2_scan")
            begin("tensor", "l2_output")
            with pe.Fori(0, NCH) as i:
                l2_output_tensor(pe, i)
                meet(pe, "tensor", "l2_output")
            begin("tensor", "pool")
            with pe.Fori(0, NCH) as i:
                route_each_tensor(pe, i)
                meet(pe, "tensor", "pool")
            begin("tensor", "route")
            route_tensor(pe)
            meet(pe, "tensor", "route")
            begin("tensor", "l2_spatial")
            with pe.Fori(0, NCH) as i:
                spatial_stage[0](pe, i)
                meet(pe, "tensor", "l2_spatial")
            begin("tensor", "l2_temporal")
            with pe.Fori(0, NCH) as i:
                temporal_stage[0](pe, i)
                meet(pe, "tensor", "l2_temporal")
            begin("tensor", "l2_cross")
            with pe.Fori(0, NCH) as i:
                cross_tensor(pe, i)
                meet(pe, "tensor", "l2_cross")
            begin("tensor", "l2_mlp")
            with pe.Fori(0, NCH) as i:
                mlp_tensor(pe, i)
                meet(pe, "tensor", "l2_mlp")
            begin("tensor", "l3_attention")
            pe.wait_ge(third_loaded, 16)
            with pe.Fori(0, NCH) as i:
                l3_tensor(pe, i)
                meet(pe, "tensor", "l3_attention")
            begin("tensor", "l3_experts")
            with pe.Fori(0, NCH) as i:
                l3e_tensor(pe, i)
                meet(pe, "tensor", "l3_experts")
            begin("tensor", "write")
            write_tensor(pe)
            meet(pe, "tensor", "write")

        @block.vector
        def _(v):
            begin("vector", "select")
            select_vector(v)
            meet(v, "vector", "select")
            begin("vector", "l0_attention")
            with v.Fori(0, NCH) as i:
                l0_vector(v, i)
                meet(v, "vector", "l0_attention")
            begin("vector", "gru_input")
            with v.Fori(0, NCH) as i:
                gru_input_vector(v, i)
                meet(v, "vector", "gru_input")
            begin("vector", "gru_start")
            start_vector(v)
            meet(v, "vector", "gru_start")
            begin("vector", "gru")
            with v.Fori(0, T) as i:
                gru_vector(v, i)
                meet(v, "vector", "gru")
            begin("vector", "gru_output")
            with v.Fori(0, NCH) as i:
                gru_output_vector(v, i)
                meet(v, "vector", "gru_output")
            begin("vector", "l1_attention")
            with v.Fori(0, NCH) as i:
                l1_vector(v, i)
                meet(v, "vector", "l1_attention")
            begin("vector", "experts")
            with v.Fori(0, NCH) as i:
                experts_vector(v, i)
                meet(v, "vector", "experts")
            begin("vector", "l2_input")
            v.wait_ge(second_loaded, 16)
            with v.Fori(0, NCH) as i:
                l2_input_vector(v, i)
                meet(v, "vector", "l2_input")
            begin("vector", "l2_scan")
            l2_scan_vector(v)
            meet(v, "vector", "l2_scan")
            begin("vector", "l2_output")
            with v.Fori(0, NCH) as i:
                l2_output_vector(v, i)
                meet(v, "vector", "l2_output")
            begin("vector", "pool")
            with v.Fori(0, NCH) as i:
                pool_vector(v, i)
                meet(v, "vector", "pool")
            begin("vector", "route")
            route_vector(v)
            meet(v, "vector", "route")
            begin("vector", "l2_spatial")
            with v.Fori(0, NCH) as i:
                spatial_stage[1](v, i)
                meet(v, "vector", "l2_spatial")
            begin("vector", "l2_temporal")
            with v.Fori(0, NCH) as i:
                temporal_stage[1](v, i)
                meet(v, "vector", "l2_temporal")
            begin("vector", "l2_cross")
            with v.Fori(0, NCH) as i:
                cross_vector(v, i)
                meet(v, "vector", "l2_cross")
            begin("vector", "l2_mlp")
            with v.Fori(0, NCH) as i:
                mlp_vector(v, i)
                meet(v, "vector", "l2_mlp")
            begin("vector", "l3_attention")
            v.wait_ge(third_loaded, 16)
            with v.Fori(0, NCH) as i:
                l3_vector(v, i)
                meet(v, "vector", "l3_attention")
            begin("vector", "l3_experts")
            with v.Fori(0, NCH) as i:
                l3e_vector(v, i)
                meet(v, "vector", "l3_experts")
            begin("vector", "write")
            meet(v, "vector", "write")

        @block.scalar
        def _(a):
            begin("scalar", "select")
            select_scalar(a)
            meet(a, "scalar", "select")
            begin("scalar", "l0_attention")
            with a.Fori(0, NCH) as i:
                l0_scalar(a, i)
                meet(a, "scalar", "l0_attention")
            begin("scalar", "gru_input")
            with a.Fori(0, NCH) as i:
                gru_input_scalar(a, i)
                meet(a, "scalar", "gru_input")
            begin("scalar", "gru_start")
            meet(a, "scalar", "gru_start")
            begin("scalar", "gru")
            with a.Fori(0, T) as i:
                gru_scalar(a, i)
                meet(a, "scalar", "gru")
            begin("scalar", "gru_output")
            with a.Fori(0, NCH) as i:
                gru_output_scalar(a, i)
                meet(a, "scalar", "gru_output")
            begin("scalar", "l1_attention")
            with a.Fori(0, NCH) as i:
                l1_scalar(a, i)
                meet(a, "scalar", "l1_attention")
            begin("scalar", "experts")
            with a.Fori(0, NCH) as i:
                experts_scalar(a, i)
                meet(a, "scalar", "experts")
            begin("scalar", "l2_input")
            a.wait_ge(second_loaded, 16)
            with a.Fori(0, NCH) as i:
                l2_input_scalar(a, i)
                meet(a, "scalar", "l2_input")
            begin("scalar", "l2_scan")
            meet(a, "scalar", "l2_scan")
            begin("scalar", "l2_output")
            with a.Fori(0, NCH) as i:
                l2_output_scalar(a, i)
                meet(a, "scalar", "l2_output")
            begin("scalar", "pool")
            with a.Fori(0, NCH) as i:
                head_scalar(a, i)
                meet(a, "scalar", "pool")
            begin("scalar", "route")
            route_scalar(a)
            meet(a, "scalar", "route")
            begin("scalar", "l2_spatial")
            with a.Fori(0, NCH) as i:
                spatial_stage[2](a, i)
                meet(a, "scalar", "l2_spatial")
            begin("scalar", "l2_temporal")
            with a.Fori(0, NCH) as i:
                temporal_stage[2](a, i)
                meet(a, "scalar", "l2_temporal")
            begin("scalar", "l2_cross")
            with a.Fori(0, NCH) as i:
                cross_scalar(a, i)
                meet(a, "scalar", "l2_cross")
            begin("scalar", "l2_mlp")
            with a.Fori(0, NCH) as i:
                mlp_scalar(a, i)
                meet(a, "scalar", "l2_mlp")
            begin("scalar", "l3_attention")
            a.wait_ge(third_loaded, 16)
            with a.Fori(0, NCH) as i:
                l3_scalar(a, i)
                meet(a, "scalar", "l3_attention")
            begin("scalar", "l3_experts")
            with a.Fori(0, NCH) as i:
                l3e_scalar(a, i)
                meet(a, "scalar", "l3_experts")
            begin("scalar", "write")
            write_scalar(a)
            meet(a, "scalar", "write")

        @block.gpsimd
        def _(g):
            begin("gpsimd", "select")
            select_gpsimd(g)
            meet(g, "gpsimd", "select")
            begin("gpsimd", "l0_attention")
            with g.Fori(0, NCH) as i:
                meet(g, "gpsimd", "l0_attention")
            begin("gpsimd", "gru_input")
            with g.Fori(0, NCH) as i:
                meet(g, "gpsimd", "gru_input")
            begin("gpsimd", "gru_start")
            meet(g, "gpsimd", "gru_start")
            begin("gpsimd", "gru")
            with g.Fori(0, T) as i:
                meet(g, "gpsimd", "gru")
            begin("gpsimd", "gru_output")
            with g.Fori(0, NCH) as i:
                meet(g, "gpsimd", "gru_output")
            begin("gpsimd", "l1_attention")
            with g.Fori(0, NCH) as i:
                meet(g, "gpsimd", "l1_attention")
            begin("gpsimd", "experts")
            with g.Fori(0, NCH) as i:
                meet(g, "gpsimd", "experts")
            begin("gpsimd", "l2_input")
            g.wait_ge(second_loaded, 16)
            with g.Fori(0, NCH) as i:
                meet(g, "gpsimd", "l2_input")
            begin("gpsimd", "l2_scan")
            meet(g, "gpsimd", "l2_scan")
            begin("gpsimd", "l2_output")
            with g.Fori(0, NCH) as i:
                meet(g, "gpsimd", "l2_output")
            begin("gpsimd", "pool")
            with g.Fori(0, NCH) as i:
                meet(g, "gpsimd", "pool")
            begin("gpsimd", "route")
            meet(g, "gpsimd", "route")
            begin("gpsimd", "l2_spatial")
            with g.Fori(0, NCH) as i:
                meet(g, "gpsimd", "l2_spatial")
            begin("gpsimd", "l2_temporal")
            with g.Fori(0, NCH) as i:
                meet(g, "gpsimd", "l2_temporal")
            begin("gpsimd", "l2_cross")
            with g.Fori(0, NCH) as i:
                meet(g, "gpsimd", "l2_cross")
            begin("gpsimd", "l2_mlp")
            with g.Fori(0, NCH) as i:
                meet(g, "gpsimd", "l2_mlp")
            begin("gpsimd", "l3_attention")
            g.wait_ge(third_loaded, 16)
            with g.Fori(0, NCH) as i:
                meet(g, "gpsimd", "l3_attention")
            begin("gpsimd", "l3_experts")
            with g.Fori(0, NCH) as i:
                meet(g, "gpsimd", "l3_experts")
            begin("gpsimd", "write")
            meet(g, "gpsimd", "write")
    if known is not None:
        steps.check_order()
    return steps


def kernel(**inputs):
    import concourse.bacc as bacc
    from concourse.bass_utils import run_bass_kernel_spmd

    x = np.ascontiguousarray(inputs["x"])
    a = {k: np.asarray(v) for k, v in inputs.items()}
    packed = np.concatenate([lay(a).astype(np.float32, copy=False) for _, _, lay in weight_list()], axis=1)
    consts = np.concatenate([np.asarray(c, np.float32).reshape(P, -1) for _, c in constant_list()], axis=1)

    def program(known):
        nc = bacc.Bacc("TRN2", target_bir_lowering=False, num_devices=1)
        args = [nc.dram_tensor(n, v.shape, F32, kind="ExternalInput").ap()
                for n, v in (("in_x", x), ("in_w", packed), ("in_c", consts))]
        o = nc.dram_tensor("out_0", (B, T, D), F32, kind="ExternalOutput").ap()
        return nc, tower(nc, *args, o, known)
    _, counts = program(None)
    nc, _ = program(counts)
    r = run_bass_kernel_spmd(nc, [{"in_x": x, "in_w": np.ascontiguousarray(packed), "in_c": consts}], core_ids=[0])
    return r.results[0]["out_0"]
```

```python
from contextlib import ExitStack

import numpy as np

import concourse.bass as bass
from concourse import mybir

F32 = mybir.dt.float32
U32 = mybir.dt.uint32
ALU = mybir.AluOpType
ACT = mybir.ActivationFunctionType
AX_X = mybir.AxisListType.X

P = 128
D = 128
B = 64
S_IN = 256
BLOCK = 128
TOP = 16
T = S_IN // BLOCK * TOP
TOK = B * T
CH = 512
NCH = TOK // CH
CB = CH // T
NT = CH // P
E1 = 8
E2 = 4
E3 = 4
GRU_U = 8
R3 = 16
EPS = 1e-5
NEG = -1e30
WIDE = 2.0 ** -10
XG = 8



def _blocks(w):
    k = w.shape[0] // P
    return w.reshape(k, P, w.shape[1]).transpose(1, 0, 2).reshape(P, k * w.shape[1])


def _rows(w):
    out = np.zeros((P, w.shape[1]), w.dtype)
    out[: w.shape[0]] = w
    return out


def _cols(v):
    return v.reshape(-1, P).T


def _adapter_a(w):
    out = np.zeros((P, E3 * R3 * E3), w.dtype)
    for e in range(E3):
        at = e * E3 * R3 + e * R3
        out[:, at:at + R3] = w[e]
    return out


def _adapter_b(w):
    out = np.zeros((P, E3 * D), w.dtype)
    for e in range(E3):
        out[e * R3:(e + 1) * R3, e * D:(e + 1) * D] = w[e]
    return out


def _relative(w):
    i, j = np.arange(T)[:, None], np.arange(T)[None, :]
    m = w[0][:, i - j + 63].reshape(2, 4, T, T)
    return m.transpose(1, 2, 0, 3).reshape(P, 2 * T)


def weight_list():
    w = []

    def add(name, n, lay):
        w.append((name, n, lay))
    for n in ("q_u", "k_u", "v_u", "q_c", "k_c", "v_c"):
        add(n, 512, lambda a, n=n: a["L0_attn_w_" + n])
    add("l0_out", 512, lambda a: _blocks(a["L0_attn_w_out"]))
    for n in ("uz", "ur", "u"):
        add("g_" + n, 256, lambda a, n=n: a["L0_ffn_W" + n].T)
    for n in ("wz", "wr", "w"):
        add("g_" + n, 512, lambda a, n=n: _blocks(a["L0_ffn_W" + n].T))
    add("g_o", 256, lambda a: _blocks(a["L0_ffn_Wo"].T))
    for s in range(3):
        add(f"l1_qkv{s}", 384, lambda a, s=s: a["L1_attn_Wqkv"][s].T)
        add(f"l1_o{s}", 128, lambda a, s=s: a["L1_attn_Wo"][s].T)
    add("l1_f", 384, lambda a: _blocks(a["L1_attn_Wf"].T))
    add("moe_r", 8, lambda a: a["L1_ffn_w_r"].T)
    add("moe_br", 8, lambda a: _rows(a["L1_ffn_b_r"][None]))
    add("moe_b2", 128, lambda a: _rows(a["L1_ffn_b2"]))
    for e in range(E1):
        add(f"moe_1_{e}", 512, lambda a, e=e: a["L1_ffn_W1"][e])
        add(f"moe_2_{e}", 512, lambda a, e=e: _blocks(a["L1_ffn_W2"][e]))
    add("l2_in", 256, lambda a: a["L2_attn_W_in"].T)
    add("l2_out", 128, lambda a: a["L2_attn_W_out"].T)
    add("rt_1", 128, lambda a: a["L2_ffn_router_w1"].T)
    add("rt_2", 8, lambda a: a["L2_ffn_router_w2"].T)
    add("rt_b2", 8, lambda a: _rows(a["L2_ffn_router_b2"][None]))
    for e in range(E2):
        add(f"sp_q{e}", 128, lambda a, e=e: a["L2_ffn_sp_in_w"][e][:D].T)
        add(f"sp_k{e}", 128, lambda a, e=e: a["L2_ffn_sp_in_w"][e][D:2 * D].T)
        add(f"sp_v{e}", 128, lambda a, e=e: a["L2_ffn_sp_in_w"][e][2 * D:].T)
        add(f"sp_o{e}", 128, lambda a, e=e: a["L2_ffn_sp_out_w"][e].T)
        for n in "qkvp":
            add(f"t{n}_{e}", 128, lambda a, e=e, n=n: a[f"L2_ffn_t{n}_w"][e].T)
    add("sp_in_b", 384, lambda a: _rows(a["L2_ffn_sp_in_b"]))
    add("sp_out_b", 128, lambda a: _rows(a["L2_ffn_sp_out_b"]))
    for n in "qkvp":
        add(f"t{n}_b", 128, lambda a, n=n: _rows(a[f"L2_ffn_t{n}_b"]))
    add("cr_in", 384, lambda a: a["L2_ffn_cross_in_w"].T)
    add("cr_out", 128, lambda a: a["L2_ffn_cross_out_w"].T)
    add("mlp_1", 512, lambda a: a["L2_ffn_mlp_w1"].T)
    add("mlp_2", 512, lambda a: _blocks(a["L2_ffn_mlp_w2"].T))
    for n in "qkv":
        add("l3_" + n, 128, lambda a, n=n: a["L3_attn_W" + n].T)
    add("l3_rel", 2 * T, lambda a: _relative(a["L3_attn_rel_pos_bias"]))
    add("l3_gate", 4, lambda a: a["L3_ffn_gate_w"].T)
    add("l3_thr", 1, lambda a: a["L3_ffn_thr_w"].T)
    for e in range(E3):
        add(f"fc1_{e}", 128, lambda a, e=e: a["L3_ffn_fc1_w"][e].T)
        add(f"fc2_{e}", 128, lambda a, e=e: a["L3_ffn_fc2_w"][e].T)
    add("lora_a", E3 * E3 * R3, lambda a: _adapter_a(a["L3_ffn_lora_A"]))
    add("lora_b", E3 * D, lambda a: _adapter_b(a["L3_ffn_lora_B"]))
    add("tok_w", D, lambda a: np.broadcast_to(a["L0_tok_W"], (P, D)))
    add("tok_b", 1, lambda a: np.broadcast_to(a["L0_tok_b"][None], (P, 1)))
    for n in ("buz", "bwz", "bur", "bwr", "bu", "bw"):
        add(n, 2, lambda a, n=n: _cols(a["L0_ffn_" + n]))
    add("g_bo", 1, lambda a: _cols(a["L0_ffn_bo"]))
    for s in range(3):
        add(f"l1_bqkv{s}", 3, lambda a, s=s: _cols(a["L1_attn_bqkv"][s]))
        add(f"l1_bo{s}", 1, lambda a, s=s: _cols(a["L1_attn_bo"][s]))
    add("l1_bf", 1, lambda a: _cols(a["L1_attn_bf"]))
    add("ln_g", 1, lambda a: _cols(a["L1_ffn_ln_g"]))
    add("ln_b", 1, lambda a: _cols(a["L1_ffn_ln_b"]))
    add("moe_b1", 4 * E1, lambda a: _cols(a["L1_ffn_b1"].reshape(-1)))
    add("l2_bin", 2, lambda a: _cols(a["L2_attn_b_in"]))
    for n in ("b_out", "A", "B", "gamma", "beta"):
        add("l2_" + n, 1, lambda a, n=n: _cols(a["L2_attn_" + n]))
    for n in ("router_b1", "norm_s_w", "norm_s_b", "norm_t_w", "norm_t_b", "norm_mlp_w", "norm_mlp_b",
              "cross_out_b", "mlp_b2"):
        add(n, 1, lambda a, n=n: _cols(a["L2_ffn_" + n]))
    add("cross_in_b", 3, lambda a: _cols(a["L2_ffn_cross_in_b"]))
    add("mlp_b1", 4, lambda a: _cols(a["L2_ffn_mlp_b1"]))
    return w


VECTORS_FROM, SECOND_FROM, THIRD_FROM = "tok_w", "l2_in", "l3_q"


def constant_list():
    p = np.arange(P)
    row = p % T
    j, q = np.arange(T), np.arange(4)
    f = np.arange(P)
    later = (j[None, :] >= row[:, None])
    same = (p[:, None] // 32 == q[None, :])

    def band(width):
        d = row[:, None] - j[None, :]
        return np.where((d >= 0) & (d < width), 0.0, NEG)
    return [
        ("ident", np.eye(P)),
        ("mean", np.full((P, P), 1.0 / P)),
        ("half", p[:, None] // 64 == np.arange(2)[None]),
        ("head", (p[:, None] // 16) % 4 == q[None]),
        ("v16", (f[None] // 16) % 4 == p[:, None] // 32),
        ("v64", f[None] // 64 == (p[:, None] // 32) % 2),
        ("t1m", (same[:, :, None] * later[:, None, :] * 0.125).reshape(P, P)),
        ("sgm", row[:, None] > j[None, :]),
        ("causal", band(T)), ("band5", band(5)), ("band10", band(10)),
        ("base", p[:, None] * BLOCK),
        ("iota8", np.broadcast_to(np.arange(8), (P, 8))),
        ("row0", np.broadcast_to(p[:, None] == 0, (P, P))),
        ("pick", (p[:, None, None] == q[None, :, None]) * np.ones((1, 1, P))),
        ("eps", np.full((P, 1), EPS)),
        ("eps_wide", np.full((P, 1), EPS * WIDE ** 2)),
        ("zero", np.zeros((P, 1))),
    ]


def offsets(items):
    at, out = 0, {}
    for name, n in items:
        out[name] = (at, n)
        at += n
    return out, at


W_AT, W_COLS = offsets([(n, c) for n, c, _ in weight_list()])
C_AT, C_COLS = offsets([(n, int(np.prod(np.asarray(a).shape[1:]))) for n, a in constant_list()])


class Steps:

    def __init__(self, known):
        self.known = known
        self.table, self.banks, self.sems, self.log = {}, {}, {}, {}

    def begin(self, who, stage):
        self.who, self.stage, self.count = who, stage, 0

    def did(self, key):
        self.count += 1
        assert (self.stage, key) not in self.table, (self.stage, key)
        self.table[self.stage, key] = (self.who, self.count)
        self.log.setdefault((self.stage, self.who), []).append(("did", key))
        return self.sems[self.stage, self.who], 1

    def after(self, key):
        self.log.setdefault((self.stage, self.who), []).append(("after", key))
        by, n = self.known.table[self.stage, key] if self.known else (ENGINES[0], 1)
        return self.sems[self.stage, by], n

    def last(self):
        return self.sems[self.stage, self.who], self.count

    def check_order(self):
        for stage in dict.fromkeys(s for s, _ in self.log):
            lists = {w: l for (s, w), l in self.log.items() if s == stage}
            at, done = dict.fromkeys(lists, 0), set()
            moved = True
            while moved:
                moved = False
                for w, l in lists.items():
                    while at[w] < len(l) and (l[at[w]][0] == "did" or l[at[w]][1] in done):
                        if l[at[w]][0] == "did":
                            done.add(l[at[w]][1])
                        at[w] += 1
                        moved = True
            stuck = {w: l[at[w]] for w, l in lists.items() if at[w] < len(l)}
            assert not stuck, (stage, stuck)


STAGES = ["select", "l0_norm", "l0_attention", "gru_norm", "gru_input", "gru_start", "gru", "gru_output", "l1_norm",
          "l1_attention", "experts_norm", "experts_norm2", "experts", "l2_norm", "l2_input", "l2_scan", "l2_output",
          "pool", "route", "l2_norm_again", "l2_spatial", "l2_temporal", "l2_cross", "mlp_norm", "l2_mlp",
          "l3_norm", "l3_attention", "l3_experts_norm", "l3_experts", "write"]
ENGINES = ("tensor", "vector", "scalar", "gpsimd")


def tower(nc, x, weights, constants, out, known):
    steps = Steps(known)
    did, after, last = steps.did, steps.after, steps.last
    with ExitStack() as ctx:
        def sem(name):
            return ctx.enter_context(nc.semaphore(name))

        h = ctx.enter_context(nc.sbuf_tensor("h", [P, TOK], F32))
        xa = ctx.enter_context(nc.sbuf_tensor("xa", [P, TOK], F32))
        ln2 = ctx.enter_context(nc.sbuf_tensor("ln2", [P, TOK], F32))
        vec_at, second_at = W_AT[VECTORS_FROM][0], W_AT[SECOND_FROM][0]
        wt = ctx.enter_context(nc.sbuf_tensor("wt", [P, second_at], F32))
        third_at, experts_at = W_AT[THIRD_FROM][0], W_AT["moe_r"][0]
        assert third_at - second_at <= experts_at
        vec = ctx.enter_context(nc.sbuf_tensor("vec", [P, W_COLS - vec_at], F32))
        cs = ctx.enter_context(nc.sbuf_tensor("cs", [P, C_COLS], F32))
        arena = ctx.enter_context(nc.sbuf_tensor("arena", [P, 18432], F32))
        psum = ctx.enter_context(nc.psum_tensor("psum", [P, 8, 512], F32))
        small = ctx.enter_context(nc.sbuf_tensor("small", [P, 944], F32))

        for s in STAGES:
            for who in ENGINES:
                steps.sems[s, who] = sem(f"{s}_{who}_done")
        x_loaded = [sem("x_loaded0"), sem("x_loaded1")]
        c_loaded, w_loaded = sem("constants_loaded"), sem("weights_loaded")
        gathered, stored = sem("rows_gathered"), [sem("output_stored0"), sem("output_stored1")]
        arrived = sem("engines_arrived")
        go = {who: sem(f"{who}_may_go") for who in ENGINES}

        def W(name, a=0, b=None):
            at, n = W_AT[name]
            b = n if b is None else b
            if at >= vec_at:
                return vec[:, at - vec_at + a:at - vec_at + b]
            if at >= third_at:
                at += experts_at - third_at
            elif at >= second_at:
                at -= second_at
            return wt[:, at + a:at + b]

        def C(name, a=0, b=None):
            at, n = C_AT[name]
            return cs[:, at + a:at + (n if b is None else b)]

        class Places:

            def __init__(self, buf, size):
                self.buf, self.at, self.size = buf, 0, size

            def take(self, n):
                a = self.at
                self.at += n
                assert self.at <= self.size, (self.at, self.size)
                return self.buf[:, a:a + n]

        def new_arena():
            return Places(arena, 18432)
        keep = Places(small, 944)

        def meet(eng, who, stage):
            eng.drain()
            eng.sem_inc(arrived, 1)
            eng.wait_ge(go[who], 1)
            eng.sem_clear(go[who])

        def lead(sp, stage):
            sp.wait_ge(arrived, len(ENGINES))
            sp.sem_clear(arrived)
            for who in ENGINES:
                sp.sem_clear(steps.sems[stage, who])
            for who in ENGINES:
                sp.sem_inc(go[who], 1)

        ring = {"next": 0, "reader": {}}

        def fill(pe, key, reader):
            b = ring["next"]
            ring["next"] = (b + 1) % 8
            if b in ring["reader"]:
                pe.wait_ge(*after(ring["reader"][b]))
            ring["reader"][b] = reader
            steps.banks[steps.stage, key] = b
            return psum[:, b, :]

        def bank(who, key):
            if steps.known is None:
                return psum[:, 0, :]
            return psum[:, steps.known.banks[steps.stage, key], :]

        def begin(who, stage):
            steps.begin(who, stage)
            if who == "tensor":
                ring["next"], ring["reader"] = 0, {}

        ATT = 8800
        att = ctx.enter_context(nc.sbuf_tensor("att", [P, ATT], F32))

        def part(buf, c):
            return buf[:, c * CH:(c + 1) * CH]

        centred, squares = att[:, 0:TOK], att[:, TOK:2 * TOK]

        def norm_tensor(pe, src, ready=None):
            for c in range(NCH):
                ps = fill(pe, f"mean{c}", f"centred{c}")
                if ready is not None:
                    pe.wait_ge(*after(f"{ready}{c}"))
                pe.matmul(ps, C("mean"), part(src, c), start=True, stop=True).then_inc(*did(f"mean{c}"))
            for c in range(NCH):
                ps = fill(pe, f"var{c}", f"log{c}")
                pe.wait_ge(*after(f"square{c}"))
                pe.matmul(ps, C("mean"), part(squares, c), start=True, stop=True).then_inc(*did(f"var{c}"))

        def norm_scalar(a, wide=False):
            for c in range(NCH):
                a.wait_ge(*after(f"centred{c}"))
                a.wait_ge(*last())
                a.activation(part(squares, c), part(centred, c), ACT.Square, scale=WIDE if wide else 1.0).then_inc(*did(f"square{c}"))
            for c in range(NCH):
                a.wait_ge(*after(f"fits{c}" if wide else f"var{c}"))
                a.wait_ge(*last())
                a.activation(part(squares, c), bank("scalar", f"var{c}"), ACT.Sqrt if wide else ACT.Ln,
                             bias=C("eps_wide") if wide else C("eps")).then_inc(*did(f"log{c}"))
            if not wide:
                for c in range(NCH):
                    a.wait_ge(*last())
                    a.activation(part(squares, c), part(squares, c), ACT.Exp, scale=-0.5, bias=C("zero")).then_inc(*did(f"rstd{c}"))

        def centre_vector(v, src, c):
            v.wait_ge(*after(f"mean{c}"))
            v.wait_ge(*last())
            v.tensor_tensor(part(centred, c), part(src, c), bank("vector", f"mean{c}"), ALU.subtract).then_inc(*did(f"centred{c}"))

        def norm(src, dst, gain=None, bias=None):
            def tensor(pe):
                norm_tensor(pe, src)

            def vector(v):
                for c in range(NCH):
                    centre_vector(v, src, c)
                for c in range(NCH):
                    v.wait_ge(*after(f"rstd{c}"))
                    v.wait_ge(*last())
                    v.tensor_tensor(part(dst, c), part(centred, c), part(squares, c), ALU.mult).then_inc(*did(f"n{c}"))
                    if gain is not None:
                        v.wait_ge(*last())
                        v.tensor_scalar(part(dst, c), part(dst, c), gain, bias, ALU.mult, ALU.add).then_inc(*did(f"gained{c}"))
            return tensor, vector, norm_scalar

        norm_h_xa, norm_h_ln2, norm_ln2_xa = norm(h, xa), norm(h, ln2), norm(ln2, xa)
        norm_experts = norm(xa, ln2, W("ln_g"), W("ln_b"))
        norm_mlp = norm(ln2, xa, W("norm_mlp_w"), W("norm_mlp_b"))

        def mm(pe, key, reader, needs, products):
            ps = fill(pe, key, reader)
            for step in needs:
                pe.wait_ge(*after(step))
            n = len(products)
            for i, (lhs, rhs) in enumerate(products):
                m = lhs.shape[1]
                ins = pe.matmul(ps[0:m, 0:rhs.shape[-1]] if len(rhs.shape) == 2 else ps[0:m, :].rearrange("p (a b) -> p a b", b=rhs.shape[-1]),
                                lhs, rhs, start=i == 0, stop=i == n - 1)
            ins.then_inc(*did(key))

        HB = lambda ap: ap.rearrange("p (b t) -> p b t", t=T)

        ar = new_arena()
        xin = [ar.take(2048), ar.take(2048)]
        prod = ar.take(2048)
        rows = ar.take(TOP * D)
        score, work = ar.take(BLOCK), ar.take(BLOCK)
        val, idx, idf = ar.take(TOP), ar.take(TOP).bitcast(U32), ar.take(TOP)
        x_blocks = x.rearrange("b (n s) d -> (b n) (s d)", s=BLOCK)
        x_rows = x.rearrange("b s d -> (b s) d")

        def select_sync(sp):
            for n in range(XG):
                if n >= 2:
                    sp.wait_ge(*after(f"prod{n - 2}"))
                sp.dma_start(xin[n % 2], x_blocks[:, 2048 * n:2048 * (n + 1)]).then_inc(x_loaded[n % 2], 16)
                if n == 1:
                    sp.dma_start(cs[:, :], constants).then_inc(c_loaded, 16)
            for a in range(0, second_at, W_STEP):
                b = min(a + W_STEP, second_at)
                sp.dma_start(wt[:, a:b], weights[:, a:b]).then_inc(w_loaded, 16)

        W_STEP = 4096
        n_weight_loads = len(range(0, second_at, W_STEP))

        def select_vector(v):
            w_row = W("tok_w").unsqueeze(1).to_broadcast([P, 16, D])
            v.wait_ge(tok_loaded, 16)
            for n in range(XG):
                v.wait_ge(x_loaded[n % 2], 16 * (n // 2 + 1))
                v.wait_ge(*last())
                v.tensor_tensor(prod.rearrange("p (s d) -> p s d", d=D), xin[n % 2].rearrange("p (s d) -> p s d", d=D),
                                w_row, ALU.mult).then_inc(*did(f"prod{n}"))
                v.wait_ge(*last())
                v.tensor_reduce(score[:, 16 * n:16 * n + 16], prod.rearrange("p (s d) -> p s d", d=D), AX_X,
                                ALU.add).then_inc(*did(f"score{n}"))
            v.wait_ge(*last())
            v.tensor_scalar(score, score, tok_b[:, 0:1], None, ALU.add).then_inc(*did("score"))
            src = score
            for r in range(2):
                v.wait_ge(*last())
                v.max(val[:, 8 * r:8 * r + 8], src).then_inc(*did(f"max{r}"))
                v.wait_ge(*last())
                v.max_index(idx[:, 8 * r:8 * r + 8], val[:, 8 * r:8 * r + 8], src).then_inc(*did(f"index{r}"))
                if r == 0:
                    v.wait_ge(*last())
                    v.match_replace(work, val[:, 0:8], src, -3e38).then_inc(*did("taken"))
                    src = work
            v.wait_ge(*last())
            v.tensor_copy(idf, idx).then_inc(*did("index_f"))
            v.wait_ge(c_loaded, 16)
            v.wait_ge(*last())
            v.tensor_scalar(idx, idf, C("base"), None, ALU.add).then_inc(*did("row_index"))

        def select_gpsimd(g):
            g.wait_ge(*after("row_index"))
            for r in range(TOP):
                g.indirect_dma_start(out=rows[:, r * D:(r + 1) * D], out_offset=None, in_=x_rows,
                                     in_offset=bass.IndirectOffsetOnAxis(ap=idx[:, r:r + 1], axis=0)).then_inc(gathered, 16)

        def select_tensor(pe):
            pe.wait_ge(c_loaded, 16)
            pe.wait_ge(gathered, 16 * TOP)
            for q in range(4):
                ps = fill(pe, f"turn{q}", f"h{q}")
                for r in range(4):
                    at = 4 * q + r
                    ins = pe.transpose(ps[:, r * P:(r + 1) * P], rows[:, at * D:(at + 1) * D], C("ident"))
                ins.then_inc(*did(f"turn{q}"))

        def select_scalar(a):
            for q in range(4):
                a.wait_ge(*after(f"turn{q}"))
                a.wait_ge(*last())
                a.activation(h[:, :].rearrange("p (n r) -> p r n", r=TOP)[:, 4 * q:4 * q + 4, :],
                             bank("scalar", f"turn{q}").rearrange("p (r n) -> p r n", n=P), ACT.Copy).then_inc(*did(f"h{q}"))
            a.wait_ge(w_loaded, 16 * n_weight_loads)
            a.wait_ge(c_loaded, 16)
            a.wait_ge(tok_loaded, 16)

        tok_loaded = sem("vectors_loaded")
        second_loaded, third_loaded = sem("layer2_weights_loaded"), sem("layer3_weights_loaded")
        tok_b = W("tok_b")

        class Attention:
            def __init__(self, places):
                self.q, self.rep, self.kx, self.vx = places.take(CH), places.take(4 * CH), places.take(4 * CH), places.take(CB * D)
                self.s = [places.take(CH), places.take(CH)]
                self.p = [places.take(CH), places.take(CH)]
                self.st = [places.take(3 * CB), places.take(3 * CB)]
                self.rep4 = self.rep.rearrange("p (b q t) -> p b q t", q=4, t=T)
                self.kx4 = self.kx.rearrange("p (b q t) -> p b q t", q=4, t=T)

        at0 = Attention(Places(att, ATT))
        at_q, at_rep, at_kx, at_vx, at_s, at_p, at_st = at0.q, at0.rep, at0.kx, at0.vx, at0.s, at0.p, at0.st

        def softmax_max_vector(v, k, s, st):
            s3 = HB(s)
            v.wait_ge(*last())
            v.tensor_reduce(st[:, 0:CB], s3, AX_X, ALU.max).then_inc(*did(f"{k}.max"))
            v.wait_ge(*last())
            v.tensor_tensor(s3, s3, st[:, 0:CB].unsqueeze(2).to_broadcast([P, CB, T]), ALU.subtract).then_inc(*did(f"{k}.sub"))

        def softmax_sum_vector(v, k, s, st, p_t, before=()):
            s3 = HB(s)
            v.wait_ge(*after(f"{k}.exp"))
            v.wait_ge(*last())
            v.tensor_reduce(st[:, CB:2 * CB], s3, AX_X, ALU.add).then_inc(*did(f"{k}.sum"))
            v.wait_ge(*last())
            v.reciprocal(st[:, 2 * CB:3 * CB], st[:, CB:2 * CB]).then_inc(*did(f"{k}.rec"))
            v.wait_ge(*last())
            v.tensor_tensor(s3, s3, st[:, 2 * CB:3 * CB].unsqueeze(2).to_broadcast([P, CB, T]), ALU.mult).then_inc(*did(f"{k}.norm"))
            for step in before:
                v.wait_ge(*after(step))
            v.wait_ge(*last())
            v.transpose(p_t, s).then_inc(*did(f"{k}.turned"))

        def exp_scalar(a, k, s, scale):
            for hh in range(2):
                a.wait_ge(*after(f"{k}.{hh}.sub"))
                a.wait_ge(*last())
                a.activation(s[hh], s[hh], ACT.Exp, scale=scale).then_inc(*did(f"{k}.{hh}.exp"))

        def rows_tensor(pe, k, rep, wv, needs):
            for g in range(4):
                ps = fill(pe, f"{k}.v{g}", f"{k}.vx{g}")
                for step in needs:
                    pe.wait_ge(*after(step))
                for b in range(4):
                    ins = pe.matmul(ps[:, b * D:(b + 1) * D], rep[:, (4 * g + b) * P:(4 * g + b + 1) * P], wv,
                                    start=True, stop=True)
                ins.then_inc(*did(f"{k}.v{g}"))

        def rows_vector(v, k, at, before=()):
            for g in range(4):
                v.wait_ge(*after(f"{k}.v{g}"))
                for step in before:
                    v.wait_ge(*after(step))
                v.wait_ge(*last())
                v.tensor_tensor(at.vx[:, 4 * g * D:4 * (g + 1) * D].rearrange("p (b f) -> p b f", f=D),
                                bank("vector", f"{k}.v{g}").rearrange("p (b f) -> p b f", f=D),
                                C("v16").unsqueeze(1).to_broadcast([P, 4, D]), ALU.mult).then_inc(*did(f"{k}.vx{g}"))

        def scores_tensor(pe, k, at):
            for hh in range(2):
                ps = fill(pe, f"{k}.s{hh}", f"{k}.in{hh}")
                pe.wait_ge(*after(f"{k}.q_read"))
                pe.wait_ge(*after(f"{k}.kx3"))
                for b in range(CB):
                    ins = pe.matmul(ps[:, b * T:(b + 1) * T], at.kx[64 * hh:64 * hh + 64, b * P:(b + 1) * P],
                                    at.q[64 * hh:64 * hh + 64, b * T:(b + 1) * T], start=True, stop=True)
                ins.then_inc(*did(f"{k}.s{hh}"))

        def scores_vector(v, k, at, scale, mask=None):
            for hh in range(2):
                kk = f"{k}.{hh}"
                v.wait_ge(*after(f"{k}.s{hh}"))
                v.wait_ge(*last())
                v.transpose(at.s[hh], bank("vector", f"{k}.s{hh}")).then_inc(*did(f"{k}.in{hh}"))
                if mask is not None:
                    v.wait_ge(*last())
                    v.scalar_tensor_tensor(out=HB(at.s[hh]), in0=HB(at.s[hh]), scalar=scale,
                                           in1=mask(hh).unsqueeze(1).to_broadcast([P, CB, T]),
                                           op0=ALU.mult, op1=ALU.add).then_inc(*did(f"{kk}.mask"))
                softmax_max_vector(v, kk, at.s[hh], at.st[hh])

        def probs_vector(v, k, at, before=()):
            for hh in range(2):
                softmax_sum_vector(v, f"{k}.{hh}", at.s[hh], at.st[hh], at.p[hh], before)

        def heads_tensor(pe, k, at):
            ps = fill(pe, f"{k}.o", f"{k}.o_read")
            for hh in range(2):
                pe.wait_ge(*after(f"{k}.{hh}.turned"))
                pe.wait_ge(*after(f"{k}.vx3"))
                for b in range(CB):
                    ins = pe.matmul(ps[64 * hh:64 * hh + 64, b * T:(b + 1) * T],
                                    at.vx[:, b * D + 64 * hh:b * D + 64 * hh + 64],
                                    at.p[hh][:, b * T:(b + 1) * T], start=True, stop=True)
            ins.then_inc(*did(f"{k}.o"))

        def rep_vector(v, k, at, src):
            for q in range(4):
                v.wait_ge(*last())
                v.tensor_copy(at.rep4[:, :, q, :], HB(src)).then_inc(*did(f"{k}.rep{q}"))

        def qk_scalar(a, k, at, bias=None, k_bias=None, needs=(), before=()):
            a.wait_ge(*after(f"{k}.q"))
            for step in before:
                a.wait_ge(*after(step))
            a.wait_ge(*last())
            if bias is None:
                a.activation(at.q, bank("scalar", f"{k}.q"), ACT.Copy).then_inc(*did(f"{k}.q_read"))
            else:
                a.activation(at.q, bank("scalar", f"{k}.q"), ACT.Identity, bias=bias).then_inc(*did(f"{k}.q_read"))
            for q in range(4):
                a.wait_ge(*after(f"{k}.k"))
                for step in needs:
                    a.wait_ge(*after(step))
                a.wait_ge(*last())
                if bias is None:
                    a.activation(at.kx4[:, :, q, :], HB(bank("scalar", f"{k}.k")), ACT.Copy,
                                 scale=C("head", q, q + 1)).then_inc(*did(f"{k}.kx{q}"))
                else:
                    a.activation(at.kx4[:, :, q, :], HB(bank("scalar", f"{k}.k")), ACT.Identity,
                                 scale=C("head", q, q + 1), bias=k_bias[:, q:q + 1]).then_inc(*did(f"{k}.kx{q}"))

        def of_pair(buf, i, c):
            return buf[:, bass.ts(i, 2 * CH)][:, c * CH:(c + 1) * CH]

        ar = new_arena()
        qu, qc, kc = ar.take(4 * CH), ar.take(4 * CH), ar.take(4 * CH)
        kux, vux = ar.take(8 * CH), ar.take(8 * CH)

        qcx_ = ar.take(8 * CH)
        t1x = [at_kx, qcx_[:, 0:4 * CH]]
        sg = [at_q, at_vx[:, 0:CH]]
        sc = at_s
        pt = at_p
        su_s = [at_vx[:, CH:2 * CH], at_vx[:, 2 * CH:3 * CH]]
        xr2 = at_rep[:, 0:2 * CH]
        vcx = kux
        o_t = qu

        def l0_tensor(pe, i):
            for name in ("q_u", "k_u", "q_c", "k_c", "v_u"):
                for f in range(4):
                    mm(pe, f"{name}{f}", f"{name}{f}.{'plain' if name == 'q_c' else 'read'}", [],
                       [(W(name, f * P, (f + 1) * P), xa[:, bass.ts(i, CH)])])

            def pairs(key, hh, reader, lhs, rhs, names):
                ps = fill(pe, f"{key}{hh}", f"{reader}{hh}")
                for f in (2 * hh, 2 * hh + 1):
                    for name, end in names:
                        pe.wait_ge(*after(f"{name}{f}.{end}"))
                    for b in range(CB):
                        ins = pe.matmul(ps[64 * (f % 2):64 * (f % 2) + 64, b * T:(b + 1) * T],
                                        lhs[:, f * 2 * CH + b * 64:f * 2 * CH + b * 64 + 64],
                                        rhs[:, f * CH + b * T:f * CH + (b + 1) * T], start=True, stop=True)
                ins.then_inc(*did(f"{key}{hh}"))
            for hh in range(2):
                pairs("lu_", hh, "sig_", kux, qu, [("k_u", "read"), ("q_u", "read")])
            for hh in range(2):
                pairs("sc_", hh, "masked_", qcx_, kc, [("q_c", "read"), ("k_c", "read")])
            for hh in range(2):
                pairs("t1_", hh, "t1x_", vux, qc, [("v_u", "read"), ("q_c", "plain")])
            wv = W("v_c").rearrange("p (u w f) -> p w u f", u=2, w=2)
            for hh in range(2):
                ps = fill(pe, f"su_{hh}", f"silu_{hh}")
                pe.wait_ge(*after(f"t1x_{hh}"))
                pe.wait_ge(*after(f"sigm_{hh}"))
                for b in range(CB):
                    ins = pe.matmul(ps[:, b * T:(b + 1) * T], t1x[hh][:, b * P:(b + 1) * P], sg[hh][:, b * T:(b + 1) * T],
                                    start=True, stop=True)
                ins.then_inc(*did(f"su_{hh}"))
                for g in range(hh * CB // 4, (hh + 1) * CB // 4):
                    ps = fill(pe, f"v{g}", f"vx{g}")
                    pe.wait_ge(*after("x.rep1"))
                    for b in range(2):
                        for w in range(2):
                            ins = pe.matmul(ps[64 * w:64 * w + 64, b * 256:(b + 1) * 256].rearrange("p (u f) -> p u f", u=2),
                                            xr2[:, (2 * g + b) * 64:(2 * g + b + 1) * 64], wv[:, w], start=True, stop=True)
                    ins.then_inc(*did(f"v{g}"))
            for f in range(4):
                hh, w = f // 2, f % 2
                ps = fill(pe, f"o{f}", f"o{f}.read")
                pe.wait_ge(*after(f"a.{hh}.turned"))
                pe.wait_ge(*after(f"vx{CB // 2 - 1}"))
                for b in range(CB):
                    ins = pe.matmul(ps[:, b * T:(b + 1) * T], vcx[64 * w:64 * w + 64, b * 256 + hh * D:b * 256 + (hh + 1) * D],
                                    pt[hh][64 * w:64 * w + 64, b * T:(b + 1) * T], start=True, stop=True)
                ins.then_inc(*did(f"o{f}"))
            mm(pe, "proj", "h_new", [f"o{f}.read" for f in range(4)],
               [(W("l0_out", f * P, (f + 1) * P), o_t[:, f * CH:(f + 1) * CH]) for f in range(4)])

        def expand(eng, who, name, dst, f):
            d4 = dst[:, f * 2 * CH:(f + 1) * 2 * CH].rearrange("p (b q t) -> p b q t", q=2, t=T)
            for q in range(2):
                key = f"{name}{f}.x{q}" if q == 0 else f"{name}{f}.read"
                eng.wait_ge(*after(f"{name}{f}"))
                eng.wait_ge(*last())
                if who == "scalar":
                    eng.activation(d4[:, :, q, :], HB(bank(who, f"{name}{f}")), ACT.Copy, scale=C("half", q, q + 1)).then_inc(*did(key))
                else:
                    eng.tensor_scalar(d4[:, :, q, :], HB(bank(who, f"{name}{f}")), C("half", q, q + 1), None, ALU.mult).then_inc(*did(key))

        def l0_vector(v, i):
            for f in range(4):
                expand(v, "vector", "k_u", kux, f)
            for f in range(4):
                expand(v, "vector", "q_c", qcx_, f)
                v.wait_ge(*last())
                v.tensor_copy(qc[:, f * CH:(f + 1) * CH], bank("vector", f"q_c{f}")).then_inc(*did(f"q_c{f}.plain"))
            for hh in range(2):
                v.wait_ge(*after(f"sig_{hh}"))
                v.wait_ge(*last())
                v.tensor_tensor(HB(sg[hh]), HB(sg[hh]), C("sgm").unsqueeze(1).to_broadcast([P, CB, T]), ALU.mult).then_inc(*did(f"sigm_{hh}"))
            for hh in range(2):
                v.wait_ge(*after(f"sc_{hh}"))
                v.wait_ge(*last())
                v.scalar_tensor_tensor(out=HB(sc[hh]), in0=HB(bank("vector", f"sc_{hh}")), scalar=0.125,
                                       in1=C("causal").unsqueeze(1).to_broadcast([P, CB, T]),
                                       op0=ALU.mult, op1=ALU.add).then_inc(*did(f"masked_{hh}"))
            for hh in range(2):
                v.wait_ge(*after(f"t1_{hh}"))
                v.wait_ge(*last())
                v.tensor_tensor(t1x[hh].rearrange("p (b q t) -> p b q t", q=4, t=T),
                                HB(bank("vector", f"t1_{hh}")).unsqueeze(2).to_broadcast([P, CB, 4, T]),
                                C("t1m").rearrange("p (q t) -> p q t", t=T).unsqueeze(1).to_broadcast([P, CB, 4, T]),
                                ALU.mult).then_inc(*did(f"t1x_{hh}"))
            for hh in range(2):
                v.wait_ge(*after(f"susig_{hh}"))
                v.wait_ge(*last())
                v.tensor_tensor(su_s[hh], su_s[hh], bank("vector", f"su_{hh}"), ALU.mult).then_inc(*did(f"silu_{hh}"))
                v.wait_ge(*last())
                v.tensor_tensor(sc[hh], sc[hh], su_s[hh], ALU.subtract).then_inc(*did(f"final_{hh}"))
                softmax_max_vector(v, f"a.{hh}", sc[hh], at_st[hh])
                for g in range(hh * CB // 4, (hh + 1) * CB // 4):
                    v.wait_ge(*after(f"v{g}"))
                    v.wait_ge(*after("lu_1"))
                    v.wait_ge(*last())
                    v.tensor_tensor(vcx[:, g * 512:(g + 1) * 512].rearrange("p (b f) -> p b f", f=D),
                                    bank("vector", f"v{g}").rearrange("p (b f) -> p b f", f=D),
                                    C("v64").unsqueeze(1).to_broadcast([P, 4, D]), ALU.mult).then_inc(*did(f"vx{g}"))
            for hh in range(2):
                softmax_sum_vector(v, f"a.{hh}", sc[hh], at_st[hh], pt[hh])
            residual_vector(v, i, "proj")

        def residual_vector(v, i, key):
            v.wait_ge(*after(key))
            v.wait_ge(*last())
            v.tensor_tensor(h[:, bass.ts(i, CH)], h[:, bass.ts(i, CH)], bank("vector", key), ALU.add).then_inc(*did("h_new"))

        def l0_scalar(a, i):
            for q in range(2):
                a.wait_ge(*last())
                a.activation(xr2.rearrange("p (b q t) -> p b q t", q=2, t=T)[:, :, q, :], HB(xa[:, bass.ts(i, CH)]), ACT.Copy).then_inc(*did(f"x.rep{q}"))
            for name, dst in (("q_u", qu), ("k_c", kc), ("v_u", vux)):
                for f in range(4):
                    if dst is vux:
                        expand(a, "scalar", name, dst, f)
                    else:
                        a.wait_ge(*after(f"{name}{f}"))
                        a.wait_ge(*last())
                        a.activation(dst[:, f * CH:(f + 1) * CH], bank("scalar", f"{name}{f}"), ACT.Copy).then_inc(*did(f"{name}{f}.read"))
            for hh in range(2):
                a.wait_ge(*after(f"lu_{hh}"))
                a.wait_ge(*last())
                a.activation(sg[hh], bank("scalar", f"lu_{hh}"), ACT.Sigmoid, scale=0.125).then_inc(*did(f"sig_{hh}"))
            for hh in range(2):
                a.wait_ge(*after(f"su_{hh}"))
                a.wait_ge(*last())
                a.activation(su_s[hh], bank("scalar", f"su_{hh}"), ACT.Sigmoid).then_inc(*did(f"susig_{hh}"))
            exp_scalar(a, "a", sc, 1.0)
            for f in range(4):
                a.wait_ge(*after(f"o{f}"))
                a.wait_ge(*after("lu_1"))
                a.wait_ge(*last())
                a.activation(o_t[:, f * CH:(f + 1) * CH], bank("scalar", f"o{f}"), ACT.Copy).then_inc(*did(f"o{f}.read"))

        ar = new_arena()
        gx = {g: ar.take(T * 2 * B) for g in ("z", "r", "c")}
        hs = ar.take(T * 2 * B)
        gb = keep.take(6)
        GRU_IN = (("z", "g_uz", "buz", "bwz"), ("r", "g_ur", "bur", "bwr"), ("c", "g_u", "bu", "bw"))

        def gru_input_tensor(pe, i):
            for g, w, _, _ in GRU_IN:
                for m in range(2):
                    mm(pe, f"{g}{m}", f"{g}{m}.read", [], [(W(w, m * P, (m + 1) * P), xa[:, bass.ts(i, CH)])])

        def gru_input_vector(v, i):
            for n, (g, _, b1, b2) in enumerate(GRU_IN):
                v.wait_ge(*last())
                v.tensor_tensor(gb[:, 2 * n:2 * n + 2], W(b1), W(b2), ALU.add).then_inc(*did(f"bias{g}"))
            for n, (g, _, _, _) in enumerate(GRU_IN):
                m = 0
                v.wait_ge(*after(f"{g}{m}"))
                v.wait_ge(*last())
                v.tensor_scalar(gx_chunk(g, m, i), HB(bank("vector", f"{g}{m}")), gb[:, 2 * n + m:2 * n + m + 1], None,
                                ALU.add).then_inc(*did(f"{g}{m}.read"))

        def gx_chunk(g, m, i):
            v4 = gx[g].rearrange("p (t m b) -> p m b t", m=2, b=B)
            return v4[:, m, bass.ts(i, CB), :]

        def gru_input_scalar(a, i):
            for n, (g, _, _, _) in enumerate(GRU_IN):
                m = 1
                a.wait_ge(*after(f"{g}{m}"))
                a.wait_ge(*after(f"bias{g}"))
                a.wait_ge(*last())
                a.activation(gx_chunk(g, m, i), HB(bank("scalar", f"{g}{m}")), ACT.Identity,
                             bias=gb[:, 2 * n + m:2 * n + m + 1]).then_inc(*did(f"{g}{m}.read"))

        gru = Places(at_kx, 4 * CH)
        HW = 2 * B
        gz, gr, gc, gt, gw = [[gru.take(HW), gru.take(HW)] for _ in range(5)]
        gh = [gru.take(HW), gru.take(HW)]

        def of_step(buf, t, u):
            return buf[:, bass.ts(t, GRU_U * HW)][:, u * HW:(u + 1) * HW]

        def gru_tensor(pe, t):
            banks = {}

            def x_terms(u):
                for g in ("r", "z", "c"):
                    banks[g, u] = fill(pe, f"{g}{u}", f"{g}{u}.sig")
                    pe.matmul(banks[g, u][:, 0:HW], C("ident"), of_step(gx[g], t, u), start=True, stop=False)

            def h_terms(g, u, w, src):
                for m in range(2):
                    for k in range(2):
                        ins = pe.matmul(banks[g, u][:, m * B:(m + 1) * B], W(w, k * 256 + m * P, k * 256 + (m + 1) * P),
                                        src[:, k * B:(k + 1) * B], start=False, stop=m == 1 and k == 1)
                ins.then_inc(*did(f"{g}{u}"))
            x_terms(0)
            for u in range(GRU_U):
                if u:
                    pe.wait_ge(*after(f"state{u - 1}"))
                h_terms("r", u, "g_wr", gh[u % 2])
                h_terms("z", u, "g_wz", gh[u % 2])
                pe.wait_ge(*after(f"hr{u}"))
                h_terms("c", u, "g_w", gt[u % 2])
                if u + 1 < GRU_U:
                    x_terms(u + 1)

        def gru_scalar(a, t):
            for u in range(GRU_U):
                for g, dst, scale in (("r", gr, 1.0), ("z", gz, 1.0), ("c", gc, 2.0)):
                    if u >= 2 and g == "r":
                        a.wait_ge(*after(f"state{u - 2}"))
                    a.wait_ge(*after(f"{g}{u}"))
                    a.wait_ge(*last())
                    a.activation(dst[u % 2], bank("scalar", f"{g}{u}")[:, 0:HW], ACT.Sigmoid, scale=scale).then_inc(*did(f"{g}{u}.sig"))

        def gru_vector(v, t):
            for u in range(GRU_U):
                p, now, then = u % 2, gh[u % 2], gh[(u + 1) % 2]
                v.wait_ge(*after(f"r{u}.sig"))
                v.wait_ge(*last())
                v.tensor_tensor(gt[p], now, gr[p], ALU.mult).then_inc(*did(f"hr{u}"))
                v.wait_ge(*after(f"z{u}.sig"))
                v.wait_ge(*last())
                v.tensor_tensor(gw[p], now, gz[p], ALU.mult).then_inc(*did(f"zh{u}"))
                v.wait_ge(*last())
                v.tensor_scalar(gz[p], gz[p], -1.0, 1.0, ALU.mult, ALU.add).then_inc(*did(f"omz{u}"))
                v.wait_ge(*last())
                v.tensor_tensor(gw[p], gw[p], gz[p], ALU.subtract).then_inc(*did(f"base{u}"))
                v.wait_ge(*after(f"c{u}.sig"))
                v.wait_ge(*last())
                v.scalar_tensor_tensor(out=gc[p], in0=gc[p], scalar=2.0, in1=gz[p], op0=ALU.mult, op1=ALU.mult).then_inc(*did(f"zc{u}"))
                if u:
                    v.wait_ge(*after(f"z{u - 1}"))
                v.wait_ge(*last())
                v.tensor_tensor(then, gc[p], gw[p], ALU.add).then_inc(*did(f"state{u}"))
                v.wait_ge(*last())
                v.tensor_copy(of_step(hs, t, u), then).then_inc(*did(f"kept{u}"))

        def gru_output_tensor(pe, i):
            mm(pe, "out", "sig", ["state0", "state1"], [(W("g_o", m * D, (m + 1) * D), hsc[:, m * CH:(m + 1) * CH]) for m in range(2)])

        hsc, gout = at_rep, at_q

        def gru_output_scalar(a, i):
            hv = hs[:, 0:T * HW].rearrange("p (t m b) -> p m b t", m=2, b=B)
            for m in range(2):
                a.wait_ge(*last())
                a.activation(HB(hsc[:, m * CH:(m + 1) * CH]), hv[:, m, bass.ts(i, CB), :], ACT.Copy).then_inc(*did(f"state{m}"))
            a.wait_ge(*after("out"))
            a.wait_ge(*last())
            a.activation(gout, bank("scalar", "out"), ACT.Sigmoid, bias=W("g_bo")).then_inc(*did("sig"))

        def gru_output_vector(v, i):
            v.wait_ge(*after("sig"))
            v.wait_ge(*last())
            v.tensor_tensor(h[:, bass.ts(i, CH)], h[:, bass.ts(i, CH)], gout, ALU.add).then_inc(*did("h_new"))

        ar = new_arena()
        at1 = Attention(ar)
        pair = [at0, at1]
        l1_o, l1_y, l1_hb = [ar.take(CH) for _ in range(3)], [ar.take(CH) for _ in range(3)], ar.take(CH)
        l1_kb = keep.take(12)
        bands = ["band5", "band10", None]

        def l1_tensor(pe, i):
            x_i = xa[:, bass.ts(i, CH)]

            def qk(s):
                mm(pe, f"s{s}.q", f"s{s}.q_read", [], [(W(f"l1_qkv{s}", 0, D), x_i)])
                mm(pe, f"s{s}.k", f"s{s}.kx3", [], [(W(f"l1_qkv{s}", D, 2 * D), x_i)])

            def rows(s):
                rows_tensor(pe, f"s{s}", at_rep, W(f"l1_qkv{s}", 2 * D, 3 * D), ["x.rep3"])

            def project(s):
                mm(pe, f"s{s}.y", f"s{s}.y_read", [f"s{s}.o_read"], [(W(f"l1_o{s}"), l1_o[s])])
            qk(0)
            qk(1)
            rows(0)
            scores_tensor(pe, "s0", at0)
            rows(1)
            qk(2)
            scores_tensor(pe, "s1", at1)
            heads_tensor(pe, "s0", at0)
            rows(2)
            scores_tensor(pe, "s2", at0)
            project(0)
            heads_tensor(pe, "s1", at1)
            project(1)
            heads_tensor(pe, "s2", at0)
            project(2)
            mm(pe, "f", "h_new", ["s2.y_read"], [(W("l1_f", s * D, (s + 1) * D), l1_y[s]) for s in range(3)])

        def l1_vector(v, i):
            def scores(s):
                scores_vector(v, f"s{s}", pair[s % 2], 0.25, None if bands[s] is None else (lambda hh: C(bands[s])))
            rep_vector(v, "x", at0, xa[:, bass.ts(i, CH)])
            for s in range(3):
                v.wait_ge(*last())
                v.tensor_scalar(l1_kb[:, 4 * s:4 * s + 4], C("head"), W(f"l1_bqkv{s}", 1, 2), None, ALU.mult).then_inc(*did(f"kb{s}"))
            v.wait_ge(*last())
            v.tensor_scalar(l1_hb, h[:, bass.ts(i, CH)], W("l1_bf"), None, ALU.add).then_inc(*did("h_bias"))
            rows_vector(v, "s0", at0)
            scores(0)
            rows_vector(v, "s1", at1)
            probs_vector(v, "s0", at0)
            scores(1)
            rows_vector(v, "s2", at0, ["s0.o"])
            probs_vector(v, "s1", at1)
            scores(2)
            probs_vector(v, "s2", at0)
            v.wait_ge(*after("f"))
            v.wait_ge(*last())
            v.tensor_tensor(h[:, bass.ts(i, CH)], l1_hb, bank("vector", "f"), ALU.add).then_inc(*did("h_new"))

        def l1_scalar(a, i):
            def qk(s, before=()):
                qk_scalar(a, f"s{s}", pair[s % 2], W(f"l1_bqkv{s}", 0, 1), l1_kb[:, 4 * s:4 * s + 4], [f"kb{s}"], before)

            def exps(s):
                exp_scalar(a, f"s{s}", pair[s % 2].s, 1.0 if bands[s] else 0.25)

            def heads(s):
                a.wait_ge(*after(f"s{s}.o"))
                a.wait_ge(*last())
                a.activation(l1_o[s], bank("scalar", f"s{s}.o"), ACT.Identity, bias=W(f"l1_bqkv{s}", 2, 3)).then_inc(*did(f"s{s}.o_read"))

            def projected(s):
                a.wait_ge(*after(f"s{s}.y"))
                a.wait_ge(*last())
                a.activation(l1_y[s], bank("scalar", f"s{s}.y"), ACT.Identity, bias=W(f"l1_bo{s}")).then_inc(*did(f"s{s}.y_read"))
            qk(0)
            qk(1)
            exps(0)
            qk(2, ["s0.s1"])
            exps(1)
            heads(0)
            exps(2)
            projected(0)
            heads(1)
            projected(1)
            heads(2)
            projected(2)

        ar = new_arena()
        en = ar.take(CH)
        hid = [[ar.take(CH) for _ in range(4)] for _ in range(2)]
        mix = ar.take(CH)
        lg, top, topi, topf = ar.take(32), ar.take(32), ar.take(32).bitcast(U32), ar.take(32)
        g2 = ar.take(12)
        oh, gate = ar.take(32), ar.take(32)
        gate_t, h_sum = ar.take(CH), ar.take(CH)
        T8 = lambda ap: ap.rearrange("p (t e) -> p t e", t=NT)

        def experts_tensor(pe, i):
            ps = fill(pe, "logits", "logits_read")
            pe.wait_ge(*after("en"))
            for t in range(NT):
                pe.matmul(ps[:, 8 * t:8 * t + 8], en[:, t * P:(t + 1) * P], W("moe_r"), start=True, stop=False)
                ins = pe.matmul(ps[:, 8 * t:8 * t + 8], C("row0"), W("moe_br"), start=False, stop=True)
            ins.then_inc(*did("logits"))

            def up(e):
                for f in range(4):
                    mm(pe, f"u{e}.{f}", f"g{e}.{f}", [], [(W(f"moe_1_{e}", f * P, (f + 1) * P), en)])

            def down(e):
                ps = fill(pe, f"y{e}", f"mix{e}.3")
                for t in range(NT):
                    for f in range(4):
                        pe.wait_ge(*after(f"g{e}.{f}"))
                        ins = pe.matmul(ps[:, t * P:(t + 1) * P], hid[e % 2][f][:, t * P:(t + 1) * P],
                                        W(f"moe_2_{e}", f * D, (f + 1) * D), start=f == 0, stop=f == 3)
                ins.then_inc(*did(f"y{e}"))
            up(0)
            for e in range(E1):
                if e + 1 < E1:
                    up(e + 1)
                if e == 1:
                    ps = fill(pe, "gate_t", "gate_t_read")
                    pe.wait_ge(*after("gate"))
                    for t in range(NT):
                        ins = pe.transpose(ps[0:8, t * P:(t + 1) * P], gate[:, 8 * t:8 * t + 8], C("ident"))
                    ins.then_inc(*did("gate_t"))
                down(e)
            ps = fill(pe, "mixed", "h_new")
            pe.wait_ge(*after(f"mix{E1 - 1}.3"))
            pe.wait_ge(*after("gate_t_read"))
            pe.matmul(ps, W("moe_b2"), gate_t, start=True, stop=False)
            for t in range(NT):
                ins = pe.matmul(ps[:, t * P:(t + 1) * P], mix[:, t * P:(t + 1) * P], C("ident"), start=False, stop=t == NT - 1)
            ins.then_inc(*did("mixed"))

        def experts_vector(v, i):
            v.wait_ge(*last())
            v.tensor_copy(en, ln2[:, bass.ts(i, CH)]).then_inc(*did("en"))
            v.wait_ge(*last())
            v.tensor_tensor(h_sum, h[:, bass.ts(i, CH)], xa[:, bass.ts(i, CH)], ALU.add).then_inc(*did("h_sum"))
            v.wait_ge(*after("logits"))
            v.wait_ge(*last())
            v.tensor_copy(lg, bank("vector", "logits")[:, 0:32]).then_inc(*did("logits_read"))
            for t in range(NT):
                v.wait_ge(*last())
                v.max(top[:, 8 * t:8 * t + 8], lg[:, 8 * t:8 * t + 8]).then_inc(*did(f"top{t}"))
                v.wait_ge(*last())
                v.max_index(topi[:, 8 * t:8 * t + 8], top[:, 8 * t:8 * t + 8], lg[:, 8 * t:8 * t + 8]).then_inc(*did(f"topi{t}"))
            v.wait_ge(*last())
            v.tensor_copy(topf, topi).then_inc(*did("topf"))
            v.wait_ge(*last())
            v.tensor_tensor(g2[:, 0:4], T8(top)[:, :, 1], T8(top)[:, :, 0], ALU.subtract).then_inc(*did("gap"))
            v.wait_ge(*after("gap_exp"))
            v.wait_ge(*last())
            v.tensor_scalar(g2[:, 8:12], g2[:, 4:8], 1.0, None, ALU.add).then_inc(*did("gate_sum"))
            v.wait_ge(*last())
            v.reciprocal(g2[:, 0:4], g2[:, 8:12]).then_inc(*did("gate_1"))
            v.wait_ge(*last())
            v.tensor_tensor(g2[:, 4:8], g2[:, 4:8], g2[:, 0:4], ALU.mult).then_inc(*did("gate_2"))
            for n, dst in ((0, gate), (1, oh)):
                v.wait_ge(*last())
                v.tensor_tensor(T8(dst), C("iota8").unsqueeze(1).to_broadcast([P, NT, 8]),
                                T8(topf)[:, :, n:n + 1].to_broadcast([P, NT, 8]), ALU.is_equal).then_inc(*did(f"hot{n}"))
                v.wait_ge(*last())
                v.tensor_tensor(T8(dst), T8(dst), g2[:, 4 * n:4 * n + 4].unsqueeze(2).to_broadcast([P, NT, 8]),
                                ALU.mult).then_inc(*did(f"weighted{n}"))
            v.wait_ge(*last())
            v.tensor_tensor(gate, gate, oh, ALU.add).then_inc(*did("gate"))
            v.wait_ge(*last())
            v.memset(gate_t, 0.0).then_inc(*did("gate_t_zero"))
            for e in range(E1):
                for t in range(NT):
                    v.wait_ge(*after(f"y{e}"))
                    v.wait_ge(*last())
                    cols = slice(t * P, (t + 1) * P)
                    y = bank("vector", f"y{e}")[:, cols]
                    if e == 0:
                        v.tensor_scalar(mix[:, cols], y, gate[:, 8 * t + e:8 * t + e + 1], None, ALU.mult).then_inc(*did(f"mix{e}.{t}"))
                    else:
                        v.scalar_tensor_tensor(out=mix[:, cols], in0=y, scalar=gate[:, 8 * t + e:8 * t + e + 1], in1=mix[:, cols],
                                               op0=ALU.mult, op1=ALU.add).then_inc(*did(f"mix{e}.{t}"))
                if e == 1:
                    v.wait_ge(*after("gate_t"))
                    v.wait_ge(*last())
                    v.tensor_copy(gate_t[0:8, :], bank("vector", "gate_t")[0:8, :]).then_inc(*did("gate_t_read"))
            v.wait_ge(*after("mixed"))
            v.wait_ge(*last())
            v.tensor_tensor(h[:, bass.ts(i, CH)], h_sum, bank("vector", "mixed"), ALU.add).then_inc(*did("h_new"))

        def experts_scalar(a, i):
            a.wait_ge(*after("gap"))
            a.wait_ge(*last())
            a.activation(g2[:, 4:8], g2[:, 0:4], ACT.Exp).then_inc(*did("gap_exp"))
            for e in range(E1):
                for f in range(4):
                    a.wait_ge(*after(f"u{e}.{f}"))
                    if e >= 2:
                        a.wait_ge(*after(f"y{e - 2}"))
                    a.wait_ge(*last())
                    a.activation(hid[e % 2][f], bank("scalar", f"u{e}.{f}"), ACT.Gelu,
                                 bias=W("moe_b1", 4 * e + f, 4 * e + f + 1)).then_inc(*did(f"g{e}.{f}"))

        ar = new_arena()
        ga, bz, hscan = ar.take(TOK), ar.take(TOK), ar.take(TOK)
        l2_bb = keep.take(1)
        gsig, scanned, with_in = ar.take(CH), ar.take(TOK), ar.take(TOK)
        pool_, pool_sum = keep.take(B), keep.take(B)

        def pos_major(ap, i):
            return ap.rearrange("p (t b) -> p b t", b=B)[:, bass.ts(i, CB), :]

        def l2_input_tensor(pe, i):
            for n, r in ((0, "bz"), (1, "g_sig")):
                mm(pe, f"in{n}", r, [], [(W("l2_in", n * D, (n + 1) * D), ln2[:, bass.ts(i, CH)])])

        def l2_input_vector(v, i):
            v.wait_ge(*last())
            v.tensor_tensor(l2_bb, W("l2_bin", 0, 1), W("l2_B"), ALU.mult).then_inc(*did("bias_b"))
            v.wait_ge(*after("in0"))
            v.wait_ge(*last())
            v.tensor_scalar(pos_major(bz, i), HB(bank("vector", "in0")), W("l2_B"), l2_bb, ALU.mult, ALU.add).then_inc(*did("bz"))
            v.wait_ge(*after("g_sig"))
            v.wait_ge(*last())
            v.tensor_scalar(pos_major(ga, i), HB(gsig), W("l2_A"), None, ALU.mult).then_inc(*did("ga"))

        def l2_input_scalar(a, i):
            a.wait_ge(*after("in1"))
            a.wait_ge(*last())
            a.activation(gsig, bank("scalar", "in1"), ACT.Sigmoid, bias=W("l2_bin", 1, 2)).then_inc(*did("g_sig"))

        def l2_scan_vector(v):
            v.wait_ge(*last())
            v.memset(ga.rearrange("p (t b) -> p t b", b=B)[:, :, 0:1], 0.0).then_inc(*did("starts"))
            v.wait_ge(*last())
            v.tensor_tensor_scan(hscan, ga, bz, 0.0, ALU.mult, ALU.add).then_inc(*did("scan"))

        def l2_output_tensor(pe):
            for c in range(NCH):
                mm(pe, f"out{c}", f"y{c}", [f"scanned{c}"], [(W("l2_out"), part(scanned, c))])
            norm_tensor(pe, with_in, "y")

        def l2_output_vector(v):
            for c in range(NCH):
                v.wait_ge(*last())
                v.tensor_scalar(part(with_in, c), part(ln2, c), W("l2_b_out"), None, ALU.add).then_inc(*did(f"x{c}"))
            for c in range(NCH):
                v.wait_ge(*after(f"out{c}"))
                v.wait_ge(*last())
                v.tensor_tensor(part(with_in, c), part(with_in, c), bank("vector", f"out{c}"), ALU.add).then_inc(*did(f"y{c}"))
            for c in range(NCH):
                centre_vector(v, with_in, c)
            for c in range(NCH):
                v.wait_ge(*after(f"var{c}"))
                v.wait_ge(*last())
                v.tensor_scalar(part(with_in, c), bank("vector", f"var{c}"), 2.0 ** 128 * WIDE ** 2 / P, None,
                                ALU.is_lt).then_inc(*did(f"fits{c}"))
            for c in range(NCH):
                v.wait_ge(*after(f"log{c}"))
                v.wait_ge(*last())
                v.reciprocal(part(squares, c), part(squares, c)).then_inc(*did(f"rstd{c}"))
                v.wait_ge(*last())
                v.tensor_tensor(part(squares, c), part(squares, c), part(with_in, c), ALU.mult).then_inc(*did(f"zeroed{c}"))
                v.wait_ge(*last())
                v.scalar_tensor_tensor(out=part(centred, c), in0=part(centred, c), scalar=WIDE, in1=part(squares, c), op0=ALU.mult,
                                       op1=ALU.mult).then_inc(*did(f"n{c}"))
                v.wait_ge(*last())
                v.tensor_scalar(part(centred, c), part(centred, c), W("l2_gamma"), W("l2_beta"), ALU.mult, ALU.add).then_inc(*did(f"scaled{c}"))
                v.wait_ge(*last())
                v.tensor_tensor(part(h, c), part(h, c), part(centred, c), ALU.add).then_inc(*did(f"h_new{c}"))

        def l2_output_scalar(a):
            for c in range(NCH):
                a.wait_ge(*last())
                a.activation(HB(part(scanned, c)), hscan.rearrange("p (t b) -> p b t", b=B)[:, c * CB:(c + 1) * CB, :],
                             ACT.Copy).then_inc(*did(f"scanned{c}"))
            norm_scalar(a, wide=True)

        r_h, r_sel = keep.take(B), keep.take(8)
        r_t = keep.take(2 * B)
        r_b = keep.take(8 * B)
        r_w = keep.take(64)

        def route_tensor(pe):
            mm(pe, "h", "gelu", [], [(W("rt_1"), pool_)])
            ps = fill(pe, "logits", "logits_read")
            pe.wait_ge(*after("gelu"))
            pe.matmul(ps[0:B, 0:8], r_h, W("rt_2"), start=True, stop=False)
            pe.matmul(ps[0:B, 0:8], C("row0", 0, B), W("rt_b2"), start=False, stop=True).then_inc(*did("logits"))
            ps = fill(pe, "turned", "turned_read")
            pe.wait_ge(*after("sel"))
            for n in range(2):
                ins = pe.transpose(ps[0:4, n * B:(n + 1) * B], r_sel[0:B, 4 * n:4 * n + 4], C("ident")[0:B, 0:B])
            ins.then_inc(*did("turned"))
            ps = fill(pe, "spread", "spread_read")
            pe.wait_ge(*after("turned_read"))
            for n in range(2):
                for e in range(E2):
                    ins = pe.matmul(ps[:, (4 * n + e) * B:(4 * n + e + 1) * B], C("pick", e * P, (e + 1) * P),
                                    r_t[:, n * B:(n + 1) * B], start=True, stop=True)
            ins.then_inc(*did("spread"))

        def route_scalar(a):
            a.wait_ge(*after("h"))
            a.wait_ge(*last())
            a.activation(r_h, bank("scalar", "h")[:, 0:B], ACT.Gelu, bias=W("router_b1")).then_inc(*did("gelu"))

        def route_vector(v):
            l3 = r_w[0:B, 0:8].rearrange("p (n e) -> p n e", n=2)
            s3 = r_sel[0:B, :].rearrange("p (n e) -> p n e", n=2)
            c3 = r_w[0:B, 16:24].rearrange("p (n e) -> p n e", n=2)
            v.wait_ge(*after("logits"))
            v.wait_ge(*last())
            v.tensor_copy(r_w[0:B, 0:8], bank("vector", "logits")[0:B, 0:8]).then_inc(*did("logits_read"))
            v.wait_ge(*last())
            v.tensor_reduce(r_w[0:B, 8:10], l3, AX_X, ALU.max).then_inc(*did("max"))
            v.wait_ge(*last())
            v.tensor_tensor(s3, l3, r_w[0:B, 8:10].unsqueeze(2).to_broadcast([B, 2, 4]), ALU.is_ge).then_inc(*did("is_max"))
            v.wait_ge(*last())
            v.tensor_copy(c3, s3).then_inc(*did("count0"))
            for e in range(1, 4):
                v.wait_ge(*last())
                v.tensor_tensor(c3[:, :, e:e + 1], c3[:, :, e:e + 1], c3[:, :, e - 1:e], ALU.add).then_inc(*did(f"count{e}"))
            v.wait_ge(*last())
            v.tensor_scalar(c3, c3, 1.0, None, ALU.is_equal).then_inc(*did("first"))
            v.wait_ge(*last())
            v.tensor_tensor(s3, s3, c3, ALU.mult).then_inc(*did("sel"))
            v.wait_ge(*last())
            v.memset(r_t, 0.0).then_inc(*did("zeroed"))
            v.wait_ge(*after("turned"))
            v.wait_ge(*last())
            v.tensor_copy(r_t[0:4, :], bank("vector", "turned")[0:4, 0:2 * B]).then_inc(*did("turned_read"))
            v.wait_ge(*after("spread"))
            v.wait_ge(*last())
            v.tensor_copy(r_b, bank("vector", "spread")[:, 0:8 * B]).then_inc(*did("spread_read"))

        def pool_vector(v):
            norm_h_ln2[1](v)
            v.wait_ge(*last())
            v.tensor_reduce(pool_sum, HB(ln2), AX_X, ALU.add).then_inc(*did("sum"))
            v.wait_ge(*last())
            v.tensor_scalar(pool_, pool_sum, 1.0 / T, None, ALU.mult).then_inc(*did("pooled"))

        ar = new_arena()
        at1 = Attention(ar)
        pair = [at0, at1]
        masked_x = [ar.take(4 * CH), ar.take(4 * CH)]
        chosen = [ar.take(CH), ar.take(CH)]
        heads_out = [ar.take(CH), ar.take(CH)]
        att_in = [ar.take(CH), ar.take(CH)]
        cr_kb = keep.take(4)
        outs = Places(wt, second_at)
        outs.at = experts_at + vec_at - third_at
        spatial, temporal = outs.take(TOK), outs.take(TOK)

        def routed(n, wq, wk, wv, bias, wo, bo, gain, gain_bias, mask):
            def masks(i, c):
                seqs = r_b.rearrange("p (e b) -> p e b", b=B)[:, 4 * n:4 * n + 4, bass.ts(i, 2 * CB)]
                return [seqs[:, e, c * CB:(c + 1) * CB].unsqueeze(2).to_broadcast([P, CB, T]) for e in range(E2)]

            def tensor(pe, i):
                def inputs(c):
                    for key, w, b, reader in (("q", wq, bias[0], "q_read"), ("k", wk, bias[1], "kx3"), ("v", wv, bias[2], "rep3")):
                        mm(pe, f"a{c}.{key}", f"a{c}.{reader}", [f"ex{c}.3", f"chosen{c}"],
                           [(w(e), part(masked_x[c], e)) for e in range(4)] + [(b, chosen[c])])

                def project(c):
                    mm(pe, f"y{c}", f"stored{c}", [f"exo{c}.3"], [(wo(e), part(masked_x[c], e)) for e in range(4)] + [(bo, chosen[c])])
                inputs(0)
                scores_tensor(pe, "a0", at0)
                rows_tensor(pe, "a0", at0.rep, C("ident"), ["a0.rep3"])
                inputs(1)
                heads_tensor(pe, "a0", at0)
                scores_tensor(pe, "a1", at1)
                rows_tensor(pe, "a1", at1.rep, C("ident"), ["a1.rep3"])
                project(0)
                heads_tensor(pe, "a1", at1)
                project(1)

            def vector(v, i):
                def inputs(c):
                    v.wait_ge(*last())
                    v.memset(chosen[c], 0.0).then_inc(*did(f"zero{c}"))
                    v.wait_ge(*last())
                    v.tensor_copy(HB(chosen[c][0:4, :]), r_t[0:4, n * B:(n + 1) * B][:, bass.ts(i, 2 * CB)][:, c * CB:(c + 1) * CB]
                                  .unsqueeze(2).to_broadcast([4, CB, T])).then_inc(*did(f"chosen{c}"))
                    v.wait_ge(*last())
                    v.tensor_scalar(att_in[c], of_pair(xa, i, c), gain, gain_bias, ALU.mult, ALU.add).then_inc(*did(f"gained{c}"))
                    for e, seqs in enumerate(masks(i, c)):
                        v.wait_ge(*last())
                        v.tensor_tensor(HB(part(masked_x[c], e)), HB(att_in[c]), seqs, ALU.mult).then_inc(*did(f"ex{c}.{e}"))

                def outputs(c):
                    for e, seqs in enumerate(masks(i, c)):
                        v.wait_ge(*after(f"a{c}.o_read"))
                        v.wait_ge(*after(f"a{c}.v"))
                        v.wait_ge(*last())
                        v.tensor_tensor(HB(part(masked_x[c], e)), HB(heads_out[c]), seqs, ALU.mult).then_inc(*did(f"exo{c}.{e}"))

                def store(c):
                    v.wait_ge(*after(f"y{c}"))
                    v.wait_ge(*last())
                    if n == 0:
                        v.tensor_copy(of_pair(spatial, i, c), bank("vector", f"y{c}")).then_inc(*did(f"stored{c}"))
                    else:
                        v.tensor_tensor(of_pair(temporal, i, c), att_in[c], bank("vector", f"y{c}"), ALU.add).then_inc(*did(f"stored{c}"))
                inputs(0)
                inputs(1)
                scores_vector(v, "a0", at0, 0.25, mask)
                rows_vector(v, "a0", at0)
                probs_vector(v, "a0", at0)
                outputs(0)
                scores_vector(v, "a1", at1, 0.25, mask)
                rows_vector(v, "a1", at1)
                probs_vector(v, "a1", at1)
                outputs(1)
                store(0)
                store(1)

            def scalar(a, i):
                def heads(c):
                    a.wait_ge(*after(f"a{c}.o"))
                    a.wait_ge(*last())
                    a.activation(heads_out[c], bank("scalar", f"a{c}.o"), ACT.Copy).then_inc(*did(f"a{c}.o_read"))
                for c in range(2):
                    qk_scalar(a, f"a{c}", pair[c])
                    for q in range(4):
                        a.wait_ge(*after(f"a{c}.v"))
                        a.wait_ge(*last())
                        a.activation(pair[c].rep4[:, :, q, :], HB(bank("scalar", f"a{c}.v")), ACT.Copy).then_inc(*did(f"a{c}.rep{q}"))
                    if c:
                        heads(0)
                    exp_scalar(a, f"a{c}", pair[c].s, 0.25 if mask is None else 1.0)
                heads(1)
            return tensor, vector, scalar

        sp_bias = [W("sp_in_b", j * D, (j + 1) * D) for j in range(3)]
        spatial_stage = routed(0, lambda e: W(f"sp_q{e}"), lambda e: W(f"sp_k{e}"), lambda e: W(f"sp_v{e}"),
                               sp_bias, lambda e: W(f"sp_o{e}"), W("sp_out_b"), W("norm_s_w"), W("norm_s_b"), None)
        temporal_stage = routed(1, lambda e: W(f"tq_{e}"), lambda e: W(f"tk_{e}"), lambda e: W(f"tv_{e}"),
                                [W("tq_b"), W("tk_b"), W("tv_b")], lambda e: W(f"tp_{e}"), W("tp_b"),
                                W("norm_t_w"), W("norm_t_b"), lambda hh: C("causal"))

        def pair_tensor(pe, i, q_src, kv_src, wq, wk, wv, project=None):
            for c in range(2):
                mm(pe, f"a{c}.q", f"a{c}.q_read", [], [(wq, of_pair(q_src, i, c))])
                mm(pe, f"a{c}.k", f"a{c}.kx3", [], [(wk, of_pair(kv_src, i, c))])
            rows_tensor(pe, "a0", at0.rep, wv, ["a0.rep3"])
            scores_tensor(pe, "a0", at0)
            rows_tensor(pe, "a1", at1.rep, wv, ["a1.rep3"])
            scores_tensor(pe, "a1", at1)
            heads_tensor(pe, "a0", at0)
            if project is not None:
                project(0)
            heads_tensor(pe, "a1", at1)
            if project is not None:
                project(1)

        def pair_vector(v, i, kv_src, scale, mask=None):
            for c in range(2):
                rep_vector(v, f"a{c}", pair[c], of_pair(kv_src, i, c))
            rows_vector(v, "a0", at0)
            scores_vector(v, "a0", at0, scale, mask)
            rows_vector(v, "a1", at1)
            probs_vector(v, "a0", at0)
            scores_vector(v, "a1", at1, scale, mask)
            probs_vector(v, "a1", at1)

        def cross_tensor(pe, i):
            def project(c):
                mm(pe, f"y{c}", f"sum{c}", [f"a{c}.o_read"], [(W("cr_out"), heads_out[c])])
            pair_tensor(pe, i, spatial, temporal, W("cr_in", 0, D), W("cr_in", D, 2 * D), W("cr_in", 2 * D, 3 * D), project)

        def cross_vector(v, i):
            v.wait_ge(*last())
            v.tensor_scalar(cr_kb, C("head"), W("cross_in_b", 1, 2), None, ALU.mult).then_inc(*did("kb"))
            pair_vector(v, i, temporal, 0.25)
            for c in range(2):
                v.wait_ge(*last())
                v.tensor_scalar(att_in[c], of_pair(ln2, i, c), W("cross_out_b"), None, ALU.add).then_inc(*did(f"x_bias{c}"))
            for c in range(2):
                v.wait_ge(*after(f"y{c}"))
                v.wait_ge(*last())
                v.tensor_tensor(of_pair(ln2, i, c), att_in[c], bank("vector", f"y{c}"), ALU.add).then_inc(*did(f"sum{c}"))

        def cross_scalar(a, i):
            for c in range(2):
                qk_scalar(a, f"a{c}", pair[c], W("cross_in_b", 0, 1), cr_kb, ["kb"])
            for c in range(2):
                exp_scalar(a, f"a{c}", pair[c].s, 0.25)
            for c in range(2):
                a.wait_ge(*after(f"a{c}.o"))
                a.wait_ge(*last())
                a.activation(heads_out[c], bank("scalar", f"a{c}.o"), ACT.Identity, bias=W("cross_in_b", 2, 3)).then_inc(*did(f"a{c}.o_read"))

        def mlp_tensor(pe, i):
            for c in range(2):
                for f in range(4):
                    mm(pe, f"u{c}.{f}", f"g{c}.{f}", [], [(W("mlp_1", f * P, (f + 1) * P), of_pair(xa, i, c))])
            for c in range(2):
                mm(pe, f"y{c}", f"h_new{c}", [f"g{c}.3"], [(W("mlp_2", f * D, (f + 1) * D), part(masked_x[c], f)) for f in range(4)])

        def mlp_vector(v, i):
            for c in range(2):
                v.wait_ge(*last())
                v.tensor_scalar(att_in[c], of_pair(ln2, i, c), W("mlp_b2"), None, ALU.add).then_inc(*did(f"x_bias{c}"))
                v.wait_ge(*last())
                v.tensor_tensor(att_in[c], att_in[c], of_pair(h, i, c), ALU.add).then_inc(*did(f"x_h{c}"))
            for c in range(2):
                v.wait_ge(*after(f"y{c}"))
                v.wait_ge(*last())
                v.tensor_tensor(of_pair(h, i, c), att_in[c], bank("vector", f"y{c}"), ALU.add).then_inc(*did(f"h_new{c}"))

        def mlp_scalar(a, i):
            for c in range(2):
                for f in range(4):
                    a.wait_ge(*after(f"u{c}.{f}"))
                    a.wait_ge(*last())
                    a.activation(part(masked_x[c], f), bank("scalar", f"u{c}.{f}"), ACT.Gelu,
                                 bias=W("mlp_b1", f, f + 1)).then_inc(*did(f"g{c}.{f}"))

        def l3_tensor(pe, i):
            pair_tensor(pe, i, xa, xa, W("l3_q"), W("l3_k"), W("l3_v"))

        def l3_vector(v, i):
            pair_vector(v, i, xa, 0.25, lambda hh: W("l3_rel", hh * T, (hh + 1) * T))
            for c in range(2):
                v.wait_ge(*after(f"a{c}.o"))
                v.wait_ge(*last())
                v.tensor_tensor(of_pair(h, i, c), of_pair(h, i, c), bank("vector", f"a{c}.o"), ALU.add).then_inc(*did(f"a{c}.o_read"))

        def l3_scalar(a, i):
            for c in range(2):
                qk_scalar(a, f"a{c}", pair[c])
            for c in range(2):
                exp_scalar(a, f"a{c}", pair[c].s, 1.0)

        ar = new_arena()
        r3 = [ar.take(CH) for _ in range(4)]
        lo2 = [ar.take(CH) for _ in range(4)]
        gl, gw3, gs3 = ar.take(NT * 5), ar.take(NT * 4), ar.take(64)
        wide = ar.take(NT * 64)
        wide_t, wlo, l3x = ar.take(CH), ar.take(CH), ar.take(CH)
        ER = E3 * R3

        def l3e_tensor(pe, i):
            ps = fill(pe, "gates", "gates_read")
            pe.wait_ge(*after("x"))
            for t in range(NT):
                ins = pe.matmul(ps[:, 5 * t:5 * t + 5], l3x[:, t * P:(t + 1) * P], W("l3_gate", 0, 5),
                                start=True, stop=True)
            ins.then_inc(*did("gates"))
            for e in range(4):
                mm(pe, f"f{e}", f"relu{e}", [], [(W(f"fc1_{e}"), l3x)])
            mm(pe, "lo", "wlo", ["relu3"], [(W("lora_a", e * ER, (e + 1) * ER), r3[e]) for e in range(4)])
            ps = fill(pe, "wide_t", "wide_t_read")
            pe.wait_ge(*after("wide"))
            for t in range(NT):
                ins = pe.transpose(ps[0:ER, t * P:(t + 1) * P], wide[:, t * ER:(t + 1) * ER], C("ident"))
            ins.then_inc(*did("wide_t"))
            for e in range(4):
                mm(pe, f"l{e}", f"lo{e}", ["wlo"], [(W("lora_b", e * D, (e + 1) * D)[0:ER, :], wlo[0:ER, :])])
            mm(pe, "y", "h_new", ["lo2", "lo3"], [(W(f"fc2_{e}"), lo2[e]) for e in range(4)])

        def l3e_vector(v, i):
            v.wait_ge(*last())
            v.tensor_copy(l3x, xa[:, bass.ts(i, CH)]).then_inc(*did("x"))
            g3 = gl.rearrange("p (t e) -> p t e", e=5)
            w3 = gw3.rearrange("p (t e) -> p t e", e=4)
            col = lambda n: gs3[:, 4 * n:4 * n + 4]
            sp = lambda n: col(n).unsqueeze(2).to_broadcast([P, NT, 4])
            v.wait_ge(*after("gates"))
            v.wait_ge(*last())
            v.tensor_copy(gl, bank("vector", "gates")[:, 0:20]).then_inc(*did("gates_read"))
            v.wait_ge(*last())
            v.tensor_reduce(col(0), g3[:, :, 0:4], AX_X, ALU.max).then_inc(*did("max"))
            v.wait_ge(*last())
            v.tensor_tensor(w3, g3[:, :, 0:4], sp(0), ALU.subtract).then_inc(*did("sub"))
            v.wait_ge(*after("gexp"))
            v.wait_ge(*last())
            v.tensor_reduce(col(1), w3, AX_X, ALU.add).then_inc(*did("esum"))
            v.wait_ge(*last())
            v.reciprocal(col(2), col(1)).then_inc(*did("erec"))
            v.wait_ge(*last())
            v.tensor_tensor(w3, w3, sp(2), ALU.mult).then_inc(*did("soft"))
            v.wait_ge(*after("tsig"))
            v.wait_ge(*last())
            v.tensor_scalar(col(4), col(3), 1.0 / E3, None, ALU.mult).then_inc(*did("thr"))
            v.wait_ge(*last())
            v.tensor_tensor(w3, w3, sp(4), ALU.subtract).then_inc(*did("adapted"))
            v.wait_ge(*last())
            v.tensor_scalar(gw3, gw3, 0.0, None, ALU.max).then_inc(*did("selected"))
            v.wait_ge(*last())
            v.tensor_reduce(col(5), w3, AX_X, ALU.add).then_inc(*did("wsum"))
            v.wait_ge(*last())
            v.tensor_scalar(col(6), col(5), 0.0, None, ALU.is_equal).then_inc(*did("none"))
            v.wait_ge(*last())
            v.tensor_tensor(col(5), col(5), col(6), ALU.add).then_inc(*did("wsum1"))
            v.wait_ge(*last())
            v.reciprocal(col(7), col(5)).then_inc(*did("wrec"))
            v.wait_ge(*last())
            v.tensor_tensor(w3, w3, sp(7), ALU.mult).then_inc(*did("weights"))
            v.wait_ge(*last())
            v.tensor_copy(wide.rearrange("p (te r) -> p te r", r=R3), gw3.unsqueeze(2).to_broadcast([P, NT * 4, R3])).then_inc(*did("wide"))
            v.wait_ge(*after("wide_t"))
            v.wait_ge(*last())
            v.tensor_copy(wide_t[0:ER, :], bank("vector", "wide_t")[0:ER, :]).then_inc(*did("wide_t_read"))
            v.wait_ge(*after("lo"))
            v.wait_ge(*last())
            v.tensor_tensor(wlo[0:ER, :], wide_t[0:ER, :], bank("vector", "lo")[0:ER, :], ALU.mult).then_inc(*did("wlo"))
            for e in range(1, 4, 2):
                v.wait_ge(*after(f"l{e}"))
                v.wait_ge(*last())
                v.tensor_copy(lo2[e], bank("vector", f"l{e}")).then_inc(*did(f"lo{e}"))
            residual_vector(v, i, "y")

        def l3e_scalar(a, i):
            a.wait_ge(*after("sub"))
            a.wait_ge(*last())
            a.activation(gw3, gw3, ACT.Exp).then_inc(*did("gexp"))
            for e in range(4):
                a.wait_ge(*after(f"f{e}"))
                a.wait_ge(*last())
                a.activation(r3[e], bank("scalar", f"f{e}"), ACT.Relu).then_inc(*did(f"relu{e}"))
            a.wait_ge(*last())
            a.activation(gs3[:, 12:16], gl.rearrange("p (t e) -> p t e", e=5)[:, :, 4], ACT.Sigmoid).then_inc(*did("tsig"))
            for e in range(0, 4, 2):
                a.wait_ge(*after(f"l{e}"))
                a.wait_ge(*last())
                a.activation(lo2[e], bank("scalar", f"l{e}"), ACT.Copy).then_inc(*did(f"lo{e}"))

        o_rows = new_arena().take(2 * CH).rearrange("p (k c) -> p k c", k=2)
        out_tiles = out.rearrange("b t d -> (b t) d").rearrange("(c k p) d -> c p k d", k=NT, p=P)

        def write_tensor(pe):
            for c in range(NCH):
                ps = fill(pe, f"t{c}", f"r{c}")
                for t in range(NT):
                    at = c * CH + t * P
                    ins = pe.transpose(ps[:, t * P:(t + 1) * P], h[:, at:at + P], C("ident"))
                ins.then_inc(*did(f"t{c}"))

        def write_scalar(a):
            for c in range(NCH):
                if c >= 2:
                    a.wait_ge(stored[c % 2], 16 * (c // 2))
                a.wait_ge(*after(f"t{c}"))
                a.wait_ge(*last())
                a.activation(o_rows[:, c % 2, :], bank("scalar", f"t{c}"), ACT.Copy).then_inc(*did(f"r{c}"))

        def write_sync(sp):
            for c in range(NCH):
                sp.wait_ge(*after(f"r{c}"))
                sp.dma_start(out_tiles[c], o_rows[:, c % 2, :].rearrange("p (k d) -> p k d", d=D)).then_inc(stored[c % 2], 16)
            for n in range(2):
                sp.wait_ge(stored[n], 16 * NCH // 2)

        def start_vector(v):
            v.wait_ge(*last())
            v.memset(gh[0], 0.0).then_inc(*did("h0"))

        block = ctx.enter_context(nc.Block())

        @block.sync
        def _(sp):
            sp.dma_start(vec[:, :], weights[:, vec_at:W_COLS]).then_inc(tok_loaded, 16)
            begin("sync", "select")
            select_sync(sp)
            lead(sp, "select")
            begin("sync", "l0_norm")
            lead(sp, "l0_norm")
            begin("sync", "l0_attention")
            with sp.Fori(0, NCH):
                lead(sp, "l0_attention")
            begin("sync", "gru_norm")
            lead(sp, "gru_norm")
            begin("sync", "gru_input")
            with sp.Fori(0, NCH):
                lead(sp, "gru_input")
            begin("sync", "gru_start")
            lead(sp, "gru_start")
            begin("sync", "gru")
            with sp.Fori(0, T // GRU_U):
                lead(sp, "gru")
            begin("sync", "gru_output")
            with sp.Fori(0, NCH):
                lead(sp, "gru_output")
            begin("sync", "l1_norm")
            lead(sp, "l1_norm")
            begin("sync", "l1_attention")
            with sp.Fori(0, NCH):
                lead(sp, "l1_attention")
            begin("sync", "experts_norm")
            lead(sp, "experts_norm")
            begin("sync", "experts_norm2")
            lead(sp, "experts_norm2")
            begin("sync", "experts")
            sp.dma_start(wt[:, 0:third_at - second_at], weights[:, second_at:third_at]).then_inc(second_loaded, 16)
            with sp.Fori(0, NCH):
                lead(sp, "experts")
            begin("sync", "l2_norm")
            lead(sp, "l2_norm")
            begin("sync", "l2_input")
            sp.dma_start(wt[:, experts_at:experts_at + vec_at - third_at],
                         weights[:, third_at:vec_at]).then_inc(third_loaded, 16)
            with sp.Fori(0, NCH):
                lead(sp, "l2_input")
            begin("sync", "l2_scan")
            lead(sp, "l2_scan")
            begin("sync", "l2_output")
            lead(sp, "l2_output")
            begin("sync", "pool")
            lead(sp, "pool")
            begin("sync", "route")
            lead(sp, "route")
            begin("sync", "l2_norm_again")
            lead(sp, "l2_norm_again")
            begin("sync", "l2_spatial")
            with sp.Fori(0, NCH // 2):
                lead(sp, "l2_spatial")
            begin("sync", "l2_temporal")
            with sp.Fori(0, NCH // 2):
                lead(sp, "l2_temporal")
            begin("sync", "l2_cross")
            with sp.Fori(0, NCH // 2):
                lead(sp, "l2_cross")
            begin("sync", "mlp_norm")
            lead(sp, "mlp_norm")
            begin("sync", "l2_mlp")
            with sp.Fori(0, NCH // 2):
                lead(sp, "l2_mlp")
            begin("sync", "l3_norm")
            lead(sp, "l3_norm")
            begin("sync", "l3_attention")
            with sp.Fori(0, NCH // 2):
                lead(sp, "l3_attention")
            begin("sync", "l3_experts_norm")
            lead(sp, "l3_experts_norm")
            begin("sync", "l3_experts")
            with sp.Fori(0, NCH):
                lead(sp, "l3_experts")
            begin("sync", "write")
            write_sync(sp)
            lead(sp, "write")

        @block.tensor
        def _(pe):
            begin("tensor", "select")
            select_tensor(pe)
            meet(pe, "tensor", "select")
            begin("tensor", "l0_norm")
            norm_h_xa[0](pe)
            meet(pe, "tensor", "l0_norm")
            begin("tensor", "l0_attention")
            with pe.Fori(0, NCH) as i:
                l0_tensor(pe, i)
                meet(pe, "tensor", "l0_attention")
            begin("tensor", "gru_norm")
            norm_h_xa[0](pe)
            meet(pe, "tensor", "gru_norm")
            begin("tensor", "gru_input")
            with pe.Fori(0, NCH) as i:
                gru_input_tensor(pe, i)
                meet(pe, "tensor", "gru_input")
            begin("tensor", "gru_start")
            meet(pe, "tensor", "gru_start")
            begin("tensor", "gru")
            with pe.Fori(0, T // GRU_U) as i:
                gru_tensor(pe, i)
                meet(pe, "tensor", "gru")
            begin("tensor", "gru_output")
            with pe.Fori(0, NCH) as i:
                gru_output_tensor(pe, i)
                meet(pe, "tensor", "gru_output")
            begin("tensor", "l1_norm")
            norm_h_xa[0](pe)
            meet(pe, "tensor", "l1_norm")
            begin("tensor", "l1_attention")
            with pe.Fori(0, NCH) as i:
                l1_tensor(pe, i)
                meet(pe, "tensor", "l1_attention")
            begin("tensor", "experts_norm")
            norm_h_xa[0](pe)
            meet(pe, "tensor", "experts_norm")
            begin("tensor", "experts_norm2")
            norm_experts[0](pe)
            meet(pe, "tensor", "experts_norm2")
            begin("tensor", "experts")
            with pe.Fori(0, NCH) as i:
                experts_tensor(pe, i)
                meet(pe, "tensor", "experts")
            begin("tensor", "l2_norm")
            norm_h_ln2[0](pe)
            meet(pe, "tensor", "l2_norm")
            begin("tensor", "l2_input")
            pe.wait_ge(second_loaded, 16)
            with pe.Fori(0, NCH) as i:
                l2_input_tensor(pe, i)
                meet(pe, "tensor", "l2_input")
            begin("tensor", "l2_scan")
            meet(pe, "tensor", "l2_scan")
            begin("tensor", "l2_output")
            l2_output_tensor(pe)
            meet(pe, "tensor", "l2_output")
            begin("tensor", "pool")
            norm_h_ln2[0](pe)
            meet(pe, "tensor", "pool")
            begin("tensor", "route")
            route_tensor(pe)
            meet(pe, "tensor", "route")
            begin("tensor", "l2_norm_again")
            norm_ln2_xa[0](pe)
            meet(pe, "tensor", "l2_norm_again")
            begin("tensor", "l2_spatial")
            with pe.Fori(0, NCH // 2) as i:
                spatial_stage[0](pe, i)
                meet(pe, "tensor", "l2_spatial")
            begin("tensor", "l2_temporal")
            with pe.Fori(0, NCH // 2) as i:
                temporal_stage[0](pe, i)
                meet(pe, "tensor", "l2_temporal")
            begin("tensor", "l2_cross")
            with pe.Fori(0, NCH // 2) as i:
                cross_tensor(pe, i)
                meet(pe, "tensor", "l2_cross")
            begin("tensor", "mlp_norm")
            norm_mlp[0](pe)
            meet(pe, "tensor", "mlp_norm")
            begin("tensor", "l2_mlp")
            with pe.Fori(0, NCH // 2) as i:
                mlp_tensor(pe, i)
                meet(pe, "tensor", "l2_mlp")
            begin("tensor", "l3_norm")
            norm_h_xa[0](pe)
            meet(pe, "tensor", "l3_norm")
            begin("tensor", "l3_attention")
            pe.wait_ge(third_loaded, 16)
            with pe.Fori(0, NCH // 2) as i:
                l3_tensor(pe, i)
                meet(pe, "tensor", "l3_attention")
            begin("tensor", "l3_experts_norm")
            norm_h_xa[0](pe)
            meet(pe, "tensor", "l3_experts_norm")
            begin("tensor", "l3_experts")
            with pe.Fori(0, NCH) as i:
                l3e_tensor(pe, i)
                meet(pe, "tensor", "l3_experts")
            begin("tensor", "write")
            write_tensor(pe)
            meet(pe, "tensor", "write")

        @block.vector
        def _(v):
            begin("vector", "select")
            select_vector(v)
            meet(v, "vector", "select")
            begin("vector", "l0_norm")
            norm_h_xa[1](v)
            meet(v, "vector", "l0_norm")
            begin("vector", "l0_attention")
            with v.Fori(0, NCH) as i:
                l0_vector(v, i)
                meet(v, "vector", "l0_attention")
            begin("vector", "gru_norm")
            norm_h_xa[1](v)
            meet(v, "vector", "gru_norm")
            begin("vector", "gru_input")
            with v.Fori(0, NCH) as i:
                gru_input_vector(v, i)
                meet(v, "vector", "gru_input")
            begin("vector", "gru_start")
            start_vector(v)
            meet(v, "vector", "gru_start")
            begin("vector", "gru")
            with v.Fori(0, T // GRU_U) as i:
                gru_vector(v, i)
                meet(v, "vector", "gru")
            begin("vector", "gru_output")
            with v.Fori(0, NCH) as i:
                gru_output_vector(v, i)
                meet(v, "vector", "gru_output")
            begin("vector", "l1_norm")
            norm_h_xa[1](v)
            meet(v, "vector", "l1_norm")
            begin("vector", "l1_attention")
            with v.Fori(0, NCH) as i:
                l1_vector(v, i)
                meet(v, "vector", "l1_attention")
            begin("vector", "experts_norm")
            norm_h_xa[1](v)
            meet(v, "vector", "experts_norm")
            begin("vector", "experts_norm2")
            norm_experts[1](v)
            meet(v, "vector", "experts_norm2")
            begin("vector", "experts")
            with v.Fori(0, NCH) as i:
                experts_vector(v, i)
                meet(v, "vector", "experts")
            begin("vector", "l2_norm")
            norm_h_ln2[1](v)
            meet(v, "vector", "l2_norm")
            begin("vector", "l2_input")
            v.wait_ge(second_loaded, 16)
            with v.Fori(0, NCH) as i:
                l2_input_vector(v, i)
                meet(v, "vector", "l2_input")
            begin("vector", "l2_scan")
            l2_scan_vector(v)
            meet(v, "vector", "l2_scan")
            begin("vector", "l2_output")
            l2_output_vector(v)
            meet(v, "vector", "l2_output")
            begin("vector", "pool")
            pool_vector(v)
            meet(v, "vector", "pool")
            begin("vector", "route")
            route_vector(v)
            meet(v, "vector", "route")
            begin("vector", "l2_norm_again")
            norm_ln2_xa[1](v)
            meet(v, "vector", "l2_norm_again")
            begin("vector", "l2_spatial")
            with v.Fori(0, NCH // 2) as i:
                spatial_stage[1](v, i)
                meet(v, "vector", "l2_spatial")
            begin("vector", "l2_temporal")
            with v.Fori(0, NCH // 2) as i:
                temporal_stage[1](v, i)
                meet(v, "vector", "l2_temporal")
            begin("vector", "l2_cross")
            with v.Fori(0, NCH // 2) as i:
                cross_vector(v, i)
                meet(v, "vector", "l2_cross")
            begin("vector", "mlp_norm")
            norm_mlp[1](v)
            meet(v, "vector", "mlp_norm")
            begin("vector", "l2_mlp")
            with v.Fori(0, NCH // 2) as i:
                mlp_vector(v, i)
                meet(v, "vector", "l2_mlp")
            begin("vector", "l3_norm")
            norm_h_xa[1](v)
            meet(v, "vector", "l3_norm")
            begin("vector", "l3_attention")
            v.wait_ge(third_loaded, 16)
            with v.Fori(0, NCH // 2) as i:
                l3_vector(v, i)
                meet(v, "vector", "l3_attention")
            begin("vector", "l3_experts_norm")
            norm_h_xa[1](v)
            meet(v, "vector", "l3_experts_norm")
            begin("vector", "l3_experts")
            with v.Fori(0, NCH) as i:
                l3e_vector(v, i)
                meet(v, "vector", "l3_experts")
            begin("vector", "write")
            meet(v, "vector", "write")

        @block.scalar
        def _(a):
            begin("scalar", "select")
            select_scalar(a)
            meet(a, "scalar", "select")
            begin("scalar", "l0_norm")
            norm_h_xa[2](a)
            meet(a, "scalar", "l0_norm")
            begin("scalar", "l0_attention")
            with a.Fori(0, NCH) as i:
                l0_scalar(a, i)
                meet(a, "scalar", "l0_attention")
            begin("scalar", "gru_norm")
            norm_h_xa[2](a)
            meet(a, "scalar", "gru_norm")
            begin("scalar", "gru_input")
            with a.Fori(0, NCH) as i:
                gru_input_scalar(a, i)
                meet(a, "scalar", "gru_input")
            begin("scalar", "gru_start")
            meet(a, "scalar", "gru_start")
            begin("scalar", "gru")
            with a.Fori(0, T // GRU_U) as i:
                gru_scalar(a, i)
                meet(a, "scalar", "gru")
            begin("scalar", "gru_output")
            with a.Fori(0, NCH) as i:
                gru_output_scalar(a, i)
                meet(a, "scalar", "gru_output")
            begin("scalar", "l1_norm")
            norm_h_xa[2](a)
            meet(a, "scalar", "l1_norm")
            begin("scalar", "l1_attention")
            with a.Fori(0, NCH) as i:
                l1_scalar(a, i)
                meet(a, "scalar", "l1_attention")
            begin("scalar", "experts_norm")
            norm_h_xa[2](a)
            meet(a, "scalar", "experts_norm")
            begin("scalar", "experts_norm2")
            norm_experts[2](a)
            meet(a, "scalar", "experts_norm2")
            begin("scalar", "experts")
            with a.Fori(0, NCH) as i:
                experts_scalar(a, i)
                meet(a, "scalar", "experts")
            begin("scalar", "l2_norm")
            norm_h_ln2[2](a)
            meet(a, "scalar", "l2_norm")
            begin("scalar", "l2_input")
            a.wait_ge(second_loaded, 16)
            with a.Fori(0, NCH) as i:
                l2_input_scalar(a, i)
                meet(a, "scalar", "l2_input")
            begin("scalar", "l2_scan")
            meet(a, "scalar", "l2_scan")
            begin("scalar", "l2_output")
            l2_output_scalar(a)
            meet(a, "scalar", "l2_output")
            begin("scalar", "pool")
            norm_h_ln2[2](a)
            meet(a, "scalar", "pool")
            begin("scalar", "route")
            route_scalar(a)
            meet(a, "scalar", "route")
            begin("scalar", "l2_norm_again")
            norm_ln2_xa[2](a)
            meet(a, "scalar", "l2_norm_again")
            begin("scalar", "l2_spatial")
            with a.Fori(0, NCH // 2) as i:
                spatial_stage[2](a, i)
                meet(a, "scalar", "l2_spatial")
            begin("scalar", "l2_temporal")
            with a.Fori(0, NCH // 2) as i:
                temporal_stage[2](a, i)
                meet(a, "scalar", "l2_temporal")
            begin("scalar", "l2_cross")
            with a.Fori(0, NCH // 2) as i:
                cross_scalar(a, i)
                meet(a, "scalar", "l2_cross")
            begin("scalar", "mlp_norm")
            norm_mlp[2](a)
            meet(a, "scalar", "mlp_norm")
            begin("scalar", "l2_mlp")
            with a.Fori(0, NCH // 2) as i:
                mlp_scalar(a, i)
                meet(a, "scalar", "l2_mlp")
            begin("scalar", "l3_norm")
            norm_h_xa[2](a)
            meet(a, "scalar", "l3_norm")
            begin("scalar", "l3_attention")
            a.wait_ge(third_loaded, 16)
            with a.Fori(0, NCH // 2) as i:
                l3_scalar(a, i)
                meet(a, "scalar", "l3_attention")
            begin("scalar", "l3_experts_norm")
            norm_h_xa[2](a)
            meet(a, "scalar", "l3_experts_norm")
            begin("scalar", "l3_experts")
            with a.Fori(0, NCH) as i:
                l3e_scalar(a, i)
                meet(a, "scalar", "l3_experts")
            begin("scalar", "write")
            write_scalar(a)
            meet(a, "scalar", "write")

        @block.gpsimd
        def _(g):
            begin("gpsimd", "select")
            select_gpsimd(g)
            meet(g, "gpsimd", "select")
            begin("gpsimd", "l0_norm")
            meet(g, "gpsimd", "l0_norm")
            begin("gpsimd", "l0_attention")
            with g.Fori(0, NCH) as i:
                meet(g, "gpsimd", "l0_attention")
            begin("gpsimd", "gru_norm")
            meet(g, "gpsimd", "gru_norm")
            begin("gpsimd", "gru_input")
            with g.Fori(0, NCH) as i:
                meet(g, "gpsimd", "gru_input")
            begin("gpsimd", "gru_start")
            meet(g, "gpsimd", "gru_start")
            begin("gpsimd", "gru")
            with g.Fori(0, T // GRU_U) as i:
                meet(g, "gpsimd", "gru")
            begin("gpsimd", "gru_output")
            with g.Fori(0, NCH) as i:
                meet(g, "gpsimd", "gru_output")
            begin("gpsimd", "l1_norm")
            meet(g, "gpsimd", "l1_norm")
            begin("gpsimd", "l1_attention")
            with g.Fori(0, NCH) as i:
                meet(g, "gpsimd", "l1_attention")
            begin("gpsimd", "experts_norm")
            meet(g, "gpsimd", "experts_norm")
            begin("gpsimd", "experts_norm2")
            meet(g, "gpsimd", "experts_norm2")
            begin("gpsimd", "experts")
            with g.Fori(0, NCH) as i:
                meet(g, "gpsimd", "experts")
            begin("gpsimd", "l2_norm")
            meet(g, "gpsimd", "l2_norm")
            begin("gpsimd", "l2_input")
            g.wait_ge(second_loaded, 16)
            with g.Fori(0, NCH) as i:
                meet(g, "gpsimd", "l2_input")
            begin("gpsimd", "l2_scan")
            meet(g, "gpsimd", "l2_scan")
            begin("gpsimd", "l2_output")
            meet(g, "gpsimd", "l2_output")
            begin("gpsimd", "pool")
            meet(g, "gpsimd", "pool")
            begin("gpsimd", "route")
            meet(g, "gpsimd", "route")
            begin("gpsimd", "l2_norm_again")
            meet(g, "gpsimd", "l2_norm_again")
            begin("gpsimd", "l2_spatial")
            with g.Fori(0, NCH // 2) as i:
                meet(g, "gpsimd", "l2_spatial")
            begin("gpsimd", "l2_temporal")
            with g.Fori(0, NCH // 2) as i:
                meet(g, "gpsimd", "l2_temporal")
            begin("gpsimd", "l2_cross")
            with g.Fori(0, NCH // 2) as i:
                meet(g, "gpsimd", "l2_cross")
            begin("gpsimd", "mlp_norm")
            meet(g, "gpsimd", "mlp_norm")
            begin("gpsimd", "l2_mlp")
            with g.Fori(0, NCH // 2) as i:
                meet(g, "gpsimd", "l2_mlp")
            begin("gpsimd", "l3_norm")
            meet(g, "gpsimd", "l3_norm")
            begin("gpsimd", "l3_attention")
            g.wait_ge(third_loaded, 16)
            with g.Fori(0, NCH // 2) as i:
                meet(g, "gpsimd", "l3_attention")
            begin("gpsimd", "l3_experts_norm")
            meet(g, "gpsimd", "l3_experts_norm")
            begin("gpsimd", "l3_experts")
            with g.Fori(0, NCH) as i:
                meet(g, "gpsimd", "l3_experts")
            begin("gpsimd", "write")
            meet(g, "gpsimd", "write")
    if known is not None:
        steps.check_order()
    return steps


def kernel(**inputs):
    import concourse.bacc as bacc
    from concourse.bass_utils import run_bass_kernel_spmd

    x = np.ascontiguousarray(inputs["x"])
    a = {k: np.asarray(v) for k, v in inputs.items()}
    packed = np.concatenate([lay(a).astype(np.float32, copy=False) for _, _, lay in weight_list()], axis=1)
    consts = np.concatenate([np.asarray(c, np.float32).reshape(P, -1) for _, c in constant_list()], axis=1)

    def program(known):
        nc = bacc.Bacc("TRN2", target_bir_lowering=False, num_devices=1)
        args = [nc.dram_tensor(n, v.shape, F32, kind="ExternalInput").ap()
                for n, v in (("in_x", x), ("in_w", packed), ("in_c", consts))]
        o = nc.dram_tensor("out_0", (B, T, D), F32, kind="ExternalOutput").ap()
        return nc, tower(nc, *args, o, known)
    _, counts = program(None)
    nc, _ = program(counts)
    r = run_bass_kernel_spmd(nc, [{"in_x": x, "in_w": np.ascontiguousarray(packed), "in_c": consts}], core_ids=[0])
    return r.results[0]["out_0"]
```

```python
from contextlib import ExitStack

import numpy as np

import concourse.bass as bass
from concourse import mybir

F32 = mybir.dt.float32
U32 = mybir.dt.uint32
ALU = mybir.AluOpType
ACT = mybir.ActivationFunctionType
AX_X = mybir.AxisListType.X

P = 128
D = 128
B = 64
S_IN = 256
BLOCK = 128
TOP = 16
T = S_IN // BLOCK * TOP
TOK = B * T
CH = 512
NCH = TOK // CH
CB = CH // T
NT = CH // P
E1 = 8
E2 = 4
E3 = 4
GRU_U = 16
NORM_TAIL = 4
R3 = 16
EPS = 1e-5
NEG = -1e30
WIDE = 2.0 ** -10
XG = 8



def _blocks(w):
    k = w.shape[0] // P
    return w.reshape(k, P, w.shape[1]).transpose(1, 0, 2).reshape(P, k * w.shape[1])


def _rows(w):
    out = np.zeros((P, w.shape[1]), w.dtype)
    out[: w.shape[0]] = w
    return out


def _cols(v):
    return v.reshape(-1, P).T


def _adapter_a(w):
    out = np.zeros((P, E3 * R3 * E3), w.dtype)
    for e in range(E3):
        at = e * E3 * R3 + e * R3
        out[:, at:at + R3] = w[e]
    return out


def _adapter_b(w):
    out = np.zeros((P, E3 * D), w.dtype)
    for e in range(E3):
        out[e * R3:(e + 1) * R3, e * D:(e + 1) * D] = w[e]
    return out


def _relative(w):
    i, j = np.arange(T)[:, None], np.arange(T)[None, :]
    m = w[0][:, i - j + 63].transpose(1, 0, 2).reshape(T, 8 * T)
    return np.tile(m, (4, 1))


def _head_pairs(w):
    return _blocks(w.reshape(2, 4, 64, w.shape[1]).transpose(1, 0, 2, 3).reshape(w.shape))


def weight_list():
    w = []

    def add(name, n, lay):
        w.append((name, n, lay))
    for n in ("q_u", "k_u", "v_u", "q_c", "k_c", "v_c"):
        add(n, 512, lambda a, n=n: a["L0_attn_w_" + n])
    add("l0_out", 512, lambda a: _head_pairs(a["L0_attn_w_out"]))
    for n in ("uz", "ur", "u"):
        add("g_" + n, 256, lambda a, n=n: a["L0_ffn_W" + n].T)
    for n in ("wz", "wr", "w"):
        add("g_" + n, 512, lambda a, n=n: _blocks(a["L0_ffn_W" + n].T))
    add("g_o", 256, lambda a: _blocks(a["L0_ffn_Wo"].T))
    for s in range(3):
        add(f"l1_qkv{s}", 384, lambda a, s=s: a["L1_attn_Wqkv"][s].T)
        add(f"l1_o{s}", 128, lambda a, s=s: a["L1_attn_Wo"][s].T)
    add("l1_f", 384, lambda a: _blocks(a["L1_attn_Wf"].T))
    add("moe_r", 8, lambda a: a["L1_ffn_w_r"].T)
    add("moe_br", 8, lambda a: _rows(a["L1_ffn_b_r"][None]))
    add("moe_b2", 128, lambda a: _rows(a["L1_ffn_b2"]))
    for e in range(E1):
        add(f"moe_1_{e}", 512, lambda a, e=e: a["L1_ffn_W1"][e])
        add(f"moe_2_{e}", 512, lambda a, e=e: _blocks(a["L1_ffn_W2"][e]))
    add("l2_in", 256, lambda a: a["L2_attn_W_in"].T)
    add("l2_out", 128, lambda a: a["L2_attn_W_out"].T)
    add("rt_1", 128, lambda a: a["L2_ffn_router_w1"].T)
    add("rt_2", 8, lambda a: a["L2_ffn_router_w2"].T)
    add("rt_b2", 8, lambda a: _rows(a["L2_ffn_router_b2"][None]))
    for e in range(E2):
        add(f"sp_q{e}", 128, lambda a, e=e: a["L2_ffn_sp_in_w"][e][:D].T)
        add(f"sp_k{e}", 128, lambda a, e=e: a["L2_ffn_sp_in_w"][e][D:2 * D].T)
        add(f"sp_v{e}", 128, lambda a, e=e: a["L2_ffn_sp_in_w"][e][2 * D:].T)
        add(f"sp_o{e}", 128, lambda a, e=e: a["L2_ffn_sp_out_w"][e].T)
        for n in "qkvp":
            add(f"t{n}_{e}", 128, lambda a, e=e, n=n: a[f"L2_ffn_t{n}_w"][e].T)
    add("sp_in_b", 384, lambda a: _rows(a["L2_ffn_sp_in_b"]))
    add("sp_out_b", 128, lambda a: _rows(a["L2_ffn_sp_out_b"]))
    for n in "qkvp":
        add(f"t{n}_b", 128, lambda a, n=n: _rows(a[f"L2_ffn_t{n}_b"]))
    add("cr_in", 384, lambda a: a["L2_ffn_cross_in_w"].T)
    add("cr_out", 128, lambda a: a["L2_ffn_cross_out_w"].T)
    add("mlp_1", 512, lambda a: a["L2_ffn_mlp_w1"].T)
    add("mlp_2", 512, lambda a: _blocks(a["L2_ffn_mlp_w2"].T))
    for n in "qkv":
        add("l3_" + n, 128, lambda a, n=n: a["L3_attn_W" + n].T)
    add("l3_rel", 8 * T, lambda a: _relative(a["L3_attn_rel_pos_bias"]))
    add("l3_gate", 4, lambda a: a["L3_ffn_gate_w"].T)
    add("l3_thr", 1, lambda a: a["L3_ffn_thr_w"].T)
    for e in range(E3):
        add(f"fc1_{e}", 128, lambda a, e=e: a["L3_ffn_fc1_w"][e].T)
        add(f"fc2_{e}", 128, lambda a, e=e: a["L3_ffn_fc2_w"][e].T)
    add("lora_a", E3 * E3 * R3, lambda a: _adapter_a(a["L3_ffn_lora_A"]))
    add("lora_b", E3 * D, lambda a: _adapter_b(a["L3_ffn_lora_B"]))
    add("tok_w", D, lambda a: np.broadcast_to(a["L0_tok_W"], (P, D)))
    add("tok_b", 1, lambda a: np.broadcast_to(a["L0_tok_b"][None], (P, 1)))
    for n in ("buz", "bwz", "bur", "bwr", "bu", "bw"):
        add(n, 2, lambda a, n=n: _cols(a["L0_ffn_" + n]))
    add("g_bo", 1, lambda a: _cols(a["L0_ffn_bo"]))
    for s in range(3):
        add(f"l1_bqkv{s}", 3, lambda a, s=s: _cols(a["L1_attn_bqkv"][s]))
        add(f"l1_bo{s}", 1, lambda a, s=s: _cols(a["L1_attn_bo"][s]))
    add("l1_bf", 1, lambda a: _cols(a["L1_attn_bf"]))
    add("ln_g", 1, lambda a: _cols(a["L1_ffn_ln_g"]))
    add("ln_b", 1, lambda a: _cols(a["L1_ffn_ln_b"]))
    add("moe_b1", 4 * E1, lambda a: _cols(a["L1_ffn_b1"].reshape(-1)))
    add("l2_bin", 2, lambda a: _cols(a["L2_attn_b_in"]))
    for n in ("b_out", "A", "B", "gamma", "beta"):
        add("l2_" + n, 1, lambda a, n=n: _cols(a["L2_attn_" + n]))
    for n in ("router_b1", "norm_s_w", "norm_s_b", "norm_t_w", "norm_t_b", "norm_mlp_w", "norm_mlp_b",
              "cross_out_b", "mlp_b2"):
        add(n, 1, lambda a, n=n: _cols(a["L2_ffn_" + n]))
    add("cross_in_b", 3, lambda a: _cols(a["L2_ffn_cross_in_b"]))
    add("mlp_b1", 4, lambda a: _cols(a["L2_ffn_mlp_b1"]))
    return w


VECTORS_FROM, SECOND_FROM, THIRD_FROM = "tok_w", "l2_in", "l3_q"


def constant_list():
    p = np.arange(P)
    row = p % T
    j, q = np.arange(T), np.arange(4)
    f = np.arange(P)
    later = (j[None, :] >= row[:, None])
    same = (p[:, None] // 32 == q[None, :])

    def band(width):
        d = row[:, None] - j[None, :]
        return np.where((d >= 0) & (d < width), 0.0, NEG)
    return [
        ("ident", np.eye(P)),
        ("mean", np.full((P, P), 1.0 / P)),
        ("first", np.broadcast_to((row == 0)[:, None], (P, P))),
        ("half", p[:, None] // 64 == np.arange(2)[None]),
        ("head", (p[:, None] // 16) % 4 == q[None]),
        ("v16", (f[None] // 16) % 4 == p[:, None] // 32),
        ("t1m", later * 0.125),
        ("sgm", same[:, :, None] * (row[:, None] > j[None])[:, None, :]),
        ("causal", band(T)), ("band5", band(5)), ("band10", band(10)),
        ("base", p[:, None] * BLOCK),
        ("iota8", np.broadcast_to(np.arange(8), (P, 8))),
        ("row0", np.broadcast_to(p[:, None] == 0, (P, P))),
        ("pick", (p[:, None, None] == q[None, :, None]) * np.ones((1, 1, P))),
        ("eps", np.full((P, 1), EPS)),
        ("eps_wide", np.full((P, 1), EPS * WIDE ** 2)),
        ("zero", np.zeros((P, 1))),
    ]


def offsets(items):
    at, out = 0, {}
    for name, n in items:
        out[name] = (at, n)
        at += n
    return out, at


W_AT, W_COLS = offsets([(n, c) for n, c, _ in weight_list()])
C_AT, C_COLS = offsets([(n, int(np.prod(np.asarray(a).shape[1:]))) for n, a in constant_list()])


class Steps:

    def __init__(self, known):
        self.known = known
        self.table, self.banks, self.sems, self.log = {}, {}, {}, {}

    def begin(self, who, stage):
        self.who, self.stage, self.count = who, stage, 0

    def did(self, key):
        self.count += 1
        assert (self.stage, key) not in self.table, (self.stage, key)
        self.table[self.stage, key] = (self.who, self.count)
        self.log.setdefault((self.stage, self.who), []).append(("did", key))
        return self.sems[self.stage, self.who], 1

    def after(self, key):
        self.log.setdefault((self.stage, self.who), []).append(("after", key))
        by, n = self.known.table[self.stage, key] if self.known else (ENGINES[0], 1)
        return self.sems[self.stage, by], n

    def last(self):
        return self.sems[self.stage, self.who], self.count

    def check_order(self):
        for stage in dict.fromkeys(s for s, _ in self.log):
            lists = {w: l for (s, w), l in self.log.items() if s == stage}
            at, done = dict.fromkeys(lists, 0), set()
            moved = True
            while moved:
                moved = False
                for w, l in lists.items():
                    while at[w] < len(l) and (l[at[w]][0] == "did" or l[at[w]][1] in done):
                        if l[at[w]][0] == "did":
                            done.add(l[at[w]][1])
                        at[w] += 1
                        moved = True
            stuck = {w: l[at[w]] for w, l in lists.items() if at[w] < len(l)}
            assert not stuck, (stage, stuck)


STAGES = ["select", "l0_norm", "l0_attention", "gru_norm", "gru_input", "gru_start", "gru", "gru_output", "l1_norm",
          "l1_attention", "experts_norm", "experts_norm2", "experts", "l2_norm", "l2_input", "l2_scan", "l2_output",
          "pool", "route", "l2_norm_again", "l2_spatial", "l2_temporal", "l2_cross", "mlp_norm", "l2_mlp",
          "l3_norm", "l3_attention", "l3_experts_norm", "l3_experts", "write"]
ENGINES = ("tensor", "vector", "scalar", "gpsimd")


def tower(nc, x, weights, constants, out, known):
    steps = Steps(known)
    did, after, last = steps.did, steps.after, steps.last
    with ExitStack() as ctx:
        def sem(name):
            return ctx.enter_context(nc.semaphore(name))

        h = ctx.enter_context(nc.sbuf_tensor("h", [P, TOK], F32))
        xa = ctx.enter_context(nc.sbuf_tensor("xa", [P, TOK], F32))
        ln2 = ctx.enter_context(nc.sbuf_tensor("ln2", [P, TOK], F32))
        vec_at, second_at = W_AT[VECTORS_FROM][0], W_AT[SECOND_FROM][0]
        wt = ctx.enter_context(nc.sbuf_tensor("wt", [P, second_at], F32))
        third_at, experts_at = W_AT[THIRD_FROM][0], W_AT["moe_r"][0]
        assert third_at - second_at <= experts_at
        vec = ctx.enter_context(nc.sbuf_tensor("vec", [P, W_COLS - vec_at], F32))
        cs = ctx.enter_context(nc.sbuf_tensor("cs", [P, C_COLS], F32))
        arena = ctx.enter_context(nc.sbuf_tensor("arena", [P, 18432], F32))
        psum = ctx.enter_context(nc.psum_tensor("psum", [P, 8, 512], F32))
        small = ctx.enter_context(nc.sbuf_tensor("small", [P, 944], F32))

        for s in STAGES:
            for who in ENGINES:
                steps.sems[s, who] = sem(f"{s}_{who}_done")
        x_loaded = [sem(f"x_loaded{n}") for n in range(4)]
        c_loaded, w_loaded, rest_loaded = sem("constants_loaded"), sem("first_weights_loaded"), sem("other_weights_loaded")
        gathered, stored = [sem(f"rows_gathered{q}") for q in range(4)], [sem("output_stored0"), sem("output_stored1")]
        arrived = sem("engines_arrived")
        go = {who: sem(f"{who}_may_go") for who in ENGINES}

        def W(name, a=0, b=None):
            at, n = W_AT[name]
            b = n if b is None else b
            if at >= vec_at:
                return vec[:, at - vec_at + a:at - vec_at + b]
            if at >= third_at:
                at += experts_at - third_at
            elif at >= second_at:
                at -= second_at
            return wt[:, at + a:at + b]

        def C(name, a=0, b=None):
            at, n = C_AT[name]
            return cs[:, at + a:at + (n if b is None else b)]

        class Places:

            def __init__(self, buf, size):
                self.buf, self.at, self.size = buf, 0, size

            def take(self, n):
                a = self.at
                self.at += n
                assert self.at <= self.size, (self.at, self.size)
                return self.buf[:, a:a + n]

        def new_arena():
            return Places(arena, 18432)
        keep = Places(small, 944)

        def meet(eng, who, stage):
            eng.drain()
            eng.sem_inc(arrived, 1)
            eng.wait_ge(go[who], 1)
            eng.sem_clear(go[who])

        def lead(sp, stage):
            sp.wait_ge(arrived, len(ENGINES))
            sp.sem_clear(arrived)
            for who in ENGINES:
                sp.sem_clear(steps.sems[stage, who])
            for who in ENGINES:
                sp.sem_inc(go[who], 1)

        ring = {"next": 0, "reader": {}}

        def fill(pe, key, reader):
            b = ring["next"]
            ring["next"] = (b + 1) % 8
            if b in ring["reader"]:
                pe.wait_ge(*after(ring["reader"][b]))
            ring["reader"][b] = reader
            steps.banks[steps.stage, key] = b
            return psum[:, b, :]

        def bank(who, key):
            if steps.known is None:
                return psum[:, 0, :]
            return psum[:, steps.known.banks[steps.stage, key], :]

        def begin(who, stage):
            steps.begin(who, stage)
            if who == "tensor":
                ring["next"], ring["reader"] = 0, {}

        ATT = 8800
        att = ctx.enter_context(nc.sbuf_tensor("att", [P, ATT], F32))

        def part(buf, c):
            return buf[:, c * CH:(c + 1) * CH]

        centred, squares = att[:, 0:TOK], att[:, TOK:2 * TOK]
        stats, fits = att[:, 2 * TOK:2 * TOK + CH], att[:, 2 * TOK + CH:2 * TOK + 2 * CH]

        def norm_tensor(pe, src):
            def mean(c):
                ps = fill(pe, f"mean{c}", f"centred{c}")
                pe.matmul(ps, C("mean"), part(src, c), start=True, stop=True).then_inc(*did(f"mean{c}"))

            def variance(c):
                ps = fill(pe, f"var{c}", f"log{c}")
                pe.wait_ge(*after(f"square{c}"))
                pe.matmul(ps, C("mean"), part(squares, c), start=True, stop=True).then_inc(*did(f"var{c}"))
            for c in range(NCH):
                mean(c)
                if c == NCH - 2:
                    variance(0)
            for c in range(1, NCH):
                variance(c)
            stay_warm(pe, NORM_TAIL)

        def square_scalar(a, c, scale=1.0):
            a.wait_ge(*after(f"centred{c}"))
            a.wait_ge(*last())
            a.activation(part(squares, c), part(centred, c), ACT.Square, scale=scale).then_inc(*did(f"square{c}"))

        def norm_scalar(a):
            a.preload_act_table_set("natural_log_exp_and_others")
            for c in range(0, NCH, 2):
                square_scalar(a, c)
            for c in range(NCH):
                a.wait_ge(*after(f"var{c}"))
                a.wait_ge(*last())
                a.activation(part(squares, c), bank("scalar", f"var{c}"), ACT.Ln, bias=C("eps")).then_inc(*did(f"log{c}"))
                a.wait_ge(*last())
                a.activation(part(squares, c), part(squares, c), ACT.Exp, scale=-0.5, bias=C("zero")).then_inc(*did(f"rstd{c}"))

        def centre_vector(v, src, c):
            v.wait_ge(*after(f"mean{c}"))
            v.wait_ge(*last())
            v.tensor_tensor(part(centred, c), part(src, c), bank("vector", f"mean{c}"), ALU.subtract).then_inc(*did(f"centred{c}"))

        def norm(src, dst, gain=None, bias=None):
            def tensor(pe):
                norm_tensor(pe, src)

            def vector(v):
                for c in range(NCH):
                    centre_vector(v, src, c)
                    if c % 2:
                        v.wait_ge(*last())
                        v.tensor_tensor(part(squares, c), part(centred, c), part(centred, c), ALU.mult).then_inc(*did(f"square{c}"))
                for c in range(NCH):
                    v.wait_ge(*after(f"rstd{c}"))
                    v.wait_ge(*last())
                    v.tensor_tensor(part(dst, c), part(centred, c), part(squares, c), ALU.mult).then_inc(*did(f"n{c}"))
                    if gain is not None:
                        v.wait_ge(*last())
                        v.tensor_scalar(part(dst, c), part(dst, c), gain, bias, ALU.mult, ALU.add).then_inc(*did(f"gained{c}"))
            return tensor, vector, norm_scalar

        def wide_norm_tensor(pe, src, ready):
            for c in range(NCH):
                ps = fill(pe, f"mean{c}", f"centred{c}")
                pe.wait_ge(*after(f"{ready}{c}"))
                pe.matmul(ps, C("mean"), part(src, c), start=True, stop=True).then_inc(*did(f"mean{c}"))
            ps = fill(pe, "var", "std")
            for c in range(NCH):
                pe.wait_ge(*after(f"square{c}"))
                ins = pe.matmul(ps[32 * c:32 * c + 32, :], C("mean", 0, 32), part(squares, c), start=True, stop=True)
            ins.then_inc(*did("var"))
            for c in range(NCH):
                ps = fill(pe, f"spread{c}", f"n{c}")
                pe.wait_ge(*after("rstd"))
                rows = slice(32 * c, 32 * c + 32)
                pe.matmul(ps, C("first")[rows, :], stats[rows, :], start=True, stop=True).then_inc(*did(f"spread{c}"))

        def wide_norm_scalar(a):
            for c in range(NCH):
                square_scalar(a, c, WIDE)
            a.wait_ge(*after("fits"))
            a.wait_ge(*last())
            a.activation(stats, bank("scalar", "var"), ACT.Sqrt, bias=C("eps_wide")).then_inc(*did("std"))

        norm_h_xa, norm_h_ln2, norm_ln2_xa = norm(h, xa), norm(h, ln2), norm(ln2, xa)
        norm_experts = norm(xa, ln2, W("ln_g"), W("ln_b"))
        norm_mlp = norm(ln2, xa, W("norm_mlp_w"), W("norm_mlp_b"))

        def stay_warm(pe, n):
            b = ring["next"]
            ring["next"] = (b + 1) % 8
            pe.wait_ge(*after(ring["reader"].pop(b)))
            for _ in range(n):
                pe.matmul(psum[:, b, :], C("mean"), h[:, 0:CH], start=True, stop=True)

        def mm(pe, key, reader, needs, products):
            ps = fill(pe, key, reader)
            for step in needs:
                pe.wait_ge(*after(step))
            n = len(products)
            for i, (lhs, rhs) in enumerate(products):
                m = lhs.shape[1]
                ins = pe.matmul(ps[0:m, 0:rhs.shape[-1]] if len(rhs.shape) == 2 else ps[0:m, :].rearrange("p (a b) -> p a b", b=rhs.shape[-1]),
                                lhs, rhs, start=i == 0, stop=i == n - 1)
            ins.then_inc(*did(key))

        HB = lambda ap: ap.rearrange("p (b t) -> p b t", t=T)
        Q4 = lambda ap: ap.rearrange("p (b q t) -> p b q t", q=4, t=T)

        ar = new_arena()
        XC = BLOCK // XG * D
        xin = [ar.take(XC) for _ in range(4)]
        prod = [ar.take(XC) for _ in range(3)]
        rows = ar.take(TOP * D)
        score, work = ar.take(BLOCK), ar.take(BLOCK)
        val, idx, idf = ar.take(TOP), ar.take(TOP).bitcast(U32), ar.take(TOP)
        x_blocks = x.rearrange("b (n s) d -> (b n) (s d)", s=BLOCK)
        x_rows = x.rearrange("b s d -> (b s) d")

        def select_sync(sp):
            for n in range(XG):
                if n >= 4:
                    sp.wait_ge(*after(f"prod{n - 4}"))
                sp.dma_start(xin[n % 4], x_blocks[:, XC * n:XC * (n + 1)]).then_inc(x_loaded[n % 4], 16)
                if n == 3:
                    sp.dma_start(cs[:, :], constants).then_inc(c_loaded, 16)
            sp.dma_start(wt[:, 0:first_at], weights[:, 0:first_at]).then_inc(w_loaded, 16)
            for q in range(4):
                sp.wait_ge(gathered[q], 16 * TOP // 4)
            for a in range(first_at, second_at, W_STEP):
                b = min(a + W_STEP, second_at)
                sp.dma_start(wt[:, a:b], weights[:, a:b]).then_inc(rest_loaded, 16)

        W_STEP = 4096
        first_at = W_AT["g_uz"][0]
        n_weight_loads = len(range(first_at, second_at, W_STEP))

        def group(buf):
            return buf.rearrange("p (s d) -> p s d", d=D)

        def select_vector(v):
            v.wait_ge(tok_loaded, 16)
            for n in range(0, XG, 2):
                v.wait_ge(x_loaded[n % 4], 16 * (n // 4 + 1))
                v.wait_ge(*last())
                v.tensor_tensor(group(prod[0]), group(xin[n % 4]), W("tok_w").unsqueeze(1).to_broadcast([P, XC // D, D]),
                                ALU.mult).then_inc(*did(f"prod{n}"))
                for m in ((n,), (n, n - 1), (n, n - 1), (n, n - 1, n + 1))[n // 2]:
                    if m % 2:
                        v.wait_ge(*after(f"prod{m}"))
                    v.wait_ge(*last())
                    v.tensor_reduce(score[:, XC // D * m:XC // D * (m + 1)], group(prod[0 if m % 2 == 0 else 1 + m // 2 % 2]), AX_X,
                                    ALU.add).then_inc(*did(f"score{m}"))
            v.wait_ge(*last())
            v.tensor_scalar(score, score, tok_b[:, 0:1], None, ALU.add).then_inc(*did("score"))
            src = score
            for r in range(2):
                v.wait_ge(*last())
                v.max(val[:, 8 * r:8 * r + 8], src).then_inc(*did(f"max{r}"))
                v.wait_ge(*last())
                v.max_index(idx[:, 8 * r:8 * r + 8], val[:, 8 * r:8 * r + 8], src).then_inc(*did(f"index{r}"))
                if r == 0:
                    v.wait_ge(*last())
                    v.match_replace(work, val[:, 0:8], src, -3e38).then_inc(*did("taken"))
                    src = work
            v.wait_ge(*last())
            v.tensor_copy(idf, idx).then_inc(*did("index_f"))
            v.wait_ge(c_loaded, 16)
            v.wait_ge(*last())
            v.tensor_scalar(idx, idf, C("base"), None, ALU.add).then_inc(*did("row_index"))

        def select_gpsimd(g):
            g.wait_ge(tok_loaded, 16)
            for n in range(1, XG, 2):
                g.wait_ge(x_loaded[n % 4], 16 * (n // 4 + 1))
                if n >= 5:
                    g.wait_ge(*after(f"score{n - 4}"))
                g.tensor_tensor(group(prod[1 + n // 2 % 2]), group(xin[n % 4]), W("tok_w").unsqueeze(1).to_broadcast([P, XC // D, D]),
                                ALU.mult).then_inc(*did(f"prod{n}"))
            g.wait_ge(*after("row_index"))
            for r in range(TOP):
                g.indirect_dma_start(out=rows[:, r * D:(r + 1) * D], out_offset=None, in_=x_rows,
                                     in_offset=bass.IndirectOffsetOnAxis(ap=idx[:, r:r + 1], axis=0)).then_inc(gathered[r // 4], 16)

        def select_tensor(pe):
            pe.wait_ge(c_loaded, 16)
            for q in range(4):
                pe.wait_ge(gathered[q], 16 * TOP // 4)
                ps = fill(pe, f"turn{q}", f"h{q}")
                for r in range(4):
                    at = 4 * q + r
                    ins = pe.transpose(ps[:, r * P:(r + 1) * P], rows[:, at * D:(at + 1) * D], C("ident"))
                ins.then_inc(*did(f"turn{q}"))

        def select_scalar(a):
            for q in range(4):
                a.wait_ge(*after(f"turn{q}"))
                a.wait_ge(*last())
                a.activation(h[:, :].rearrange("p (n r) -> p r n", r=TOP)[:, 4 * q:4 * q + 4, :],
                             bank("scalar", f"turn{q}").rearrange("p (r n) -> p r n", n=P), ACT.Copy).then_inc(*did(f"h{q}"))
            a.wait_ge(w_loaded, 16)
            a.wait_ge(c_loaded, 16)
            a.wait_ge(tok_loaded, 16)

        tok_loaded = sem("vectors_loaded")
        second_loaded, third_loaded = sem("layer2_weights_loaded"), sem("layer3_weights_loaded")
        tok_b = W("tok_b")

        class Attention:
            def __init__(self, places):
                self.q, self.rep, self.kx, self.vx = places.take(CH), places.take(4 * CH), places.take(4 * CH), places.take(CB * D)
                self.s = [places.take(CH), places.take(CH)]
                self.p = [places.take(CH), places.take(CH)]
                self.st = [places.take(3 * CB), places.take(3 * CB)]
                self.rep4 = self.rep.rearrange("p (b q t) -> p b q t", q=4, t=T)
                self.kx4 = self.kx.rearrange("p (b q t) -> p b q t", q=4, t=T)

        at0 = Attention(Places(att, ATT))
        at_q, at_rep, at_kx, at_vx, at_s, at_p, at_st = at0.q, at0.rep, at0.kx, at0.vx, at0.s, at0.p, at0.st

        def softmax_max_vector(v, k, s, st):
            s3 = HB(s)
            v.wait_ge(*last())
            v.tensor_reduce(st[:, 0:CB], s3, AX_X, ALU.max).then_inc(*did(f"{k}.max"))
            v.wait_ge(*last())
            v.tensor_tensor(s3, s3, st[:, 0:CB].unsqueeze(2).to_broadcast([P, CB, T]), ALU.subtract).then_inc(*did(f"{k}.sub"))

        def softmax_sum_vector(v, k, s, st):
            s3 = HB(s)
            v.wait_ge(*after(f"{k}.exp"))
            v.wait_ge(*last())
            v.tensor_reduce(st[:, CB:2 * CB], s3, AX_X, ALU.add).then_inc(*did(f"{k}.sum"))
            v.wait_ge(*last())
            v.reciprocal(st[:, 2 * CB:3 * CB], st[:, CB:2 * CB]).then_inc(*did(f"{k}.rec"))
            v.wait_ge(*last())
            v.tensor_tensor(s3, s3, st[:, 2 * CB:3 * CB].unsqueeze(2).to_broadcast([P, CB, T]), ALU.mult).then_inc(*did(f"{k}.norm"))

        def turn_half(pe, k, hh, s):
            ps = fill(pe, f"{k}.{hh}.turned", f"{k}.{hh}.p")
            pe.wait_ge(*after(f"{k}.{hh}.norm"))
            for bb in range(NT):
                ins = pe.transpose(ps[:, bb * P:(bb + 1) * P], s[:, bb * P:(bb + 1) * P], C("ident"))
            ins.then_inc(*did(f"{k}.{hh}.turned"))

        def turn_tensor(pe, k, s):
            for hh in range(2):
                turn_half(pe, k, hh, s[hh])

        def turned_scalar(a, k, p, before=()):
            for hh in range(2):
                a.wait_ge(*after(f"{k}.{hh}.turned"))
                for step in before:
                    a.wait_ge(*after(step))
                a.wait_ge(*last())
                a.activation(p[hh], bank("scalar", f"{k}.{hh}.turned"), ACT.Copy).then_inc(*did(f"{k}.{hh}.p"))

        def exp_scalar(a, k, s, scale):
            for hh in range(2):
                a.wait_ge(*after(f"{k}.{hh}.sub"))
                a.wait_ge(*last())
                a.activation(s[hh], s[hh], ACT.Exp, scale=scale).then_inc(*did(f"{k}.{hh}.exp"))

        def rows_tensor(pe, k, rep, wv, needs):
            for g in range(4):
                ps = fill(pe, f"{k}.v{g}", f"{k}.vx{g}")
                for step in needs:
                    pe.wait_ge(*after(step))
                for b in range(4):
                    ins = pe.matmul(ps[:, b * D:(b + 1) * D], rep[:, (4 * g + b) * P:(4 * g + b + 1) * P], wv,
                                    start=True, stop=True)
                ins.then_inc(*did(f"{k}.v{g}"))

        def rows_vector(v, k, at, before=()):
            for g in range(4):
                v.wait_ge(*after(f"{k}.v{g}"))
                for step in before:
                    v.wait_ge(*after(step))
                v.wait_ge(*last())
                v.tensor_tensor(at.vx[:, 4 * g * D:4 * (g + 1) * D].rearrange("p (b f) -> p b f", f=D),
                                bank("vector", f"{k}.v{g}").rearrange("p (b f) -> p b f", f=D),
                                C("v16").unsqueeze(1).to_broadcast([P, 4, D]), ALU.mult).then_inc(*did(f"{k}.vx{g}"))

        def scores_tensor(pe, k, at, masked):
            for hh in range(2):
                ps = fill(pe, f"{k}.s{hh}", f"{k}.in{hh}" if masked else f"{k}.{hh}.sub")
                pe.wait_ge(*after(f"{k}.q_read"))
                pe.wait_ge(*after(f"{k}.kx3"))
                for b in range(CB):
                    b4, bb = b % 4, b // 4
                    ins = pe.matmul(ps[b4 * T:(b4 + 1) * T, bb * P:(bb + 1) * P], at.q[64 * hh:64 * hh + 64, b * T:(b + 1) * T],
                                    at.kx[64 * hh:64 * hh + 64, b * P:(b + 1) * P], start=True, stop=True)
                ins.then_inc(*did(f"{k}.s{hh}"))

        def scores_vector(v, k, at, scale, mask=None, before=()):
            for hh in range(2):
                kk, scores, st = f"{k}.{hh}", bank("vector", f"{k}.s{hh}"), at.st[hh]
                v.wait_ge(*after(f"{k}.s{hh}"))
                for step in before:
                    v.wait_ge(*after(step))
                if mask is not None:
                    m = mask(hh)
                    n = m.shape[-1]
                    v.wait_ge(*last())
                    v.scalar_tensor_tensor(out=at.s[hh].rearrange("p (r c) -> p r c", c=n),
                                           in0=scores.rearrange("p (r c) -> p r c", c=n), scalar=scale,
                                           in1=m.unsqueeze(1).to_broadcast([P, CH // n, n]), op0=ALU.mult, op1=ALU.add).then_inc(*did(f"{k}.in{hh}"))
                    softmax_max_vector(v, kk, at.s[hh], st)
                    continue
                v.wait_ge(*last())
                v.tensor_reduce(st[:, 0:CB], HB(scores), AX_X, ALU.max).then_inc(*did(f"{kk}.max"))
                v.wait_ge(*last())
                v.tensor_tensor(HB(at.s[hh]), HB(scores), st[:, 0:CB].unsqueeze(2).to_broadcast([P, CB, T]),
                                ALU.subtract).then_inc(*did(f"{kk}.sub"))

        def probs_vector(v, k, at):
            for hh in range(2):
                softmax_sum_vector(v, f"{k}.{hh}", at.s[hh], at.st[hh])

        def heads_tensor(pe, k, at):
            ps = fill(pe, f"{k}.o", f"{k}.o_read")
            for hh in range(2):
                pe.wait_ge(*after(f"{k}.{hh}.p"))
                pe.wait_ge(*after(f"{k}.vx3"))
                for b in range(CB):
                    ins = pe.matmul(ps[64 * hh:64 * hh + 64, b * T:(b + 1) * T],
                                    at.vx[:, b * D + 64 * hh:b * D + 64 * hh + 64],
                                    at.p[hh][:, b * T:(b + 1) * T], start=True, stop=True)
            ins.then_inc(*did(f"{k}.o"))

        def rep_vector(v, k, at, src):
            for q in range(4):
                v.wait_ge(*last())
                v.tensor_copy(at.rep4[:, :, q, :], HB(src)).then_inc(*did(f"{k}.rep{q}"))

        def qk_scalar(a, k, at, bias=None, k_bias=None, needs=(), before=()):
            a.wait_ge(*after(f"{k}.q"))
            for step in before:
                a.wait_ge(*after(step))
            a.wait_ge(*last())
            if bias is None:
                a.activation(at.q, bank("scalar", f"{k}.q"), ACT.Copy).then_inc(*did(f"{k}.q_read"))
            else:
                a.activation(at.q, bank("scalar", f"{k}.q"), ACT.Identity, bias=bias).then_inc(*did(f"{k}.q_read"))
            k_scalar(a, k, at, bias, k_bias, needs)

        def k_scalar(a, k, at, bias=None, k_bias=None, needs=()):
            for q in range(4):
                a.wait_ge(*after(f"{k}.k"))
                for step in needs:
                    a.wait_ge(*after(step))
                a.wait_ge(*last())
                if bias is None:
                    a.activation(at.kx4[:, :, q, :], HB(bank("scalar", f"{k}.k")), ACT.Copy,
                                 scale=C("head", q, q + 1)).then_inc(*did(f"{k}.kx{q}"))
                else:
                    a.activation(at.kx4[:, :, q, :], HB(bank("scalar", f"{k}.k")), ACT.Identity,
                                 scale=C("head", q, q + 1), bias=k_bias[:, q:q + 1]).then_inc(*did(f"{k}.kx{q}"))

        def of_pair(buf, i, c):
            return buf[:, bass.ts(i, 2 * CH)][:, c * CH:(c + 1) * CH]

        ar = new_arena()
        qu, qc = ar.take(4 * CH), ar.take(4 * CH)
        kux, vux, kcx = ar.take(8 * CH), ar.take(8 * CH), ar.take(8 * CH)
        xs = ar.take(CH)
        t1 = [at_q, ar.take(CH)]
        su_s = [ar.take(CH), ar.take(CH)]
        sgx = [at_kx, at_rep]
        v_rows = at_vx
        sc, sg, pt = at_s, at_p, at_p
        o_tok, o_t = kux, qu

        def l0_tensor(pe, i):
            def project(name, f, reader="read"):
                mm(pe, f"{name}{f}", f"{name}{f}.{reader}", [], [(W(name, f * P, (f + 1) * P), xa[:, bass.ts(i, CH)])])
            for f in range(4):
                project("q_u", f)
                project("k_u", f)
            for f in range(4):
                project("v_u", f)
                project("q_c", f)

            def pairs(key, hh, reader, lhs, rhs, names):
                ps = fill(pe, f"{key}{hh}", f"{reader}{hh}")
                for f in (2 * hh, 2 * hh + 1):
                    for name in names:
                        pe.wait_ge(*after(f"{name}{f}.read"))
                    for b in range(CB):
                        ins = pe.matmul(ps[64 * (f % 2):64 * (f % 2) + 64, b * T:(b + 1) * T],
                                        lhs[:, f * 2 * CH + b * 64:f * 2 * CH + b * 64 + 64],
                                        rhs[:, f * CH + b * T:f * CH + (b + 1) * T], start=True, stop=True)
                ins.then_inc(*did(f"{key}{hh}"))
            pairs("lu_", 0, "sig_", kux, qu, ["k_u", "q_u"])
            pairs("lu_", 1, "sig_", kux, qu, ["k_u", "q_u"])
            project("k_c", 0)
            project("k_c", 1)
            pairs("t1_", 0, "t1s_", vux, qc, ["v_u", "q_c"])
            project("k_c", 2)
            project("k_c", 3)
            pairs("t1_", 1, "t1s_", vux, qc, ["v_u", "q_c"])
            for hh in range(2):
                ps = fill(pe, f"su_{hh}", f"silu_{hh}")
                pe.wait_ge(*after(f"t1s_{hh}"))
                pe.wait_ge(*after(f"sgx_{hh}"))
                for b in range(CB):
                    b4, bb = b % 4, b // 4
                    ins = pe.matmul(ps[b4 * T:(b4 + 1) * T, bb * P:(bb + 1) * P], t1[hh][:, b * T:(b + 1) * T],
                                    sgx[hh][:, b * P:(b + 1) * P], start=True, stop=True)
                ins.then_inc(*did(f"su_{hh}"))
            for hh in range(2):
                ps = fill(pe, f"sc_{hh}", f"masked_{hh}")
                for f in (2 * hh, 2 * hh + 1):
                    pe.wait_ge(*after(f"k_c{f}.read"))
                    for b in range(CB):
                        b4, at = b % 4, b // 4 * P + 64 * (f % 2)
                        ins = pe.matmul(ps[b4 * T:(b4 + 1) * T, at:at + 64], qc[:, f * CH + b * T:f * CH + (b + 1) * T],
                                        kcx[:, f * 2 * CH + b * 64:f * 2 * CH + b * 64 + 64], start=True, stop=True)
                ins.then_inc(*did(f"sc_{hh}"))
            wv = W("v_c").rearrange("p (u q d) -> p q u d", u=2, q=4)
            for g in range(4):
                ps = fill(pe, f"v{g}", f"v{g}.read")
                pe.wait_ge(*after("xs"))
                for b in range(4):
                    for h4 in range(4):
                        ins = pe.matmul(ps[h4 * T:(h4 + 1) * T, b * P:(b + 1) * P].rearrange("p (u d) -> p u d", u=2),
                                        xs[:, (4 * g + b) * T:(4 * g + b + 1) * T], wv[:, h4], start=True, stop=True)
                ins.then_inc(*did(f"v{g}"))
            outputs = None
            for hh in range(2):
                turn_half(pe, "a", hh, sc[hh])
                if outputs is None:
                    outputs = [fill(pe, f"o{h4}", f"o{h4}.read") for h4 in range(4)]
                pe.wait_ge(*after("v3.read"))
                pe.wait_ge(*after(f"a.{hh}.p"))
                for h4 in range(4):
                    for b in range(CB):
                        b4, at = b % 4, b // 4 * P + 64 * hh
                        ins = pe.matmul(outputs[h4][b4 * T:(b4 + 1) * T, at:at + 64], pt[hh][h4 * T:(h4 + 1) * T, b * T:(b + 1) * T],
                                        v_rows[h4 * T:(h4 + 1) * T, b * P + 64 * hh:b * P + 64 * hh + 64], start=True, stop=True)
                    if hh == 1:
                        ins.then_inc(*did(f"o{h4}"))
            for h4 in range(4):
                ps = fill(pe, f"ot{h4}", f"ot{h4}.read")
                pe.wait_ge(*after(f"o{h4}.read"))
                for bb in range(NT):
                    ins = pe.transpose(ps[:, bb * P:(bb + 1) * P], o_tok[:, h4 * CH + bb * P:h4 * CH + (bb + 1) * P], C("ident"))
                ins.then_inc(*did(f"ot{h4}"))
            mm(pe, "proj", "h_new", [f"ot{h4}.read" for h4 in range(4)],
               [(W("l0_out", h4 * P, (h4 + 1) * P), o_t[:, h4 * CH:(h4 + 1) * CH]) for h4 in range(4)])

        def expand(eng, who, name, dst, f):
            d4 = dst[:, f * 2 * CH:(f + 1) * 2 * CH].rearrange("p (b q t) -> p b q t", q=2, t=T)
            for q in range(2):
                key = f"{name}{f}.x{q}" if q == 0 else f"{name}{f}.read"
                eng.wait_ge(*after(f"{name}{f}"))
                eng.wait_ge(*last())
                if who == "scalar":
                    eng.activation(d4[:, :, q, :], HB(bank(who, f"{name}{f}")), ACT.Copy, scale=C("half", q, q + 1)).then_inc(*did(key))
                else:
                    eng.tensor_scalar(d4[:, :, q, :], HB(bank(who, f"{name}{f}")), C("half", q, q + 1), None, ALU.mult).then_inc(*did(key))

        def l0_vector(v, i):
            for f in range(4):
                expand(v, "vector", "k_u", kux, f)
            for f in range(4):
                v.wait_ge(*after(f"q_c{f}"))
                v.wait_ge(*last())
                v.tensor_copy(part(qc, f), bank("vector", f"q_c{f}")).then_inc(*did(f"q_c{f}.read"))
            for hh in range(2):
                v.wait_ge(*after(f"sig_{hh}"))
                v.wait_ge(*last())
                v.tensor_tensor(Q4(sgx[hh]), HB(sg[hh]).unsqueeze(2).to_broadcast([P, CB, 4, T]),
                                C("sgm").rearrange("p (q t) -> p q t", t=T).unsqueeze(1).to_broadcast([P, CB, 4, T]),
                                ALU.mult).then_inc(*did(f"sgx_{hh}"))
            for hh in range(2):
                expand(v, "vector", "k_c", kcx, 2 * hh + 1)
                v.wait_ge(*after(f"t1_{hh}"))
                v.wait_ge(*last())
                v.tensor_tensor(HB(t1[hh]), HB(bank("vector", f"t1_{hh}")), C("t1m").unsqueeze(1).to_broadcast([P, CB, T]),
                                ALU.mult).then_inc(*did(f"t1s_{hh}"))
            for hh in range(2):
                v.wait_ge(*after(f"susig_{hh}"))
                v.wait_ge(*last())
                v.tensor_tensor(su_s[hh], su_s[hh], bank("vector", f"su_{hh}"), ALU.mult).then_inc(*did(f"silu_{hh}"))
                v.wait_ge(*last())
                v.tensor_tensor(HB(su_s[hh]), C("causal").unsqueeze(1).to_broadcast([P, CB, T]), HB(su_s[hh]),
                                ALU.subtract).then_inc(*did(f"update_{hh}"))
            for hh in range(2):
                v.wait_ge(*after(f"sc_{hh}"))
                v.wait_ge(*last())
                v.scalar_tensor_tensor(out=sc[hh], in0=bank("vector", f"sc_{hh}"), scalar=0.125, in1=su_s[hh],
                                       op0=ALU.mult, op1=ALU.add).then_inc(*did(f"masked_{hh}"))
                softmax_max_vector(v, f"a.{hh}", sc[hh], at_st[hh])
            for hh in range(2):
                softmax_sum_vector(v, f"a.{hh}", sc[hh], at_st[hh])
            for h4 in (1, 3):
                v.wait_ge(*after(f"o{h4}"))
                v.wait_ge(*last())
                v.tensor_copy(part(o_tok, h4), bank("vector", f"o{h4}")).then_inc(*did(f"o{h4}.read"))
            for h4 in (1, 3):
                v.wait_ge(*after(f"ot{h4}"))
                v.wait_ge(*last())
                v.tensor_copy(part(o_t, h4), bank("vector", f"ot{h4}")).then_inc(*did(f"ot{h4}.read"))
            v.wait_ge(*after("proj"))
            v.wait_ge(*last())
            v.tensor_tensor(h[:, bass.ts(i, CH)], h[:, bass.ts(i, CH)], bank("vector", "proj"), ALU.add).then_inc(*did("h_new"))

        def l0_scalar(a, i):
            for f in range(4):
                a.wait_ge(*after(f"q_u{f}"))
                a.wait_ge(*last())
                a.activation(part(qu, f), bank("scalar", f"q_u{f}"), ACT.Copy).then_inc(*did(f"q_u{f}.read"))
            for f in range(4):
                expand(a, "scalar", "v_u", vux, f)
            a.wait_ge(*last())
            a.activation(xs, xa[:, bass.ts(i, CH)], ACT.Copy).then_inc(*did("xs"))
            for hh in range(2):
                a.wait_ge(*after(f"lu_{hh}"))
                a.wait_ge(*last())
                a.activation(sg[hh], bank("scalar", f"lu_{hh}"), ACT.Sigmoid, scale=0.125).then_inc(*did(f"sig_{hh}"))
            for f in (0, 2):
                expand(a, "scalar", "k_c", kcx, f)
            for hh in range(2):
                a.wait_ge(*after(f"su_{hh}"))
                a.wait_ge(*last())
                a.activation(su_s[hh], bank("scalar", f"su_{hh}"), ACT.Sigmoid).then_inc(*did(f"susig_{hh}"))
            def values(g):
                a.wait_ge(*after(f"v{g}"))
                a.wait_ge(*last())
                a.activation(part(v_rows, g), bank("scalar", f"v{g}"), ACT.Copy).then_inc(*did(f"v{g}.read"))
            values(0)
            values(1)
            exp_scalar(a, "a", sc, 1.0)
            values(2)
            values(3)
            turned_scalar(a, "a", pt)
            for h4 in (0, 2):
                a.wait_ge(*after(f"o{h4}"))
                a.wait_ge(*last())
                a.activation(part(o_tok, h4), bank("scalar", f"o{h4}"), ACT.Copy).then_inc(*did(f"o{h4}.read"))
            for h4 in (0, 2):
                a.wait_ge(*after(f"ot{h4}"))
                a.wait_ge(*last())
                a.activation(part(o_t, h4), bank("scalar", f"ot{h4}"), ACT.Copy).then_inc(*did(f"ot{h4}.read"))

        ar = new_arena()
        gx = {g: ar.take(T * 2 * B) for g in ("z", "r", "c")}
        hs = ar.take(T * 2 * B)
        gb = keep.take(6)
        GRU_IN = (("z", "g_uz", "buz", "bwz"), ("r", "g_ur", "bur", "bwr"), ("c", "g_u", "bu", "bw"))

        def gru_input_tensor(pe, i):
            pe.wait_ge(rest_loaded, 16 * n_weight_loads)
            for c in range(2):
                for g, w, _, _ in GRU_IN:
                    for m in range(2):
                        mm(pe, f"{g}{m}{c}", f"{g}{m}{c}.read", [], [(W(w, m * P, (m + 1) * P), of_pair(xa, i, c))])

        def gru_input_vector(v, i):
            for n, (g, _, b1, b2) in enumerate(GRU_IN):
                v.wait_ge(*last())
                v.tensor_tensor(gb[:, 2 * n:2 * n + 2], W(b1), W(b2), ALU.add).then_inc(*did(f"bias{g}"))
            for c in range(2):
                for n, (g, _, _, _) in enumerate(GRU_IN):
                    v.wait_ge(*after(f"{g}0{c}"))
                    v.wait_ge(*last())
                    v.tensor_scalar(gx_chunk(g, 0, i, c), HB(bank("vector", f"{g}0{c}")), gb[:, 2 * n:2 * n + 1], None,
                                    ALU.add).then_inc(*did(f"{g}0{c}.read"))

        def gx_chunk(g, m, i, c):
            v4 = gx[g].rearrange("p (t m b) -> p m b t", m=2, b=B)
            return v4[:, m, bass.ts(i, 2 * CB), :][:, c * CB:(c + 1) * CB, :]

        def gru_input_scalar(a, i):
            for c in range(2):
                for n, (g, _, _, _) in enumerate(GRU_IN):
                    a.wait_ge(*after(f"{g}1{c}"))
                    a.wait_ge(*after(f"bias{g}"))
                    a.wait_ge(*last())
                    a.activation(gx_chunk(g, 1, i, c), HB(bank("scalar", f"{g}1{c}")), ACT.Identity,
                                 bias=gb[:, 2 * n + 1:2 * n + 2]).then_inc(*did(f"{g}1{c}.read"))

        gru = Places(at_kx, 4 * CH)
        HW = 2 * B
        gz, gr, gc, gt, gw = [[gru.take(HW), gru.take(HW)] for _ in range(5)]
        gh = [gru.take(HW), gru.take(HW)]

        def of_step(buf, t, u):
            return buf[:, bass.ts(t, GRU_U * HW)][:, u * HW:(u + 1) * HW]

        def gru_tensor(pe, t):
            banks = {}

            def x_terms(u):
                for g in ("r", "z", "c"):
                    banks[g, u] = fill(pe, f"{g}{u}", f"{g}{u}.sig")
                    if g == "r":
                        pe.matmul(banks[g, u], C("ident"), gx[g][:, 0:CH], start=True, stop=True)
                    pe.matmul(banks[g, u][:, 0:HW], C("ident"), of_step(gx[g], t, u), start=True, stop=False)

            def h_terms(g, u, w, src):
                for m in range(2):
                    for k in range(2):
                        ins = pe.matmul(banks[g, u][:, m * B:(m + 1) * B], W(w, k * 256 + m * P, k * 256 + (m + 1) * P),
                                        src[:, k * B:(k + 1) * B], start=False, stop=m == 1 and k == 1)
                ins.then_inc(*did(f"{g}{u}"))
            x_terms(0)
            for u in range(GRU_U):
                if u:
                    pe.wait_ge(*after(f"state{u - 1}"))
                h_terms("r", u, "g_wr", gh[u % 2])
                h_terms("z", u, "g_wz", gh[u % 2])
                pe.wait_ge(*after(f"hr{u}"))
                h_terms("c", u, "g_w", gt[u % 2])
                if u + 1 < GRU_U:
                    x_terms(u + 1)

        def gru_scalar(a, t):
            for u in range(GRU_U):
                for g, dst, scale in (("r", gr, 1.0), ("z", gz, 1.0), ("c", gc, 2.0)):
                    if u >= 2 and g == "r":
                        a.wait_ge(*after(f"state{u - 2}"))
                    a.wait_ge(*after(f"{g}{u}"))
                    a.wait_ge(*last())
                    a.activation(dst[u % 2], bank("scalar", f"{g}{u}")[:, 0:HW], ACT.Sigmoid, scale=scale).then_inc(*did(f"{g}{u}.sig"))

        def gru_vector(v, t):
            for u in range(GRU_U):
                p, now, then = u % 2, gh[u % 2], gh[(u + 1) % 2]
                v.wait_ge(*after(f"r{u}.sig"))
                v.wait_ge(*last())
                v.tensor_tensor(gt[p], now, gr[p], ALU.mult).then_inc(*did(f"hr{u}"))
                v.wait_ge(*after(f"z{u}.sig"))
                v.wait_ge(*last())
                v.tensor_tensor(gw[p], now, gz[p], ALU.mult).then_inc(*did(f"zh{u}"))
                v.wait_ge(*last())
                v.tensor_scalar(gz[p], gz[p], -1.0, 1.0, ALU.mult, ALU.add).then_inc(*did(f"omz{u}"))
                v.wait_ge(*last())
                v.tensor_tensor(gw[p], gw[p], gz[p], ALU.subtract).then_inc(*did(f"base{u}"))
                v.wait_ge(*after(f"c{u}.sig"))
                v.wait_ge(*last())
                v.scalar_tensor_tensor(out=gc[p], in0=gc[p], scalar=2.0, in1=gz[p], op0=ALU.mult, op1=ALU.mult).then_inc(*did(f"zc{u}"))
                if u:
                    v.wait_ge(*after(f"z{u - 1}"))
                v.wait_ge(*last())
                v.tensor_tensor(then, gc[p], gw[p], ALU.add).then_inc(*did(f"state{u}"))
                v.wait_ge(*last())
                v.tensor_copy(of_step(hs, t, u), then).then_inc(*did(f"kept{u}"))

        states, gout = at_rep, [at_q, at_vx[:, 0:CH]]

        def gru_output_tensor(pe, i):
            for c in range(2):
                mm(pe, f"out{c}", f"sig{c}", [f"state{c}1"], [(W("g_o", m * D, (m + 1) * D), part(states, 2 * c + m)) for m in range(2)])

        def gru_output_scalar(a, i):
            for c in range(2):
                a.wait_ge(*last())
                a.activation(HB(part(states, 2 * c)), state_chunk(0, i, c), ACT.Copy).then_inc(*did(f"state{c}0"))
            for c in range(2):
                a.wait_ge(*after(f"out{c}"))
                a.wait_ge(*last())
                a.activation(gout[c], bank("scalar", f"out{c}"), ACT.Sigmoid, bias=W("g_bo")).then_inc(*did(f"sig{c}"))

        def state_chunk(m, i, c):
            return hs.rearrange("p (t m b) -> p m b t", m=2, b=B)[:, m, bass.ts(i, 2 * CB), :][:, c * CB:(c + 1) * CB, :]

        def gru_output_vector(v, i):
            for c in range(2):
                v.wait_ge(*after(f"state{c}0"))
                v.wait_ge(*last())
                v.tensor_copy(HB(part(states, 2 * c + 1)), state_chunk(1, i, c)).then_inc(*did(f"state{c}1"))
            for c in range(2):
                v.wait_ge(*after(f"sig{c}"))
                v.wait_ge(*last())
                v.tensor_tensor(of_pair(h, i, c), of_pair(h, i, c), gout[c], ALU.add).then_inc(*did(f"h_new{c}"))

        ar = new_arena()
        at1 = Attention(ar)
        pair = [at0, at1]
        l1_o, l1_y, l1_hb = [ar.take(CH) for _ in range(2)], [ar.take(CH) for _ in range(6)], [ar.take(CH) for _ in range(2)]
        l1_kb = keep.take(12)
        bands = ["band5", "band10", None]
        L1N = 6

        def l1_tensor(pe, i):
            def qk(n):
                c, s = divmod(n, 3)
                mm(pe, f"s{n}.q", f"s{n}.q_read", [], [(W(f"l1_qkv{s}", 0, D), of_pair(xa, i, c))])
                mm(pe, f"s{n}.k", f"s{n}.kx3", [], [(W(f"l1_qkv{s}", D, 2 * D), of_pair(xa, i, c))])

            def scores(n):
                scores_tensor(pe, f"s{n}", pair[n % 2], bands[n % 3] is not None)

            def rows(n):
                c, s = divmod(n, 3)
                rows_tensor(pe, f"s{n}", pair[c].rep, W(f"l1_qkv{s}", 2 * D, 3 * D), [f"x{c}.rep3"])

            def project(n):
                c, s = divmod(n, 3)
                mm(pe, f"s{n}.y", f"s{n}.y_read", [f"s{n}.o_read"], [(W(f"l1_o{s}"), l1_o[n % 2])])
                if s == 2:
                    mm(pe, f"f{c}", f"h_new{c}", [f"s{n}.y_read"], [(W("l1_f", m * D, (m + 1) * D), l1_y[3 * c + m]) for m in range(3)])
            qk(0)
            qk(1)
            rows(0)
            scores(0)
            for n in range(L1N):
                if n + 1 < L1N:
                    scores(n + 1)
                if n + 2 < L1N:
                    qk(n + 2)
                turn_tensor(pe, f"s{n}", pair[n % 2].s)
                if n + 1 < L1N:
                    rows(n + 1)
                heads_tensor(pe, f"s{n}", pair[n % 2])
                if n:
                    project(n - 1)
            project(L1N - 1)

        def l1_vector(v, i):
            def rows(n):
                rows_vector(v, f"s{n}", pair[n % 2], [f"s{n - 2}.o"] if n >= 2 else [])

            def scores(n):
                band = bands[n % 3]
                scores_vector(v, f"s{n}", pair[n % 2], 0.25, None if band is None else (lambda hh: C(band)),
                              [f"s{n - 2}.1.turned"] if n >= 2 else [])
            for c in range(2):
                rep_vector(v, f"x{c}", pair[c], of_pair(xa, i, c))
                if c == 0:
                    for s in range(3):
                        v.wait_ge(*last())
                        v.tensor_scalar(l1_kb[:, 4 * s:4 * s + 4], C("head"), W(f"l1_bqkv{s}", 1, 2), None, ALU.mult).then_inc(*did(f"kb{s}"))
            rows(0)
            scores(0)
            for n in range(L1N):
                probs_vector(v, f"s{n}", pair[n % 2])
                if n == 4:
                    l1_residual(v, i, 0)
                if n + 1 < L1N:
                    scores(n + 1)
                    rows(n + 1)
                if n < 2:
                    v.wait_ge(*last())
                    v.tensor_scalar(l1_hb[n], of_pair(h, i, n), W("l1_bf"), None, ALU.add).then_inc(*did(f"h_bias{n}"))
            l1_residual(v, i, 1)

        def l1_residual(v, i, c):
            v.wait_ge(*after(f"f{c}"))
            v.wait_ge(*last())
            v.tensor_tensor(of_pair(h, i, c), l1_hb[c], bank("vector", f"f{c}"), ALU.add).then_inc(*did(f"h_new{c}"))

        def l1_scalar(a, i):
            def qk(n):
                s = n % 3
                qk_scalar(a, f"s{n}", pair[n % 2], W(f"l1_bqkv{s}", 0, 1), l1_kb[:, 4 * s:4 * s + 4], [f"kb{s}"],
                          [f"s{n - 2}.s1"] if n >= 2 else [])

            def exps(n):
                exp_scalar(a, f"s{n}", pair[n % 2].s, 1.0 if bands[n % 3] else 0.25)

            def heads(n):
                a.wait_ge(*after(f"s{n}.o"))
                if n >= 2:
                    a.wait_ge(*after(f"s{n - 2}.y"))
                a.wait_ge(*last())
                a.activation(l1_o[n % 2], bank("scalar", f"s{n}.o"), ACT.Identity, bias=W(f"l1_bqkv{n % 3}", 2, 3)).then_inc(*did(f"s{n}.o_read"))

            def projected(n):
                a.wait_ge(*after(f"s{n}.y"))
                a.wait_ge(*last())
                a.activation(l1_y[n], bank("scalar", f"s{n}.y"), ACT.Identity, bias=W(f"l1_bo{n % 3}")).then_inc(*did(f"s{n}.y_read"))
            qk(0)
            qk(1)
            exps(0)
            for n in range(L1N):
                if n + 2 < L1N:
                    qk(n + 2)
                turned_scalar(a, f"s{n}", pair[n % 2].p)
                if n + 1 < L1N:
                    exps(n + 1)
                heads(n)
                if n:
                    projected(n - 1)
            projected(L1N - 1)

        ar = new_arena()
        hid = [[ar.take(CH) for _ in range(4)] for _ in range(2)]
        T8 = lambda ap: ap.rearrange("p (t e) -> p t e", t=NT)

        class Gating:

            def __init__(self):
                self.en = ar.take(CH)
                self.mix = ar.take(CH)
                self.lg, self.top, self.topi, self.topf = ar.take(32), ar.take(32), ar.take(32).bitcast(U32), ar.take(32)
                self.g2 = ar.take(12)
                self.oh, self.gate = ar.take(32), ar.take(32)
                self.gate_t, self.h_sum = ar.take(CH), ar.take(CH)
        gating = [Gating(), Gating()]
        EN = 2 * E1
        SECOND = 2

        def experts_tensor(pe, i):
            def logits(c):
                ps = fill(pe, f"logits{c}", f"logits{c}_read")
                pe.wait_ge(*after(f"en{c}"))
                for t in range(NT):
                    pe.matmul(ps[:, 8 * t:8 * t + 8], gating[c].en[:, t * P:(t + 1) * P], W("moe_r"), start=True, stop=False)
                    ins = pe.matmul(ps[:, 8 * t:8 * t + 8], C("row0"), W("moe_br"), start=False, stop=True)
                ins.then_inc(*did(f"logits{c}"))

            def up(n):
                c, e = divmod(n, E1)
                for f in range(4):
                    mm(pe, f"u{n}.{f}", f"g{n}.{f}", [], [(W(f"moe_1_{e}", f * P, (f + 1) * P), gating[c].en)])

            def gate_t(c):
                ps = fill(pe, f"gate_t{c}", f"gate_t{c}_read")
                pe.wait_ge(*after(f"gate{c}"))
                for t in range(NT):
                    ins = pe.transpose(ps[0:8, t * P:(t + 1) * P], gating[c].gate[:, 8 * t:8 * t + 8], C("ident"))
                ins.then_inc(*did(f"gate_t{c}"))

            def down(n):
                e = n % E1
                ps = fill(pe, f"y{n}", f"mix{n}.3")
                for t in range(NT):
                    for f in range(4):
                        pe.wait_ge(*after(f"g{n}.{f}"))
                        ins = pe.matmul(ps[:, t * P:(t + 1) * P], hid[n % 2][f][:, t * P:(t + 1) * P],
                                        W(f"moe_2_{e}", f * D, (f + 1) * D), start=f == 0, stop=f == 3)
                ins.then_inc(*did(f"y{n}"))

            def mixed(c):
                ps = fill(pe, f"mixed{c}", f"h_new{c}")
                pe.wait_ge(*after(f"gate_t{c}_read"))
                pe.matmul(ps, W("moe_b2"), gating[c].gate_t, start=True, stop=False)
                for t in range(NT):
                    pe.wait_ge(*after(f"mix{E1 * c + E1 - 1}.{t}"))
                    ins = pe.matmul(ps[:, t * P:(t + 1) * P], gating[c].mix[:, t * P:(t + 1) * P], C("ident"), start=False, stop=t == NT - 1)
                ins.then_inc(*did(f"mixed{c}"))
            logits(0)
            up(0)
            for n in range(EN):
                if n + 1 < EN:
                    up(n + 1)
                if n == SECOND:
                    logits(1)
                if n == 1:
                    gate_t(0)
                if n == SECOND + 2:
                    gate_t(1)
                down(n)
                if n == E1:
                    mixed(0)
            mixed(1)

        def gates_vector(v, c):
            gs = gating[c]
            g2, gate, oh = gs.g2, gs.gate, gs.oh
            v.wait_ge(*after(f"logits{c}"))
            v.wait_ge(*last())
            v.tensor_copy(gs.lg, bank("vector", f"logits{c}")[:, 0:32]).then_inc(*did(f"logits{c}_read"))
            for t in range(NT):
                v.wait_ge(*last())
                v.max(gs.top[:, 8 * t:8 * t + 8], gs.lg[:, 8 * t:8 * t + 8]).then_inc(*did(f"top{c}.{t}"))
                v.wait_ge(*last())
                v.max_index(gs.topi[:, 8 * t:8 * t + 8], gs.top[:, 8 * t:8 * t + 8], gs.lg[:, 8 * t:8 * t + 8]).then_inc(*did(f"topi{c}.{t}"))
            v.wait_ge(*last())
            v.tensor_copy(gs.topf, gs.topi).then_inc(*did(f"topf{c}"))
            v.wait_ge(*last())
            v.tensor_tensor(g2[:, 0:4], T8(gs.top)[:, :, 1], T8(gs.top)[:, :, 0], ALU.subtract).then_inc(*did(f"gap{c}"))
            v.wait_ge(*after(f"gap_exp{c}"))
            v.wait_ge(*last())
            v.tensor_scalar(g2[:, 8:12], g2[:, 4:8], 1.0, None, ALU.add).then_inc(*did(f"gate_sum{c}"))
            v.wait_ge(*last())
            v.reciprocal(g2[:, 0:4], g2[:, 8:12]).then_inc(*did(f"gate_1{c}"))
            v.wait_ge(*last())
            v.tensor_tensor(g2[:, 4:8], g2[:, 4:8], g2[:, 0:4], ALU.mult).then_inc(*did(f"gate_2{c}"))
            for n, dst in ((0, gate), (1, oh)):
                v.wait_ge(*last())
                v.tensor_tensor(T8(dst), C("iota8").unsqueeze(1).to_broadcast([P, NT, 8]),
                                T8(gs.topf)[:, :, n:n + 1].to_broadcast([P, NT, 8]), ALU.is_equal).then_inc(*did(f"hot{c}.{n}"))
                v.wait_ge(*last())
                v.tensor_tensor(T8(dst), T8(dst), g2[:, 4 * n:4 * n + 4].unsqueeze(2).to_broadcast([P, NT, 8]),
                                ALU.mult).then_inc(*did(f"weighted{c}.{n}"))
            v.wait_ge(*last())
            v.tensor_tensor(gate, gate, oh, ALU.add).then_inc(*did(f"gate{c}"))

        def experts_vector(v, i):
            for c in range(2):
                v.wait_ge(*last())
                v.tensor_copy(gating[c].en, of_pair(ln2, i, c)).then_inc(*did(f"en{c}"))
            gates_vector(v, 0)
            for c in range(2):
                v.wait_ge(*last())
                v.tensor_tensor(gating[c].h_sum, of_pair(h, i, c), of_pair(xa, i, c), ALU.add).then_inc(*did(f"h_sum{c}"))
                v.wait_ge(*last())
                v.memset(gating[c].gate_t, 0.0).then_inc(*did(f"gate_t{c}_zero"))
            for n in range(EN):
                c, e = divmod(n, E1)
                mix, gate = gating[c].mix, gating[c].gate
                for t in range(NT):
                    v.wait_ge(*after(f"y{n}"))
                    v.wait_ge(*last())
                    cols = slice(t * P, (t + 1) * P)
                    y = bank("vector", f"y{n}")[:, cols]
                    if e == 0:
                        v.tensor_scalar(mix[:, cols], y, gate[:, 8 * t + e:8 * t + e + 1], None, ALU.mult).then_inc(*did(f"mix{n}.{t}"))
                    else:
                        v.scalar_tensor_tensor(out=mix[:, cols], in0=y, scalar=gate[:, 8 * t + e:8 * t + e + 1], in1=mix[:, cols],
                                               op0=ALU.mult, op1=ALU.add).then_inc(*did(f"mix{n}.{t}"))
                if n == SECOND - 1:
                    gates_vector(v, 1)
                if n in (1, SECOND + 2):
                    k = 0 if n == 1 else 1
                    v.wait_ge(*after(f"gate_t{k}"))
                    v.wait_ge(*last())
                    v.tensor_copy(gating[k].gate_t[0:8, :], bank("vector", f"gate_t{k}")[0:8, :]).then_inc(*did(f"gate_t{k}_read"))
                if n in (E1, EN - 1):
                    k = 0 if n == E1 else 1
                    v.wait_ge(*after(f"mixed{k}"))
                    v.wait_ge(*last())
                    v.tensor_tensor(of_pair(h, i, k), gating[k].h_sum, bank("vector", f"mixed{k}"), ALU.add).then_inc(*did(f"h_new{k}"))

        def experts_scalar(a, i):
            def gap_exp(c):
                a.wait_ge(*after(f"gap{c}"))
                a.wait_ge(*last())
                a.activation(gating[c].g2[:, 4:8], gating[c].g2[:, 0:4], ACT.Exp).then_inc(*did(f"gap_exp{c}"))
            gap_exp(0)
            for n in range(EN):
                e = n % E1
                for f in range(4):
                    a.wait_ge(*after(f"u{n}.{f}"))
                    if n >= 2:
                        a.wait_ge(*after(f"y{n - 2}"))
                    a.wait_ge(*last())
                    a.activation(hid[n % 2][f], bank("scalar", f"u{n}.{f}"), ACT.Gelu,
                                 bias=W("moe_b1", 4 * e + f, 4 * e + f + 1)).then_inc(*did(f"g{n}.{f}"))
                if n == SECOND + 1:
                    gap_exp(1)

        ar = new_arena()
        ga, bz, hscan = ar.take(TOK), ar.take(TOK), ar.take(TOK)
        l2_bb = keep.take(1)
        gsig, scanned, with_in = [ar.take(CH), ar.take(CH)], ar.take(TOK), ar.take(TOK)
        pool_, pool_sum = keep.take(B), keep.take(B)

        def pos_major(ap, i, c):
            return ap.rearrange("p (t b) -> p b t", b=B)[:, bass.ts(i, 2 * CB), :][:, c * CB:(c + 1) * CB, :]

        def l2_input_tensor(pe, i):
            for c in range(2):
                for n, r in ((1, "g_sig"), (0, "bz")):
                    mm(pe, f"in{n}{c}", f"{r}{c}", [], [(W("l2_in", n * D, (n + 1) * D), of_pair(ln2, i, c))])

        def l2_input_vector(v, i):
            v.wait_ge(*last())
            v.tensor_tensor(l2_bb, W("l2_bin", 0, 1), W("l2_B"), ALU.mult).then_inc(*did("bias_b"))
            for c in range(2):
                v.wait_ge(*after(f"in0{c}"))
                v.wait_ge(*last())
                v.tensor_scalar(pos_major(bz, i, c), HB(bank("vector", f"in0{c}")), W("l2_B"), l2_bb, ALU.mult, ALU.add).then_inc(*did(f"bz{c}"))
            for c in range(2):
                v.wait_ge(*after(f"g_sig{c}"))
                v.wait_ge(*last())
                v.tensor_scalar(pos_major(ga, i, c), HB(gsig[c]), W("l2_A"), None, ALU.mult).then_inc(*did(f"ga{c}"))

        def l2_input_scalar(a, i):
            for c in range(2):
                a.wait_ge(*after(f"in1{c}"))
                a.wait_ge(*last())
                a.activation(gsig[c], bank("scalar", f"in1{c}"), ACT.Sigmoid, bias=W("l2_bin", 1, 2)).then_inc(*did(f"g_sig{c}"))

        def l2_scan_vector(v):
            v.wait_ge(*last())
            v.memset(ga.rearrange("p (t b) -> p t b", b=B)[:, :, 0:1], 0.0).then_inc(*did("starts"))
            v.wait_ge(*last())
            v.tensor_tensor_scan(hscan, ga, bz, 0.0, ALU.mult, ALU.add).then_inc(*did("scan"))

        def l2_output_tensor(pe):
            for c in range(NCH):
                mm(pe, f"out{c}", f"y{c}", [f"scanned{c}"], [(W("l2_out"), part(scanned, c))])
            wide_norm_tensor(pe, with_in, "y")

        def l2_output_vector(v):
            for c in range(NCH):
                v.wait_ge(*last())
                v.tensor_scalar(part(with_in, c), part(ln2, c), W("l2_b_out"), None, ALU.add).then_inc(*did(f"x{c}"))
            for c in range(NCH):
                v.wait_ge(*after(f"out{c}"))
                v.wait_ge(*last())
                v.tensor_tensor(part(with_in, c), part(with_in, c), bank("vector", f"out{c}"), ALU.add).then_inc(*did(f"y{c}"))
            for c in range(NCH):
                centre_vector(v, with_in, c)
            v.wait_ge(*after("var"))
            v.wait_ge(*last())
            v.tensor_scalar(fits, bank("vector", "var"), 2.0 ** 128 * WIDE ** 2 / P, None, ALU.is_lt).then_inc(*did("fits"))
            v.wait_ge(*after("std"))
            v.wait_ge(*last())
            v.reciprocal(stats, stats).then_inc(*did("reciprocal"))
            v.wait_ge(*last())
            v.tensor_tensor(stats, stats, fits, ALU.mult).then_inc(*did("rstd"))
            for c in range(NCH):
                v.wait_ge(*after(f"spread{c}"))
                v.wait_ge(*last())
                v.scalar_tensor_tensor(out=part(centred, c), in0=part(centred, c), scalar=WIDE, in1=bank("vector", f"spread{c}"),
                                       op0=ALU.mult, op1=ALU.mult).then_inc(*did(f"n{c}"))
                v.wait_ge(*last())
                v.tensor_scalar(part(centred, c), part(centred, c), W("l2_gamma"), W("l2_beta"), ALU.mult, ALU.add).then_inc(*did(f"scaled{c}"))
                v.wait_ge(*last())
                v.tensor_tensor(part(h, c), part(h, c), part(centred, c), ALU.add).then_inc(*did(f"h_new{c}"))

        def l2_output_scalar(a):
            for c in range(NCH):
                a.wait_ge(*last())
                a.activation(HB(part(scanned, c)), hscan.rearrange("p (t b) -> p b t", b=B)[:, c * CB:(c + 1) * CB, :],
                             ACT.Copy).then_inc(*did(f"scanned{c}"))
            wide_norm_scalar(a)

        r_h, r_sel = keep.take(B), keep.take(8)
        r_t = keep.take(2 * B)
        r_b = keep.take(8 * B)
        r_w = keep.take(64)
        outs = Places(wt, second_at)
        outs.at = experts_at + vec_at - third_at
        spatial, temporal, routed_bias = outs.take(TOK), outs.take(TOK), outs.take(6 * B)

        def route_tensor(pe):
            mm(pe, "h", "gelu", [], [(W("rt_1"), pool_)])
            ps = fill(pe, "logits", "logits_read")
            pe.wait_ge(*after("gelu"))
            pe.matmul(ps[0:B, 0:8], r_h, W("rt_2"), start=True, stop=False)
            pe.matmul(ps[0:B, 0:8], C("row0", 0, B), W("rt_b2"), start=False, stop=True).then_inc(*did("logits"))
            ps = fill(pe, "turned", "turned_read")
            pe.wait_ge(*after("sel"))
            for n in range(2):
                ins = pe.transpose(ps[0:4, n * B:(n + 1) * B], r_sel[0:B, 4 * n:4 * n + 4], C("ident")[0:B, 0:B])
            ins.then_inc(*did("turned"))
            ps = fill(pe, "spread", "spread_read")
            pe.wait_ge(*after("turned_read"))
            for n in range(2):
                for e in range(E2):
                    ins = pe.matmul(ps[:, (4 * n + e) * B:(4 * n + e + 1) * B], C("pick", e * P, (e + 1) * P),
                                    r_t[:, n * B:(n + 1) * B], start=True, stop=True)
            ins.then_inc(*did("spread"))
            ps = fill(pe, "biases", "biases_read")
            rows = (W("sp_in_b", 0, D), W("sp_in_b", 2 * D, 3 * D), W("sp_out_b"), W("tq_b"), W("tv_b"), W("tp_b"))
            for n, w in enumerate(rows):
                at = n // 3 * B
                ins = pe.matmul(ps[:, n * B:(n + 1) * B], w, r_t[:, at:at + B], start=True, stop=True)
            ins.then_inc(*did("biases"))

        def route_scalar(a):
            a.wait_ge(*after("h"))
            a.wait_ge(*last())
            a.activation(r_h, bank("scalar", "h")[:, 0:B], ACT.Gelu, bias=W("router_b1")).then_inc(*did("gelu"))
            a.wait_ge(*after("biases"))
            a.wait_ge(*last())
            a.activation(routed_bias, bank("scalar", "biases")[:, 0:6 * B], ACT.Copy).then_inc(*did("biases_read"))

        def route_vector(v):
            l3 = r_w[0:B, 0:8].rearrange("p (n e) -> p n e", n=2)
            s3 = r_sel[0:B, :].rearrange("p (n e) -> p n e", n=2)
            c3 = r_w[0:B, 16:24].rearrange("p (n e) -> p n e", n=2)
            v.wait_ge(*after("logits"))
            v.wait_ge(*last())
            v.tensor_copy(r_w[0:B, 0:8], bank("vector", "logits")[0:B, 0:8]).then_inc(*did("logits_read"))
            v.wait_ge(*last())
            v.tensor_reduce(r_w[0:B, 8:10], l3, AX_X, ALU.max).then_inc(*did("max"))
            v.wait_ge(*last())
            v.tensor_tensor(s3, l3, r_w[0:B, 8:10].unsqueeze(2).to_broadcast([B, 2, 4]), ALU.is_ge).then_inc(*did("is_max"))
            v.wait_ge(*last())
            v.tensor_copy(c3, s3).then_inc(*did("count0"))
            for e in range(1, 4):
                v.wait_ge(*last())
                v.tensor_tensor(c3[:, :, e:e + 1], c3[:, :, e:e + 1], c3[:, :, e - 1:e], ALU.add).then_inc(*did(f"count{e}"))
            v.wait_ge(*last())
            v.tensor_scalar(c3, c3, 1.0, None, ALU.is_equal).then_inc(*did("first"))
            v.wait_ge(*last())
            v.tensor_tensor(s3, s3, c3, ALU.mult).then_inc(*did("sel"))
            v.wait_ge(*last())
            v.memset(r_t, 0.0).then_inc(*did("zeroed"))
            v.wait_ge(*after("turned"))
            v.wait_ge(*last())
            v.tensor_copy(r_t[0:4, :], bank("vector", "turned")[0:4, 0:2 * B]).then_inc(*did("turned_read"))
            v.wait_ge(*after("spread"))
            v.wait_ge(*last())
            v.tensor_copy(r_b, bank("vector", "spread")[:, 0:8 * B]).then_inc(*did("spread_read"))

        def pool_vector(v):
            norm_h_ln2[1](v)
            v.wait_ge(*last())
            v.tensor_reduce(pool_sum, HB(ln2), AX_X, ALU.add).then_inc(*did("sum"))
            v.wait_ge(*last())
            v.tensor_scalar(pool_, pool_sum, 1.0 / T, None, ALU.mult).then_inc(*did("pooled"))

        ar = new_arena()
        at1 = Attention(ar)
        pair = [at0, at1]
        masked_x = [ar.take(4 * CH) for _ in range(3)]
        heads_out = [ar.take(CH), ar.take(CH)]
        att_in = [ar.take(CH) for _ in range(4)]
        cr_kb = keep.take(4)

        def routed(n, wq, wk, wv, k_bias, wo, gain, gain_bias, mask):
            def masks(c):
                seqs = r_b.rearrange("p (e b) -> p e b", b=B)[:, 4 * n:4 * n + 4, c * CB:(c + 1) * CB]
                return [seqs[:, e, :].unsqueeze(2).to_broadcast([P, CB, T]) for e in range(E2)]

            def chosen(c):
                return r_t[:, n * B + c * CB:n * B + (c + 1) * CB].unsqueeze(2).to_broadcast([P, CB, T])

            def biases(j, c):
                at = (3 * n + j) * B + c * CB
                return routed_bias[:, at:at + CB].unsqueeze(2).to_broadcast([P, CB, T])

            def tensor(pe):
                def inputs(c):
                    for key, w, b, reader in (("q", wq, None, "q_read"), ("k", wk, k_bias, "kx3"), ("v", wv, None, "rep3")):
                        ps = fill(pe, f"a{c}.{key}", f"a{c}.{reader}")
                        if b is not None:
                            pe.matmul(ps.rearrange("p (b t) -> p b t", t=T), b, chosen(c), start=True, stop=False)
                        for e in range(4):
                            pe.wait_ge(*after(f"ex{c}.{e}"))
                            ins = pe.matmul(ps, w(e), part(masked_x[c % 3], e), start=b is None and e == 0, stop=e == 3)
                        ins.then_inc(*did(f"a{c}.{key}"))

                def project(c):
                    ps = fill(pe, f"y{c}", f"stored{c}")
                    for e in range(4):
                        pe.wait_ge(*after(f"exo{c}.{e}"))
                        ins = pe.matmul(ps, wo(e), part(masked_x[c % 3], e), start=e == 0, stop=e == 3)
                    ins.then_inc(*did(f"y{c}"))

                def scores(c):
                    scores_tensor(pe, f"a{c}", pair[c % 2], mask is not None)

                def rows(c):
                    rows_tensor(pe, f"a{c}", pair[c % 2].rep, C("ident"), [f"a{c}.rep3"])
                inputs(0)
                scores(0)
                rows(0)
                for c in range(NCH):
                    if c + 1 < NCH:
                        inputs(c + 1)
                    turn_tensor(pe, f"a{c}", pair[c % 2].s)
                    if c + 1 < NCH:
                        scores(c + 1)
                    heads_tensor(pe, f"a{c}", pair[c % 2])
                    if c + 1 < NCH:
                        rows(c + 1)
                    project(c)

            def vector(v):
                def inputs(c):
                    if c >= 3:
                        v.wait_ge(*after(f"y{c - 3}"))
                    v.wait_ge(*last())
                    v.tensor_scalar(att_in[c], part(xa, c), gain, gain_bias, ALU.mult, ALU.add).then_inc(*did(f"gained{c}"))
                    for e, seqs in enumerate(masks(c)):
                        v.wait_ge(*last())
                        v.tensor_tensor(HB(part(masked_x[c % 3], e)), HB(att_in[c]), seqs, ALU.mult).then_inc(*did(f"ex{c}.{e}"))

                def query(c):
                    v.wait_ge(*after(f"a{c}.q"))
                    if c >= 2:
                        v.wait_ge(*after(f"a{c - 2}.s1"))
                    v.wait_ge(*last())
                    v.tensor_tensor(HB(pair[c % 2].q), HB(bank("vector", f"a{c}.q")), biases(0, c), ALU.add).then_inc(*did(f"a{c}.q_read"))

                def outputs(c):
                    v.wait_ge(*after(f"a{c}.o"))
                    v.wait_ge(*last())
                    v.tensor_tensor(HB(heads_out[c % 2]), HB(bank("vector", f"a{c}.o")), biases(1, c), ALU.add).then_inc(*did(f"a{c}.o_read"))
                    for e, seqs in enumerate(masks(c)):
                        v.wait_ge(*after(f"a{c}.v"))
                        v.wait_ge(*last())
                        v.tensor_tensor(HB(part(masked_x[c % 3], e)), HB(heads_out[c % 2]), seqs, ALU.mult).then_inc(*did(f"exo{c}.{e}"))

                def store(c):
                    if n == 0:
                        v.wait_ge(*after(f"y{c}"))
                        v.wait_ge(*last())
                        v.tensor_tensor(HB(part(spatial, c)), HB(bank("vector", f"y{c}")), biases(2, c), ALU.add).then_inc(*did(f"stored{c}"))
                    else:
                        v.wait_ge(*last())
                        v.tensor_tensor(HB(att_in[c]), HB(att_in[c]), biases(2, c), ALU.add).then_inc(*did(f"in_bias{c}"))
                        v.wait_ge(*after(f"y{c}"))
                        v.wait_ge(*last())
                        v.tensor_tensor(part(temporal, c), att_in[c], bank("vector", f"y{c}"), ALU.add).then_inc(*did(f"stored{c}"))

                def scores(c):
                    scores_vector(v, f"a{c}", pair[c % 2], 0.25, mask, [f"a{c - 2}.1.turned"] if c >= 2 else [])

                def rows(c):
                    rows_vector(v, f"a{c}", pair[c % 2], [f"a{c - 2}.o"] if c >= 2 else [])
                inputs(0)
                inputs(1)
                query(0)
                scores(0)
                rows(0)
                for c in range(NCH):
                    probs_vector(v, f"a{c}", pair[c % 2])
                    if c + 1 < NCH:
                        query(c + 1)
                    if c:
                        store(c - 1)
                    if c + 2 < NCH:
                        inputs(c + 2)
                    if c + 1 < NCH:
                        scores(c + 1)
                    outputs(c)
                    if c + 1 < NCH:
                        rows(c + 1)
                store(NCH - 1)

            def scalar(a):
                def inputs(c):
                    if c >= 2:
                        a.wait_ge(*after(f"a{c - 2}.s1"))
                    k_scalar(a, f"a{c}", pair[c % 2])
                    for q in range(4):
                        a.wait_ge(*after(f"a{c}.v"))
                        if c >= 2:
                            a.wait_ge(*after(f"a{c - 2}.v3"))
                        a.wait_ge(*last())
                        a.activation(pair[c % 2].rep4[:, :, q, :], HB(bank("scalar", f"a{c}.v")), ACT.Copy).then_inc(*did(f"a{c}.rep{q}"))

                def exps(c):
                    exp_scalar(a, f"a{c}", pair[c % 2].s, 0.25 if mask is None else 1.0)
                inputs(0)
                exps(0)
                for c in range(NCH):
                    if c + 1 < NCH:
                        inputs(c + 1)
                    turned_scalar(a, f"a{c}", pair[c % 2].p)
                    if c + 1 < NCH:
                        exps(c + 1)
            return tensor, vector, scalar

        spatial_stage = routed(0, lambda e: W(f"sp_q{e}"), lambda e: W(f"sp_k{e}"), lambda e: W(f"sp_v{e}"),
                               W("sp_in_b", D, 2 * D), lambda e: W(f"sp_o{e}"), W("norm_s_w"), W("norm_s_b"), None)
        temporal_stage = routed(1, lambda e: W(f"tq_{e}"), lambda e: W(f"tk_{e}"), lambda e: W(f"tv_{e}"),
                                W("tk_b"), lambda e: W(f"tp_{e}"), W("norm_t_w"), W("norm_t_b"), lambda hh: C("causal"))

        def series_tensor(pe, q_src, kv_src, wq, wk, wv, masked, project=None):
            def qk(c):
                mm(pe, f"a{c}.q", f"a{c}.q_read", [], [(wq, part(q_src, c))])
                mm(pe, f"a{c}.k", f"a{c}.kx3", [], [(wk, part(kv_src, c))])

            def scores(c):
                scores_tensor(pe, f"a{c}", pair[c % 2], masked)

            def rows(c):
                rows_tensor(pe, f"a{c}", pair[c % 2].rep, wv, [f"a{c}.rep3"])
            qk(0)
            qk(1)
            rows(0)
            scores(0)
            for c in range(NCH):
                if c + 1 < NCH:
                    scores(c + 1)
                if c + 2 < NCH:
                    qk(c + 2)
                turn_tensor(pe, f"a{c}", pair[c % 2].s)
                if c + 1 < NCH:
                    rows(c + 1)
                heads_tensor(pe, f"a{c}", pair[c % 2])
                if c and project is not None:
                    project(c - 1)
            if project is not None:
                project(NCH - 1)

        def series_vector(v, kv_src, scale, mask, finish, lag):
            def copies(c):
                if c >= 2:
                    v.wait_ge(*after(f"a{c - 2}.v3"))
                rep_vector(v, f"a{c}", pair[c % 2], part(kv_src, c))

            def scores(c):
                scores_vector(v, f"a{c}", pair[c % 2], scale, mask, [f"a{c - 2}.1.turned"] if c >= 2 else [])

            def rows(c):
                rows_vector(v, f"a{c}", pair[c % 2], [f"a{c - 2}.o"] if c >= 2 else [])
            copies(0)
            copies(1)
            rows(0)
            scores(0)
            for c in range(NCH):
                probs_vector(v, f"a{c}", pair[c % 2])
                if c >= lag:
                    finish(c - lag)
                if c + 1 < NCH:
                    scores(c + 1)
                    rows(c + 1)
                if c + 2 < NCH:
                    copies(c + 2)
            for c in range(NCH - lag, NCH):
                finish(c)

        def series_scalar(a, scale, bias=None, k_bias=None, needs=(), heads=None):
            def qk(c):
                qk_scalar(a, f"a{c}", pair[c % 2], bias, k_bias, needs, [f"a{c - 2}.s1"] if c >= 2 else [])

            def exps(c):
                exp_scalar(a, f"a{c}", pair[c % 2].s, scale)
            qk(0)
            qk(1)
            exps(0)
            for c in range(NCH):
                if c + 2 < NCH:
                    qk(c + 2)
                turned_scalar(a, f"a{c}", pair[c % 2].p)
                if c + 1 < NCH:
                    exps(c + 1)
                if heads is not None:
                    heads(c)

        def cross_tensor(pe):
            def project(c):
                mm(pe, f"y{c}", f"sum{c}", [f"a{c}.o_read"], [(W("cr_out"), heads_out[c % 2])])
            series_tensor(pe, spatial, temporal, W("cr_in", 0, D), W("cr_in", D, 2 * D), W("cr_in", 2 * D, 3 * D), False, project)

        def cross_vector(v):
            def finish(c):
                v.wait_ge(*last())
                v.tensor_scalar(att_in[c], part(ln2, c), W("cross_out_b"), None, ALU.add).then_inc(*did(f"x_bias{c}"))
                v.wait_ge(*after(f"y{c}"))
                v.wait_ge(*last())
                v.tensor_tensor(part(ln2, c), att_in[c], bank("vector", f"y{c}"), ALU.add).then_inc(*did(f"sum{c}"))
            v.wait_ge(*last())
            v.tensor_scalar(cr_kb, C("head"), W("cross_in_b", 1, 2), None, ALU.mult).then_inc(*did("kb"))
            series_vector(v, temporal, 0.25, None, finish, 2)

        def cross_scalar(a):
            def heads(c):
                a.wait_ge(*after(f"a{c}.o"))
                if c >= 2:
                    a.wait_ge(*after(f"y{c - 2}"))
                a.wait_ge(*last())
                a.activation(heads_out[c % 2], bank("scalar", f"a{c}.o"), ACT.Identity, bias=W("cross_in_b", 2, 3)).then_inc(*did(f"a{c}.o_read"))
            series_scalar(a, 0.25, W("cross_in_b", 0, 1), cr_kb, ["kb"], heads)

        def mlp_tensor(pe):
            def up(c):
                for f in range(4):
                    mm(pe, f"u{c}.{f}", f"g{c}.{f}", [], [(W("mlp_1", f * P, (f + 1) * P), part(xa, c))])
            up(0)
            for c in range(NCH):
                if c + 1 < NCH:
                    up(c + 1)
                mm(pe, f"y{c}", f"h_new{c}", [f"g{c}.3"], [(W("mlp_2", f * D, (f + 1) * D), part(masked_x[c % 2], f)) for f in range(4)])

        def mlp_vector(v):
            for c in range(NCH):
                v.wait_ge(*last())
                v.tensor_scalar(att_in[c], part(ln2, c), W("mlp_b2"), None, ALU.add).then_inc(*did(f"x_bias{c}"))
                v.wait_ge(*last())
                v.tensor_tensor(att_in[c], att_in[c], part(h, c), ALU.add).then_inc(*did(f"x_h{c}"))
            for c in range(NCH):
                v.wait_ge(*after(f"y{c}"))
                v.wait_ge(*last())
                v.tensor_tensor(part(h, c), att_in[c], bank("vector", f"y{c}"), ALU.add).then_inc(*did(f"h_new{c}"))

        def mlp_scalar(a):
            for c in range(NCH):
                for f in range(4):
                    a.wait_ge(*after(f"u{c}.{f}"))
                    if c >= 2:
                        a.wait_ge(*after(f"y{c - 2}"))
                    a.wait_ge(*last())
                    a.activation(part(masked_x[c % 2], f), bank("scalar", f"u{c}.{f}"), ACT.Gelu,
                                 bias=W("mlp_b1", f, f + 1)).then_inc(*did(f"g{c}.{f}"))

        def l3_tensor(pe):
            series_tensor(pe, xa, xa, W("l3_q"), W("l3_k"), W("l3_v"), True)

        def l3_vector(v):
            def finish(c):
                v.wait_ge(*after(f"a{c}.o"))
                v.wait_ge(*last())
                v.tensor_tensor(part(h, c), part(h, c), bank("vector", f"a{c}.o"), ALU.add).then_inc(*did(f"a{c}.o_read"))
            series_vector(v, xa, 0.25, lambda hh: W("l3_rel", hh * 4 * T, (hh + 1) * 4 * T), finish, 1)

        def l3_scalar(a):
            series_scalar(a, 1.0)

        ar = new_arena()
        class Adapters:
            def __init__(self):
                self.x = ar.take(CH)
                self.hidden, self.lo2 = [ar.take(CH) for _ in range(4)], [ar.take(CH) for _ in range(4)]
                self.logits, self.weights, self.st = ar.take(NT * 5), ar.take(NT * 4), ar.take(32)
                self.wide, self.wide_t, self.lo = ar.take(NT * 64), ar.take(CH), ar.take(CH)
        adapters = [Adapters(), Adapters()]
        ER = E3 * R3

        def l3e_tensor(pe, i):
            for c, ad in enumerate(adapters):
                ps = fill(pe, f"gates{c}", f"gates{c}_read")
                pe.wait_ge(*after(f"x{c}"))
                for t in range(NT):
                    ins = pe.matmul(ps[:, 5 * t:5 * t + 5], ad.x[:, t * P:(t + 1) * P], W("l3_gate", 0, 5),
                                    start=True, stop=True)
                ins.then_inc(*did(f"gates{c}"))
            for c, ad in enumerate(adapters):
                for e in range(4):
                    mm(pe, f"f{c}{e}", f"relu{c}{e}", [], [(W(f"fc1_{e}"), ad.x)])
            for c, ad in enumerate(adapters):
                mm(pe, f"lo{c}", f"wlo{c}", [f"relu{c}2", f"relu{c}3"], [(W("lora_a", e * ER, (e + 1) * ER), ad.hidden[e]) for e in range(4)])
                ps = fill(pe, f"wide_t{c}", f"wide_t{c}_read")
                pe.wait_ge(*after(f"wide{c}"))
                for t in range(NT):
                    ins = pe.transpose(ps[0:ER, t * P:(t + 1) * P], ad.wide[:, t * ER:(t + 1) * ER], C("ident"))
                ins.then_inc(*did(f"wide_t{c}"))
            for c, ad in enumerate(adapters):
                for e in range(4):
                    mm(pe, f"l{c}{e}", f"lo{c}{e}", [f"wlo{c}"], [(W("lora_b", e * D, (e + 1) * D)[0:ER, :], ad.lo[0:ER, :])])
            for c, ad in enumerate(adapters):
                mm(pe, f"y{c}", f"h_new{c}", [f"lo{c}2", f"lo{c}3"], [(W(f"fc2_{e}"), ad.lo2[e]) for e in range(4)])

        def l3_weights_vector(v, c, ad):
            g3 = ad.logits.rearrange("p (t e) -> p t e", e=5)
            w3 = ad.weights.rearrange("p (t e) -> p t e", e=4)
            col = lambda n: ad.st[:, 4 * n:4 * n + 4]
            sp = lambda n: col(n).unsqueeze(2).to_broadcast([P, NT, 4])
            v.wait_ge(*after(f"gexp{c}"))
            v.wait_ge(*last())
            v.tensor_reduce(col(1), w3, AX_X, ALU.add).then_inc(*did(f"esum{c}"))
            v.wait_ge(*last())
            v.reciprocal(col(2), col(1)).then_inc(*did(f"erec{c}"))
            v.wait_ge(*last())
            v.tensor_tensor(w3, w3, sp(2), ALU.mult).then_inc(*did(f"soft{c}"))
            v.wait_ge(*after(f"tsig{c}"))
            v.wait_ge(*last())
            v.tensor_scalar(col(4), col(3), 1.0 / E3, None, ALU.mult).then_inc(*did(f"thr{c}"))
            v.wait_ge(*last())
            v.tensor_tensor(w3, w3, sp(4), ALU.subtract).then_inc(*did(f"adapted{c}"))
            v.wait_ge(*last())
            v.tensor_scalar(ad.weights, ad.weights, 0.0, None, ALU.max).then_inc(*did(f"selected{c}"))
            v.wait_ge(*last())
            v.tensor_reduce(col(5), w3, AX_X, ALU.add).then_inc(*did(f"wsum{c}"))
            v.wait_ge(*last())
            v.tensor_scalar(col(6), col(5), 0.0, None, ALU.is_equal).then_inc(*did(f"empty{c}"))
            v.wait_ge(*last())
            v.tensor_tensor(col(5), col(5), col(6), ALU.add).then_inc(*did(f"wsum1{c}"))
            v.wait_ge(*last())
            v.reciprocal(col(7), col(5)).then_inc(*did(f"wrec{c}"))
            v.wait_ge(*last())
            v.tensor_tensor(w3, w3, sp(7), ALU.mult).then_inc(*did(f"weights{c}"))
            v.wait_ge(*last())
            v.tensor_copy(ad.wide.rearrange("p (te r) -> p te r", r=R3), ad.weights.unsqueeze(2).to_broadcast([P, NT * 4, R3])).then_inc(*did(f"wide{c}"))

        def l3e_vector(v, i):
            for c, ad in enumerate(adapters):
                v.wait_ge(*last())
                v.tensor_copy(ad.x, of_pair(xa, i, c)).then_inc(*did(f"x{c}"))
            for c, ad in enumerate(adapters):
                g3 = ad.logits.rearrange("p (t e) -> p t e", e=5)
                v.wait_ge(*after(f"gates{c}"))
                v.wait_ge(*last())
                v.tensor_copy(ad.logits, bank("vector", f"gates{c}")[:, 0:20]).then_inc(*did(f"gates{c}_read"))
                v.wait_ge(*last())
                v.tensor_reduce(ad.st[:, 0:4], g3[:, :, 0:4], AX_X, ALU.max).then_inc(*did(f"max{c}"))
                v.wait_ge(*last())
                v.tensor_tensor(ad.weights.rearrange("p (t e) -> p t e", e=4), g3[:, :, 0:4],
                                ad.st[:, 0:4].unsqueeze(2).to_broadcast([P, NT, 4]), ALU.subtract).then_inc(*did(f"sub{c}"))
            for c, ad in enumerate(adapters):
                l3_weights_vector(v, c, ad)
                for e in (1, 3):
                    v.wait_ge(*after(f"f{c}{e}"))
                    v.wait_ge(*last())
                    v.tensor_scalar(ad.hidden[e], bank("vector", f"f{c}{e}"), 0.0, None, ALU.max).then_inc(*did(f"relu{c}{e}"))
            for c, ad in enumerate(adapters):
                v.wait_ge(*after(f"wide_t{c}"))
                v.wait_ge(*last())
                v.tensor_copy(ad.wide_t[0:ER, :], bank("vector", f"wide_t{c}")[0:ER, :]).then_inc(*did(f"wide_t{c}_read"))
                v.wait_ge(*after(f"lo{c}"))
                v.wait_ge(*last())
                v.tensor_tensor(ad.lo[0:ER, :], ad.wide_t[0:ER, :], bank("vector", f"lo{c}")[0:ER, :], ALU.mult).then_inc(*did(f"wlo{c}"))
            for c, ad in enumerate(adapters):
                for e in (1, 3):
                    v.wait_ge(*after(f"l{c}{e}"))
                    v.wait_ge(*last())
                    v.tensor_copy(ad.lo2[e], bank("vector", f"l{c}{e}")).then_inc(*did(f"lo{c}{e}"))
            for c in range(2):
                v.wait_ge(*after(f"y{c}"))
                v.wait_ge(*last())
                v.tensor_tensor(of_pair(h, i, c), of_pair(h, i, c), bank("vector", f"y{c}"), ALU.add).then_inc(*did(f"h_new{c}"))

        def l3e_scalar(a, i):
            for c, ad in enumerate(adapters):
                a.wait_ge(*after(f"sub{c}"))
                a.wait_ge(*last())
                a.activation(ad.weights, ad.weights, ACT.Exp).then_inc(*did(f"gexp{c}"))
            for c, ad in enumerate(adapters):
                a.wait_ge(*after(f"gates{c}_read"))
                a.wait_ge(*last())
                a.activation(ad.st[:, 12:16], ad.logits.rearrange("p (t e) -> p t e", e=5)[:, :, 4], ACT.Sigmoid).then_inc(*did(f"tsig{c}"))
            for c, ad in enumerate(adapters):
                for e in (0, 2):
                    a.wait_ge(*after(f"f{c}{e}"))
                    a.wait_ge(*last())
                    a.activation(ad.hidden[e], bank("scalar", f"f{c}{e}"), ACT.Relu).then_inc(*did(f"relu{c}{e}"))
            for c, ad in enumerate(adapters):
                for e in (0, 2):
                    a.wait_ge(*after(f"l{c}{e}"))
                    a.wait_ge(*last())
                    a.activation(ad.lo2[e], bank("scalar", f"l{c}{e}"), ACT.Copy).then_inc(*did(f"lo{c}{e}"))

        o_rows = new_arena().take(2 * CH).rearrange("p (k c) -> p k c", k=2)
        out_tiles = out.rearrange("b t d -> (b t) d").rearrange("(c k p) d -> c p k d", k=NT, p=P)

        def write_tensor(pe):
            for c in range(NCH):
                ps = fill(pe, f"t{c}", f"r{c}")
                for t in range(NT):
                    at = c * CH + t * P
                    ins = pe.transpose(ps[:, t * P:(t + 1) * P], h[:, at:at + P], C("ident"))
                ins.then_inc(*did(f"t{c}"))

        def write_scalar(a):
            for c in range(NCH):
                if c >= 2:
                    a.wait_ge(stored[c % 2], 16 * (c // 2))
                a.wait_ge(*after(f"t{c}"))
                a.wait_ge(*last())
                a.activation(o_rows[:, c % 2, :], bank("scalar", f"t{c}"), ACT.Copy).then_inc(*did(f"r{c}"))

        def write_sync(sp):
            for c in range(NCH):
                sp.wait_ge(*after(f"r{c}"))
                sp.dma_start(out_tiles[c], o_rows[:, c % 2, :].rearrange("p (k d) -> p k d", d=D)).then_inc(stored[c % 2], 16)
            for n in range(2):
                sp.wait_ge(stored[n], 16 * NCH // 2)

        def start_vector(v):
            v.wait_ge(*last())
            v.memset(gh[0], 0.0).then_inc(*did("h0"))

        block = ctx.enter_context(nc.Block())

        @block.sync
        def _(sp):
            sp.dma_start(vec[:, :], weights[:, vec_at:W_COLS]).then_inc(tok_loaded, 16)
            begin("sync", "select")
            select_sync(sp)
            lead(sp, "select")
            begin("sync", "l0_norm")
            lead(sp, "l0_norm")
            begin("sync", "l0_attention")
            with sp.Fori(0, NCH):
                lead(sp, "l0_attention")
            begin("sync", "gru_norm")
            lead(sp, "gru_norm")
            begin("sync", "gru_input")
            with sp.Fori(0, NCH // 2):
                lead(sp, "gru_input")
            begin("sync", "gru_start")
            lead(sp, "gru_start")
            begin("sync", "gru")
            with sp.Fori(0, T // GRU_U):
                lead(sp, "gru")
            begin("sync", "gru_output")
            with sp.Fori(0, NCH // 2):
                lead(sp, "gru_output")
            begin("sync", "l1_norm")
            lead(sp, "l1_norm")
            begin("sync", "l1_attention")
            with sp.Fori(0, NCH // 2):
                lead(sp, "l1_attention")
            begin("sync", "experts_norm")
            lead(sp, "experts_norm")
            begin("sync", "experts_norm2")
            lead(sp, "experts_norm2")
            begin("sync", "experts")
            sp.dma_start(wt[:, 0:third_at - second_at], weights[:, second_at:third_at]).then_inc(second_loaded, 16)
            with sp.Fori(0, NCH // 2):
                lead(sp, "experts")
            begin("sync", "l2_norm")
            lead(sp, "l2_norm")
            begin("sync", "l2_input")
            sp.dma_start(wt[:, experts_at:experts_at + vec_at - third_at],
                         weights[:, third_at:vec_at]).then_inc(third_loaded, 16)
            with sp.Fori(0, NCH // 2):
                lead(sp, "l2_input")
            begin("sync", "l2_scan")
            lead(sp, "l2_scan")
            begin("sync", "l2_output")
            lead(sp, "l2_output")
            begin("sync", "pool")
            lead(sp, "pool")
            begin("sync", "route")
            lead(sp, "route")
            begin("sync", "l2_norm_again")
            lead(sp, "l2_norm_again")
            begin("sync", "l2_spatial")
            lead(sp, "l2_spatial")
            begin("sync", "l2_temporal")
            lead(sp, "l2_temporal")
            begin("sync", "l2_cross")
            lead(sp, "l2_cross")
            begin("sync", "mlp_norm")
            lead(sp, "mlp_norm")
            begin("sync", "l2_mlp")
            lead(sp, "l2_mlp")
            begin("sync", "l3_norm")
            lead(sp, "l3_norm")
            begin("sync", "l3_attention")
            lead(sp, "l3_attention")
            begin("sync", "l3_experts_norm")
            lead(sp, "l3_experts_norm")
            begin("sync", "l3_experts")
            with sp.Fori(0, NCH // 2):
                lead(sp, "l3_experts")
            begin("sync", "write")
            write_sync(sp)
            lead(sp, "write")

        @block.tensor
        def _(pe):
            begin("tensor", "select")
            select_tensor(pe)
            meet(pe, "tensor", "select")
            begin("tensor", "l0_norm")
            norm_h_xa[0](pe)
            meet(pe, "tensor", "l0_norm")
            begin("tensor", "l0_attention")
            with pe.Fori(0, NCH) as i:
                l0_tensor(pe, i)
                meet(pe, "tensor", "l0_attention")
            begin("tensor", "gru_norm")
            norm_h_xa[0](pe)
            meet(pe, "tensor", "gru_norm")
            begin("tensor", "gru_input")
            with pe.Fori(0, NCH // 2) as i:
                gru_input_tensor(pe, i)
                meet(pe, "tensor", "gru_input")
            begin("tensor", "gru_start")
            meet(pe, "tensor", "gru_start")
            begin("tensor", "gru")
            with pe.Fori(0, T // GRU_U) as i:
                gru_tensor(pe, i)
                meet(pe, "tensor", "gru")
            begin("tensor", "gru_output")
            with pe.Fori(0, NCH // 2) as i:
                gru_output_tensor(pe, i)
                meet(pe, "tensor", "gru_output")
            begin("tensor", "l1_norm")
            norm_h_xa[0](pe)
            meet(pe, "tensor", "l1_norm")
            begin("tensor", "l1_attention")
            with pe.Fori(0, NCH // 2) as i:
                l1_tensor(pe, i)
                meet(pe, "tensor", "l1_attention")
            begin("tensor", "experts_norm")
            norm_h_xa[0](pe)
            meet(pe, "tensor", "experts_norm")
            begin("tensor", "experts_norm2")
            norm_experts[0](pe)
            meet(pe, "tensor", "experts_norm2")
            begin("tensor", "experts")
            with pe.Fori(0, NCH // 2) as i:
                experts_tensor(pe, i)
                meet(pe, "tensor", "experts")
            begin("tensor", "l2_norm")
            norm_h_ln2[0](pe)
            meet(pe, "tensor", "l2_norm")
            begin("tensor", "l2_input")
            pe.wait_ge(second_loaded, 16)
            with pe.Fori(0, NCH // 2) as i:
                l2_input_tensor(pe, i)
                meet(pe, "tensor", "l2_input")
            begin("tensor", "l2_scan")
            meet(pe, "tensor", "l2_scan")
            begin("tensor", "l2_output")
            l2_output_tensor(pe)
            meet(pe, "tensor", "l2_output")
            begin("tensor", "pool")
            norm_h_ln2[0](pe)
            meet(pe, "tensor", "pool")
            begin("tensor", "route")
            route_tensor(pe)
            meet(pe, "tensor", "route")
            begin("tensor", "l2_norm_again")
            norm_ln2_xa[0](pe)
            meet(pe, "tensor", "l2_norm_again")
            begin("tensor", "l2_spatial")
            spatial_stage[0](pe)
            meet(pe, "tensor", "l2_spatial")
            begin("tensor", "l2_temporal")
            temporal_stage[0](pe)
            meet(pe, "tensor", "l2_temporal")
            begin("tensor", "l2_cross")
            cross_tensor(pe)
            meet(pe, "tensor", "l2_cross")
            begin("tensor", "mlp_norm")
            norm_mlp[0](pe)
            meet(pe, "tensor", "mlp_norm")
            begin("tensor", "l2_mlp")
            mlp_tensor(pe)
            meet(pe, "tensor", "l2_mlp")
            begin("tensor", "l3_norm")
            norm_h_xa[0](pe)
            meet(pe, "tensor", "l3_norm")
            begin("tensor", "l3_attention")
            pe.wait_ge(third_loaded, 16)
            l3_tensor(pe)
            meet(pe, "tensor", "l3_attention")
            begin("tensor", "l3_experts_norm")
            norm_h_xa[0](pe)
            meet(pe, "tensor", "l3_experts_norm")
            begin("tensor", "l3_experts")
            with pe.Fori(0, NCH // 2) as i:
                l3e_tensor(pe, i)
                meet(pe, "tensor", "l3_experts")
            begin("tensor", "write")
            write_tensor(pe)
            meet(pe, "tensor", "write")

        @block.vector
        def _(v):
            begin("vector", "select")
            select_vector(v)
            meet(v, "vector", "select")
            begin("vector", "l0_norm")
            norm_h_xa[1](v)
            meet(v, "vector", "l0_norm")
            begin("vector", "l0_attention")
            with v.Fori(0, NCH) as i:
                l0_vector(v, i)
                meet(v, "vector", "l0_attention")
            begin("vector", "gru_norm")
            norm_h_xa[1](v)
            meet(v, "vector", "gru_norm")
            begin("vector", "gru_input")
            with v.Fori(0, NCH // 2) as i:
                gru_input_vector(v, i)
                meet(v, "vector", "gru_input")
            begin("vector", "gru_start")
            start_vector(v)
            meet(v, "vector", "gru_start")
            begin("vector", "gru")
            with v.Fori(0, T // GRU_U) as i:
                gru_vector(v, i)
                meet(v, "vector", "gru")
            begin("vector", "gru_output")
            with v.Fori(0, NCH // 2) as i:
                gru_output_vector(v, i)
                meet(v, "vector", "gru_output")
            begin("vector", "l1_norm")
            norm_h_xa[1](v)
            meet(v, "vector", "l1_norm")
            begin("vector", "l1_attention")
            with v.Fori(0, NCH // 2) as i:
                l1_vector(v, i)
                meet(v, "vector", "l1_attention")
            begin("vector", "experts_norm")
            norm_h_xa[1](v)
            meet(v, "vector", "experts_norm")
            begin("vector", "experts_norm2")
            norm_experts[1](v)
            meet(v, "vector", "experts_norm2")
            begin("vector", "experts")
            with v.Fori(0, NCH // 2) as i:
                experts_vector(v, i)
                meet(v, "vector", "experts")
            begin("vector", "l2_norm")
            norm_h_ln2[1](v)
            meet(v, "vector", "l2_norm")
            begin("vector", "l2_input")
            v.wait_ge(second_loaded, 16)
            with v.Fori(0, NCH // 2) as i:
                l2_input_vector(v, i)
                meet(v, "vector", "l2_input")
            begin("vector", "l2_scan")
            l2_scan_vector(v)
            meet(v, "vector", "l2_scan")
            begin("vector", "l2_output")
            l2_output_vector(v)
            meet(v, "vector", "l2_output")
            begin("vector", "pool")
            pool_vector(v)
            meet(v, "vector", "pool")
            begin("vector", "route")
            route_vector(v)
            meet(v, "vector", "route")
            begin("vector", "l2_norm_again")
            norm_ln2_xa[1](v)
            meet(v, "vector", "l2_norm_again")
            begin("vector", "l2_spatial")
            spatial_stage[1](v)
            meet(v, "vector", "l2_spatial")
            begin("vector", "l2_temporal")
            temporal_stage[1](v)
            meet(v, "vector", "l2_temporal")
            begin("vector", "l2_cross")
            cross_vector(v)
            meet(v, "vector", "l2_cross")
            begin("vector", "mlp_norm")
            norm_mlp[1](v)
            meet(v, "vector", "mlp_norm")
            begin("vector", "l2_mlp")
            mlp_vector(v)
            meet(v, "vector", "l2_mlp")
            begin("vector", "l3_norm")
            norm_h_xa[1](v)
            meet(v, "vector", "l3_norm")
            begin("vector", "l3_attention")
            v.wait_ge(third_loaded, 16)
            l3_vector(v)
            meet(v, "vector", "l3_attention")
            begin("vector", "l3_experts_norm")
            norm_h_xa[1](v)
            meet(v, "vector", "l3_experts_norm")
            begin("vector", "l3_experts")
            with v.Fori(0, NCH // 2) as i:
                l3e_vector(v, i)
                meet(v, "vector", "l3_experts")
            begin("vector", "write")
            meet(v, "vector", "write")

        @block.scalar
        def _(a):
            begin("scalar", "select")
            select_scalar(a)
            meet(a, "scalar", "select")
            begin("scalar", "l0_norm")
            norm_h_xa[2](a)
            meet(a, "scalar", "l0_norm")
            begin("scalar", "l0_attention")
            with a.Fori(0, NCH) as i:
                l0_scalar(a, i)
                meet(a, "scalar", "l0_attention")
            begin("scalar", "gru_norm")
            norm_h_xa[2](a)
            meet(a, "scalar", "gru_norm")
            begin("scalar", "gru_input")
            with a.Fori(0, NCH // 2) as i:
                gru_input_scalar(a, i)
                meet(a, "scalar", "gru_input")
            begin("scalar", "gru_start")
            meet(a, "scalar", "gru_start")
            begin("scalar", "gru")
            with a.Fori(0, T // GRU_U) as i:
                gru_scalar(a, i)
                meet(a, "scalar", "gru")
            begin("scalar", "gru_output")
            with a.Fori(0, NCH // 2) as i:
                gru_output_scalar(a, i)
                meet(a, "scalar", "gru_output")
            begin("scalar", "l1_norm")
            norm_h_xa[2](a)
            meet(a, "scalar", "l1_norm")
            begin("scalar", "l1_attention")
            with a.Fori(0, NCH // 2) as i:
                l1_scalar(a, i)
                meet(a, "scalar", "l1_attention")
            begin("scalar", "experts_norm")
            norm_h_xa[2](a)
            meet(a, "scalar", "experts_norm")
            begin("scalar", "experts_norm2")
            norm_experts[2](a)
            meet(a, "scalar", "experts_norm2")
            begin("scalar", "experts")
            with a.Fori(0, NCH // 2) as i:
                experts_scalar(a, i)
                meet(a, "scalar", "experts")
            begin("scalar", "l2_norm")
            norm_h_ln2[2](a)
            meet(a, "scalar", "l2_norm")
            begin("scalar", "l2_input")
            a.wait_ge(second_loaded, 16)
            with a.Fori(0, NCH // 2) as i:
                l2_input_scalar(a, i)
                meet(a, "scalar", "l2_input")
            begin("scalar", "l2_scan")
            meet(a, "scalar", "l2_scan")
            begin("scalar", "l2_output")
            l2_output_scalar(a)
            meet(a, "scalar", "l2_output")
            begin("scalar", "pool")
            norm_h_ln2[2](a)
            meet(a, "scalar", "pool")
            begin("scalar", "route")
            route_scalar(a)
            meet(a, "scalar", "route")
            begin("scalar", "l2_norm_again")
            norm_ln2_xa[2](a)
            meet(a, "scalar", "l2_norm_again")
            begin("scalar", "l2_spatial")
            spatial_stage[2](a)
            meet(a, "scalar", "l2_spatial")
            begin("scalar", "l2_temporal")
            temporal_stage[2](a)
            meet(a, "scalar", "l2_temporal")
            begin("scalar", "l2_cross")
            cross_scalar(a)
            meet(a, "scalar", "l2_cross")
            begin("scalar", "mlp_norm")
            norm_mlp[2](a)
            meet(a, "scalar", "mlp_norm")
            begin("scalar", "l2_mlp")
            mlp_scalar(a)
            meet(a, "scalar", "l2_mlp")
            begin("scalar", "l3_norm")
            norm_h_xa[2](a)
            meet(a, "scalar", "l3_norm")
            begin("scalar", "l3_attention")
            a.wait_ge(third_loaded, 16)
            l3_scalar(a)
            meet(a, "scalar", "l3_attention")
            begin("scalar", "l3_experts_norm")
            norm_h_xa[2](a)
            meet(a, "scalar", "l3_experts_norm")
            begin("scalar", "l3_experts")
            with a.Fori(0, NCH // 2) as i:
                l3e_scalar(a, i)
                meet(a, "scalar", "l3_experts")
            begin("scalar", "write")
            write_scalar(a)
            meet(a, "scalar", "write")

        @block.gpsimd
        def _(g):
            begin("gpsimd", "select")
            select_gpsimd(g)
            meet(g, "gpsimd", "select")
            begin("gpsimd", "l0_norm")
            meet(g, "gpsimd", "l0_norm")
            begin("gpsimd", "l0_attention")
            with g.Fori(0, NCH) as i:
                meet(g, "gpsimd", "l0_attention")
            begin("gpsimd", "gru_norm")
            meet(g, "gpsimd", "gru_norm")
            begin("gpsimd", "gru_input")
            with g.Fori(0, NCH // 2) as i:
                meet(g, "gpsimd", "gru_input")
            begin("gpsimd", "gru_start")
            meet(g, "gpsimd", "gru_start")
            begin("gpsimd", "gru")
            with g.Fori(0, T // GRU_U) as i:
                meet(g, "gpsimd", "gru")
            begin("gpsimd", "gru_output")
            with g.Fori(0, NCH // 2) as i:
                meet(g, "gpsimd", "gru_output")
            begin("gpsimd", "l1_norm")
            meet(g, "gpsimd", "l1_norm")
            begin("gpsimd", "l1_attention")
            with g.Fori(0, NCH // 2) as i:
                meet(g, "gpsimd", "l1_attention")
            begin("gpsimd", "experts_norm")
            meet(g, "gpsimd", "experts_norm")
            begin("gpsimd", "experts_norm2")
            meet(g, "gpsimd", "experts_norm2")
            begin("gpsimd", "experts")
            with g.Fori(0, NCH // 2) as i:
                meet(g, "gpsimd", "experts")
            begin("gpsimd", "l2_norm")
            meet(g, "gpsimd", "l2_norm")
            begin("gpsimd", "l2_input")
            g.wait_ge(second_loaded, 16)
            with g.Fori(0, NCH // 2) as i:
                meet(g, "gpsimd", "l2_input")
            begin("gpsimd", "l2_scan")
            meet(g, "gpsimd", "l2_scan")
            begin("gpsimd", "l2_output")
            meet(g, "gpsimd", "l2_output")
            begin("gpsimd", "pool")
            meet(g, "gpsimd", "pool")
            begin("gpsimd", "route")
            meet(g, "gpsimd", "route")
            begin("gpsimd", "l2_norm_again")
            meet(g, "gpsimd", "l2_norm_again")
            begin("gpsimd", "l2_spatial")
            meet(g, "gpsimd", "l2_spatial")
            begin("gpsimd", "l2_temporal")
            meet(g, "gpsimd", "l2_temporal")
            begin("gpsimd", "l2_cross")
            meet(g, "gpsimd", "l2_cross")
            begin("gpsimd", "mlp_norm")
            meet(g, "gpsimd", "mlp_norm")
            begin("gpsimd", "l2_mlp")
            meet(g, "gpsimd", "l2_mlp")
            begin("gpsimd", "l3_norm")
            meet(g, "gpsimd", "l3_norm")
            begin("gpsimd", "l3_attention")
            g.wait_ge(third_loaded, 16)
            meet(g, "gpsimd", "l3_attention")
            begin("gpsimd", "l3_experts_norm")
            meet(g, "gpsimd", "l3_experts_norm")
            begin("gpsimd", "l3_experts")
            with g.Fori(0, NCH // 2) as i:
                meet(g, "gpsimd", "l3_experts")
            begin("gpsimd", "write")
            meet(g, "gpsimd", "write")
    if known is not None:
        steps.check_order()
    return steps


def kernel(**inputs):
    import concourse.bacc as bacc
    from concourse.bass_utils import run_bass_kernel_spmd

    x = np.ascontiguousarray(inputs["x"])
    a = {k: np.asarray(v) for k, v in inputs.items()}
    packed = np.concatenate([lay(a).astype(np.float32, copy=False) for _, _, lay in weight_list()], axis=1)
    consts = np.concatenate([np.asarray(c, np.float32).reshape(P, -1) for _, c in constant_list()], axis=1)

    def program(known):
        nc = bacc.Bacc("TRN2", target_bir_lowering=False, num_devices=1)
        args = [nc.dram_tensor(n, v.shape, F32, kind="ExternalInput").ap()
                for n, v in (("in_x", x), ("in_w", packed), ("in_c", consts))]
        o = nc.dram_tensor("out_0", (B, T, D), F32, kind="ExternalOutput").ap()
        return nc, tower(nc, *args, o, known)
    _, counts = program(None)
    nc, _ = program(counts)
    r = run_bass_kernel_spmd(nc, [{"in_x": x, "in_w": np.ascontiguousarray(packed), "in_c": consts}], core_ids=[0])
    return r.results[0]["out_0"]
```
